# Optimizing a Trainium2 kernel written in Bass

```python
import numpy as np
import jax
import jax.numpy as jnp

def _softmax(x, axis=-1):
    return jax.nn.softmax(x, axis=axis)

def _gelu(x):
    return jax.nn.gelu(x, approximate=True)

def _silu(x):
    return jax.nn.silu(x)

def _sigmoid(x):
    return jax.nn.sigmoid(x)

def _layernorm(x, axis=-1, eps=1e-05):
    m = jnp.mean(x, axis=axis, keepdims=True)
    v = jnp.var(x, axis=axis, keepdims=True)
    return (x - m) / jnp.sqrt(v + eps)

def _scatter_add(tgt, idx, src, axis=0):
    return tgt.at[idx].add(src)

def _segment_sum(src, seg, n):
    return jax.ops.segment_sum(src, seg, n)
kernel_name = 'mk_seq_preln_d2_jaxref_r8_42a38d'

def setup_inputs(seed: int=0):
    np.random.seed(seed)
    _w = jnp.asarray

    def _L0_attn_setup():
        import jax, jax.numpy as jnp
        import numpy as np
        N_HEADS = 16
        SCALE = 8.0
        key = jax.random.key(seed)
        k1, k2, k3, k4 = jax.random.split(key, 4)
        b, n, d_model, inner = (8, 256, 128, 128)
        x = jax.random.normal(k1, (b, n, d_model), dtype=jnp.float32)
        Wqkv = jax.random.normal(k2, (3 * inner, d_model), dtype=jnp.float32) * (1.0 / np.sqrt(d_model))
        Wproj = jax.random.normal(k3, (d_model, inner), dtype=jnp.float32) * (1.0 / np.sqrt(inner))
        bproj = jax.random.normal(k4, (d_model,), dtype=jnp.float32) * 0.01
        return {'x': x, 'Wqkv': Wqkv, 'Wproj': Wproj, 'bproj': bproj}
    _L0_attn_in = _L0_attn_setup()

    def _L0_ffn_setup():
        import jax, jax.numpy as jnp
        import numpy as np
        HIDDEN = 128
        INTER = 512
        N_EXPERTS = 8
        TOP_K = 2
        INIT_STD = 0.02
        key = jax.random.key(seed)
        ks = jax.random.split(key, 6)
        x = jax.random.normal(ks[0], (2, 128, HIDDEN), dtype=jnp.float32)
        Wg = jax.random.normal(ks[1], (N_EXPERTS, HIDDEN), dtype=jnp.float32) * INIT_STD
        W1 = jax.random.normal(ks[2], (N_EXPERTS, HIDDEN, INTER), dtype=jnp.float32) * INIT_STD
        b1 = jnp.zeros((N_EXPERTS, INTER), dtype=jnp.float32)
        W2 = jax.random.normal(ks[3], (N_EXPERTS, INTER, HIDDEN), dtype=jnp.float32) * INIT_STD
        b2 = jnp.zeros((N_EXPERTS, HIDDEN), dtype=jnp.float32)
        return {'x': x, 'Wg': Wg, 'W1': W1, 'b1': b1, 'W2': W2, 'b2': b2}
    _L0_ffn_in = _L0_ffn_setup()

    def _L1_attn_setup():
        import jax, jax.numpy as jnp
        import numpy as np
        N_STREAMS = 8
        DIM = 128
        N_HEADS = 16
        HEAD_DIM = DIM // N_HEADS
        STREAM_DIM = DIM // N_STREAMS
        EPS = 1e-06

        def delta_operator(x, decay_logits):
            beta = jax.nn.sigmoid(decay_logits)

            def step(s, xt):
                out = xt - s
                s_new = beta * s + (1.0 - beta) * xt
                return (s_new, out)
            xT = jnp.swapaxes(x, 0, 1)
            s0 = jnp.zeros_like(xT[0])
            _, ysT = jax.lax.scan(step, s0, xT)
            return jnp.swapaxes(ysT, 0, 1)

        def rms_norm(x, w):
            var = jnp.mean(x * x, axis=-1, keepdims=True)
            return x * jax.lax.rsqrt(var + EPS) * w

        def sinkhorn_knopp(phi, iterations=15):
            K = jnp.exp(phi)
            for _ in range(iterations):
                K = K / jnp.sum(K, axis=1, keepdims=True)
                K = K / jnp.sum(K, axis=0, keepdims=True)
            return K

        def causal_mha(x, in_proj_w, in_proj_b, out_w, out_b):
            B, S, D = x.shape
            qkv = x @ in_proj_w.T + in_proj_b
            q, k, v = jnp.split(qkv, 3, axis=-1)

            def heads(t):
                return t.reshape(B, S, N_HEADS, HEAD_DIM).transpose(0, 2, 1, 3)
            q, k, v = (heads(q), heads(k), heads(v))
            scores = jnp.einsum('bhqd,bhkd->bhqk', q, k) / jnp.sqrt(jnp.float32(HEAD_DIM))
            mask = jnp.tril(jnp.ones((S, S), bool))
            scores = jnp.where(mask, scores, jnp.float32(-1000000000.0))
            attn = jax.nn.softmax(scores, axis=-1)
            o = jnp.einsum('bhqk,bhkd->bhqd', attn, v)
            o = o.transpose(0, 2, 1, 3).reshape(B, S, D)
            return o @ out_w.T + out_b
        key = jax.random.key(seed)
        ks = jax.random.split(key, 20)
        B, S, D = (2, 256, DIM)
        inp = {'x': jax.random.normal(ks[0], (B, S, D), jnp.float32), 'rope_cos': jax.random.uniform(ks[1], (S, HEAD_DIM), jnp.float32), 'rope_sin': jax.random.uniform(ks[2], (S, HEAD_DIM), jnp.float32), 'delta_decay': jax.random.normal(ks[3], (D,), jnp.float32) * 0.02, 'gate_w': jax.random.normal(ks[4], (3 * N_STREAMS, D), jnp.float32) * 0.02, 'gate_b': jnp.zeros((3 * N_STREAMS,), jnp.float32), 'phi_res': jax.random.normal(ks[5], (N_STREAMS, N_STREAMS), jnp.float32) * 0.02, 'ln1_w': jnp.ones((D,), jnp.float32), 'ln2_w': jnp.ones((D,), jnp.float32), 'w1': jax.random.normal(ks[6], (4 * D, D), jnp.float32) * 0.02, 'b1': jnp.zeros((4 * D,), jnp.float32), 'w2': jax.random.normal(ks[7], (D, 4 * D), jnp.float32) * 0.02, 'b2': jnp.zeros((D,), jnp.float32), 'in_proj_w': jax.random.normal(ks[8], (3 * D, D), jnp.float32) * 0.02, 'in_proj_b': jnp.zeros((3 * D,), jnp.float32), 'out_w': jax.random.normal(ks[9], (D, D), jnp.float32) * 0.02, 'out_b': jnp.zeros((D,), jnp.float32)}
        return inp
    _L1_attn_in = _L1_attn_setup()

    def _L1_ffn_setup():
        import jax, jax.numpy as jnp
        import numpy as np
        EPS = 1e-12

        def _l2norm(v):
            n = jnp.sqrt(jnp.sum(v * v, axis=-1, keepdims=True))
            return v / jnp.maximum(n, EPS)
        key = jax.random.key(seed)
        ks = jax.random.split(key, 6)
        B, S, D, F, E = (2, 256, 128, 512, 8)
        std = 0.02
        return {'x': jax.random.normal(ks[0], (B, S, D), jnp.float32), 'Wp': jax.random.normal(ks[1], (D, D), jnp.float32) * (1.0 / np.sqrt(D)), 'sim_matrix': jax.random.normal(ks[2], (E, D), jnp.float32) * std, 'temperature': jnp.asarray(1.0, jnp.float32), 'W1': jax.random.normal(ks[3], (E, D, F), jnp.float32) * (1.0 / np.sqrt(D)), 'b1': jnp.zeros((E, F), jnp.float32), 'W2': jax.random.normal(ks[4], (E, F, D), jnp.float32) * (1.0 / np.sqrt(F)), 'b2': jnp.zeros((E, D), jnp.float32)}
    _L1_ffn_in = _L1_ffn_setup()
    _d = {'L0_attn_x': _L0_attn_in['x'], 'L0_attn_Wqkv': _L0_attn_in['Wqkv'], 'L0_attn_Wproj': _L0_attn_in['Wproj'], 'L0_attn_bproj': _L0_attn_in['bproj'], 'L0_ffn_Wg': _L0_ffn_in['Wg'], 'L0_ffn_W1': _L0_ffn_in['W1'], 'L0_ffn_b1': _L0_ffn_in['b1'], 'L0_ffn_W2': _L0_ffn_in['W2'], 'L0_ffn_b2': _L0_ffn_in['b2'], 'L1_attn_rope_cos': _L1_attn_in['rope_cos'], 'L1_attn_rope_sin': _L1_attn_in['rope_sin'], 'L1_attn_delta_decay': _L1_attn_in['delta_decay'], 'L1_attn_gate_w': _L1_attn_in['gate_w'], 'L1_attn_gate_b': _L1_attn_in['gate_b'], 'L1_attn_phi_res': _L1_attn_in['phi_res'], 'L1_attn_ln1_w': _L1_attn_in['ln1_w'], 'L1_attn_ln2_w': _L1_attn_in['ln2_w'], 'L1_attn_w1': _L1_attn_in['w1'], 'L1_attn_b1': _L1_attn_in['b1'], 'L1_attn_w2': _L1_attn_in['w2'], 'L1_attn_b2': _L1_attn_in['b2'], 'L1_attn_in_proj_w': _L1_attn_in['in_proj_w'], 'L1_attn_in_proj_b': _L1_attn_in['in_proj_b'], 'L1_attn_out_w': _L1_attn_in['out_w'], 'L1_attn_out_b': _L1_attn_in['out_b'], 'L1_ffn_Wp': _L1_ffn_in['Wp'], 'L1_ffn_sim_matrix': _L1_ffn_in['sim_matrix'], 'L1_ffn_temperature': _L1_ffn_in['temperature'], 'L1_ffn_W1': _L1_ffn_in['W1'], 'L1_ffn_b1': _L1_ffn_in['b1'], 'L1_ffn_W2': _L1_ffn_in['W2'], 'L1_ffn_b2': _L1_ffn_in['b2']}
    _x0 = _d['L0_attn_x']
    _d['L0_attn_x'] = jax.random.normal(jax.random.fold_in(jax.random.key(seed), 1), (16, 256, 128), dtype=_x0.dtype)
    del _x0
    return _d

def reference(L0_attn_x, L0_attn_Wqkv, L0_attn_Wproj, L0_attn_bproj, L0_ffn_Wg, L0_ffn_W1, L0_ffn_b1, L0_ffn_W2, L0_ffn_b2, L1_attn_rope_cos, L1_attn_rope_sin, L1_attn_delta_decay, L1_attn_gate_w, L1_attn_gate_b, L1_attn_phi_res, L1_attn_ln1_w, L1_attn_ln2_w, L1_attn_w1, L1_attn_b1, L1_attn_w2, L1_attn_b2, L1_attn_in_proj_w, L1_attn_in_proj_b, L1_attn_out_w, L1_attn_out_b, L1_ffn_Wp, L1_ffn_sim_matrix, L1_ffn_temperature, L1_ffn_W1, L1_ffn_b1, L1_ffn_W2, L1_ffn_b2):

    def _L0_attn_ref(x, Wqkv, Wproj, bproj):
        import jax, jax.numpy as jnp
        import numpy as np
        N_HEADS = 16
        SCALE = 8.0
        b, n, _ = x.shape
        qkv = jnp.einsum('bnm,fm->bnf', x, Wqkv)
        qkv = qkv.reshape(b, n, N_HEADS, -1)
        dh = qkv.shape[3] // 3
        q, k, v = (qkv[..., :dh], qkv[..., dh:2 * dh], qkv[..., 2 * dh:])
        scores = jnp.einsum('bnhd,bngd->bnhg', q, k) / SCALE
        attn = jax.nn.softmax(scores, axis=-1)
        out = jnp.einsum('bnhg,bngd->bnhd', attn, v)
        out = out.reshape(b, n, -1)
        return jnp.einsum('bni,mi->bnm', out, Wproj) + bproj

    def _L0_ffn_ref(x, Wg, W1, b1, W2, b2):
        import jax, jax.numpy as jnp
        import numpy as np
        HIDDEN = 128
        INTER = 512
        N_EXPERTS = 8
        TOP_K = 2
        INIT_STD = 0.02
        orig_shape = x.shape
        xt = x.reshape(-1, HIDDEN)
        T = xt.shape[0]
        logits = xt @ Wg.T
        topk_logits, topk_idx = jax.lax.top_k(logits, TOP_K)
        w = jax.nn.softmax(topk_logits, axis=-1)
        rows = jnp.arange(T)[:, None]
        gates = jnp.zeros((T, N_EXPERTS), xt.dtype).at[rows, topk_idx].add(w)
        h = jnp.einsum('th,ehi->tei', xt, W1) + b1
        h = jax.nn.gelu(h, approximate=False)
        o = jnp.einsum('tei,eih->teh', h, W2) + b2
        y = jnp.einsum('te,teh->th', gates, o)
        return y.reshape(orig_shape)

    def _L1_attn_ref(x, rope_cos, rope_sin, delta_decay, gate_w, gate_b, phi_res, ln1_w, ln2_w, w1, b1, w2, b2, in_proj_w, in_proj_b, out_w, out_b):
        import jax, jax.numpy as jnp
        import numpy as np
        N_STREAMS = 8
        DIM = 128
        N_HEADS = 16
        HEAD_DIM = DIM // N_HEADS
        STREAM_DIM = DIM // N_STREAMS
        EPS = 1e-06

        def delta_operator(x, decay_logits):
            beta = jax.nn.sigmoid(decay_logits)

            def step(s, xt):
                out = xt - s
                s_new = beta * s + (1.0 - beta) * xt
                return (s_new, out)
            xT = jnp.swapaxes(x, 0, 1)
            s0 = jnp.zeros_like(xT[0])
            _, ysT = jax.lax.scan(step, s0, xT)
            return jnp.swapaxes(ysT, 0, 1)

        def rms_norm(x, w):
            var = jnp.mean(x * x, axis=-1, keepdims=True)
            return x * jax.lax.rsqrt(var + EPS) * w

        def sinkhorn_knopp(phi, iterations=15):
            K = jnp.exp(phi)
            for _ in range(iterations):
                K = K / jnp.sum(K, axis=1, keepdims=True)
                K = K / jnp.sum(K, axis=0, keepdims=True)
            return K

        def causal_mha(x, in_proj_w, in_proj_b, out_w, out_b):
            B, S, D = x.shape
            qkv = x @ in_proj_w.T + in_proj_b
            q, k, v = jnp.split(qkv, 3, axis=-1)

            def heads(t):
                return t.reshape(B, S, N_HEADS, HEAD_DIM).transpose(0, 2, 1, 3)
            q, k, v = (heads(q), heads(k), heads(v))
            scores = jnp.einsum('bhqd,bhkd->bhqk', q, k) / jnp.sqrt(jnp.float32(HEAD_DIM))
            mask = jnp.tril(jnp.ones((S, S), bool))
            scores = jnp.where(mask, scores, jnp.float32(-1000000000.0))
            attn = jax.nn.softmax(scores, axis=-1)
            o = jnp.einsum('bhqk,bhkd->bhqd', attn, v)
            o = o.transpose(0, 2, 1, 3).reshape(B, S, D)
            return o @ out_w.T + out_b
        B, S, D = x.shape
        n = N_STREAMS
        x_delta = delta_operator(x, delta_decay)
        x_state = jnp.mean(x_delta, axis=1)
        gates = x_state @ gate_w.T + gate_b
        g_res = jax.nn.sigmoid(gates[:, 2 * n:])[:, None, :, None]
        H_res = sinkhorn_knopp(phi_res, 15)
        x_streams = x_delta.reshape(B, S, n, STREAM_DIM)
        mhc_out = jnp.einsum('bsnd,mn->bsmd', x_streams * g_res, H_res).reshape(B, S, D)
        normed = rms_norm(x_delta, ln1_w)
        attn_out = causal_mha(normed, in_proj_w, in_proj_b, out_w, out_b)
        normed2 = rms_norm(x_delta + attn_out, ln2_w)
        h = jax.nn.gelu(normed2 @ w1.T + b1, approximate=False)
        ffn_out = h @ w2.T + b2
        return x_delta + attn_out + ffn_out + mhc_out

    def _L1_ffn_ref(x, Wp, sim_matrix, temperature, W1, b1, W2, b2):
        import jax, jax.numpy as jnp
        import numpy as np
        EPS = 1e-12

        def _l2norm(v):
            n = jnp.sqrt(jnp.sum(v * v, axis=-1, keepdims=True))
            return v / jnp.maximum(n, EPS)
        E = sim_matrix.shape[0]
        top_k = 2
        proj = jnp.einsum('bsd,ed->bse', x, Wp)
        pn = _l2norm(proj)
        sn = _l2norm(sim_matrix)
        gate_scores = jnp.einsum('bsd,ed->bse', pn, sn) / temperature
        top_v, top_i = jax.lax.top_k(gate_scores, top_k)
        gate_probs = jax.nn.softmax(top_v, axis=-1)
        comb = jnp.sum(jax.nn.one_hot(top_i, E, dtype=x.dtype) * gate_probs[..., None], axis=-2)
        h = jax.nn.gelu(jnp.einsum('bsd,edf->ebsf', x, W1) + b1[:, None, None, :], approximate=False)
        eo = jnp.einsum('ebsf,efd->ebsd', h, W2) + b2[:, None, None, :]
        out = jnp.einsum('ebsd,bse->bsd', eo, comb)
        return out
    x = L0_attn_x
    x = x + _L0_attn_ref(_layernorm(x, axis=-1), L0_attn_Wqkv, L0_attn_Wproj, L0_attn_bproj)
    x = x + _L0_ffn_ref(_layernorm(x, axis=-1), L0_ffn_Wg, L0_ffn_W1, L0_ffn_b1, L0_ffn_W2, L0_ffn_b2)
    x = x + _L1_attn_ref(_layernorm(x, axis=-1), L1_attn_rope_cos, L1_attn_rope_sin, L1_attn_delta_decay, L1_attn_gate_w, L1_attn_gate_b, L1_attn_phi_res, L1_attn_ln1_w, L1_attn_ln2_w, L1_attn_w1, L1_attn_b1, L1_attn_w2, L1_attn_b2, L1_attn_in_proj_w, L1_attn_in_proj_b, L1_attn_out_w, L1_attn_out_b)
    x = x + _L1_ffn_ref(_layernorm(x, axis=-1), L1_ffn_Wp, L1_ffn_sim_matrix, L1_ffn_temperature, L1_ffn_W1, L1_ffn_b1, L1_ffn_W2, L1_ffn_b2)
    return x

_drawn_inputs = setup_inputs


def setup_inputs(seed=0):
    import zlib

    import numpy as np

    out = dict(_drawn_inputs(seed))
    spreads = {'L0_ffn_b1': (0.0, 0.269),
     'L0_ffn_b2': (0.0, 0.1),
     'L1_attn_gate_b': (0.0, 0.553),
     'L1_attn_ln1_w': (1.0, 0.6),
     'L1_attn_ln2_w': (1.0, 0.6),
     'L1_attn_b1': (0.0, 0.1),
     'L1_attn_b2': (0.0, 0.1),
     'L1_attn_in_proj_b': (0.0, 0.1),
     'L1_attn_out_b': (0.0, 0.1),
     'L1_ffn_b1': (0.0, 0.374),
     'L1_ffn_b2': (0.0, 0.1)}
    factors = {'L0_attn_bproj': 3.766,
     'L1_attn_delta_decay': 6.495,
     'L1_attn_gate_w': 200.0,
     'L1_attn_phi_res': 7.146,
     'L1_attn_in_proj_w': 8.0}
    for name, (base, spread) in spreads.items():
        noise = np.random.default_rng([zlib.crc32(name.encode()), seed]).standard_normal(out[name].shape)
        drawn = base * np.exp(spread * noise) if base else spread * noise
        out[name] = jnp.asarray(drawn.astype(out[name].dtype))
    for name, factor in factors.items():
        out[name] = (out[name] * factor).astype(out[name].dtype)
    return out
```

```python
from contextlib import ExitStack, contextmanager

import concourse.bass as bass
from concourse import mybir

P = 128
ALU = mybir.AluOpType
ACT = mybir.ActivationFunctionType
AX = mybir.AxisListType
F32 = mybir.dt.float32
BF16 = mybir.dt.bfloat16
U32 = mybir.dt.uint32

B, S, D = 16, 256, 128
T = B * S // P
H, DH = 16, 8
E, F = 8, 512
FC = F // P
NS, SD = 8, 16
LN_EPS, RMS_EPS, L2_EPS = 1e-5, 1e-6, 1e-12
SINKHORN = 15
EULER = 2.718281828459045

QKV0, PROJ0, IN1, OUT1, FF1, WP1, FF2, GATE1, VECS = 0, 3, 4, 7, 8, 12, 13, 17, 18
SLOTS = 20
V_B1A, V_B1B, V_FB1, V_LN1, V_LN2, V_DECAY, V_BQ, V_BK, NVEC = 0, 32, 64, 68, 69, 70, 71, 72, 73
R_PROJ, R_OUT, R_V, R_FB2 = range(4)

PADS = P
REGION = T * P + PADS
TOPK = 2
XT = T * TOPK + E
ROW = D + 2
NROWS = E * REGION + E * P
NRES = TOPK * T * P + 2 * E * P
ROUND = 8388608.0


def after(eng, sem, t, back=0, per=1):
    n = (t + 1 - back) * per
    if isinstance(n, int) and n <= 0:
        return
    eng.wait_ge(sem, n)


def apart(eng, t):
    if not isinstance(t, int):
        eng.nop(nofuse=True)


def pipeline(eng, tiles, stages, most, start=2, ring=2):

    def step(s, par):
        for f, a in stages:
            if isinstance(s, int) and not 0 <= s + a < tiles:
                continue
            f(s + a, (par + a) % ring)

    for s in range(-most, start):
        step(s, s % ring)
    bodies = (tiles - most - start) // ring
    with eng.Fori(0, bodies) as i:
        for k in range(ring):
            step(i * ring + (start + k), (start + k) % ring)
    end = start + ring * bodies
    for s in range(end, tiles):
        step(s, s % ring)


@contextmanager
def semaphores(nc):
    used = []

    def sem(name):
        used.append(nc.alloc_semaphore(name=name))
        return used[-1]

    yield sem
    with nc.Block() as block:
        @block.gpsimd
        def _(pool):
            numbers = sorted(handle.num for handle in used)
            first = 0
            for i in range(1, len(numbers) + 1):
                if i == len(numbers) or numbers[i] != numbers[i - 1] + 1:
                    pool.sem_clear(range(numbers[first], numbers[i - 1] + 1))
                    first = i
    for handle in used:
        nc.release_semaphore(handle)


class Core:
    pass


def load_and_prepare(nc, ctx, c, a):
    def sb(name, shape, dt=F32):
        return ctx.enter_context(nc.sbuf_tensor(name, shape, dt))

    keep = ctx.enter_context(semaphores(nc))

    c.x = sb("x", [P, T * D])
    c.wT = sb("wT", [P, SLOTS, P])
    c.rows = sb("rows", [1, 4, D])
    c.ones = sb("ones", [1, P])
    c.ident = sb("ident", [P, P])
    c.identb = sb("identb", [P, P], BF16)
    c.neghalf = sb("neghalf", [P, 4])
    c.negone = sb("negone", [P, 4])
    c.onesc = sb("onesc", [P, 2])
    c.euler = sb("euler", [P, 4])
    c.iota8 = sb("iota8", [P, E])
    c.wgT = sb("wgT", [P, E])
    c.snT = sb("snT", [P, E])
    c.itemp = sb("itemp", [P, 1])
    c.omb = sb("omb", [P, 1])
    c.beta = sb("beta", [P, 1])
    c.ngb = sb("ngb", [P, 1])
    c.hbig = sb("hbig", [P, P])
    c.w_in = keep("w_in")
    c.x_in = keep("x_in")

    c.before = sb("before", [P, P], BF16)
    c.onesb = sb("onesb", [P, P], BF16)
    c.region = sb("region", [P, E])
    c.padrow = sb("padrow", [P, E, ROW])
    c.rows_x = nc.dram_tensor("rows_x", (NROWS, ROW), F32, kind="Internal").ap()
    c.res = nc.dram_tensor("res", (NRES, D), F32, kind="Internal").ap()
    c.spare_out = keep("spare_out")

    with ExitStack() as tmp:
        sem = tmp.enter_context(semaphores(nc))

        def tb(name, shape, dt=F32):
            return tmp.enter_context(nc.sbuf_tensor(name, shape, dt))

        wnat = tb("wnat", [P, SLOTS, P])
        wg = tb("wg", [E, D])
        sim = tb("sim", [E, D])
        simq = tb("simq", [E, D])
        sn = tb("sn", [E, D])
        nrm = tb("nrm", [E, 4])
        gb = tb("gb", [NS, 1])
        phi = tb("phi", [NS, NS])
        k0 = tb("k0", [NS, NS])
        k0T = tb("k0T", [NS, NS])
        rc = tb("rc", [NS, 2])
        hr = tb("hr", [NS, NS])
        hTe = tb("hTe", [NS, NS, SD])
        esel = tb("esel", [NS, NS, SD])
        dsel = tb("dsel", [SD, NS, SD])
        dmask = tb("dmask", [P, P])
        edec = tb("edec", [P, 2])
        tempr = tb("tempr", [P, 1])
        spare = tb("spare", [P, E, ROW])
        padded = sem("padded")
        wps = [tmp.enter_context(nc.psum_tensor(f"wps{i}", [P, 512], F32)) for i in range(2)]
        sps = tmp.enter_context(nc.psum_tensor("sps", [P, 512], F32))
        mps = tmp.enter_context(nc.psum_tensor("mps", [P, 512], F32))
        zeroed, made, consts = sem("zeroed"), sem("made"), sem("consts")
        turned, kept = sem("turned"), sem("kept")
        s_small, small_kept = sem("s_small"), sem("small_kept")
        simn, expd, matv, scaled, built = sem("simn"), sem("expd"), sem("matv"), sem("scaled"), sem("built")
        NW = 23
        block = tmp.enter_context(nc.Block())

        @block.sync
        def _(sp):
            sp.wait_ge(zeroed, 1)
            def load(dst, src):
                sp.dma_start(dst, src).then_inc(c.w_in, 16)
            load(wnat[:, QKV0:QKV0 + 3, :], a["L0_attn_Wqkv"].rearrange("(s p) d -> p s d", p=P))
            load(wnat[:, PROJ0, :], a["L0_attn_Wproj"])
            load(wnat[:, IN1:IN1 + 3, :], a["L1_attn_in_proj_w"].rearrange("(s p) d -> p s d", p=P))
            load(wnat[:, OUT1, :], a["L1_attn_out_w"])
            load(wnat[:, FF1:FF1 + FC, :], a["L1_attn_w1"].rearrange("(s p) d -> p s d", p=P))
            load(wnat[:, WP1, :], a["L1_ffn_Wp"])
            load(wnat[:, FF2:FF2 + FC, :].rearrange("p s d -> p (s d)"), a["L1_attn_w2"])
            load(wnat[:, GATE1, :], a["L1_attn_gate_w"][2 * NS:3 * NS, :].unsqueeze(1).to_broadcast([NS, SD, D]))
            load(wnat[V_B1A:V_B1A + 32, VECS, :], a["L0_ffn_b1"].rearrange("e (c p) -> (e c) p", p=P))
            load(wnat[V_B1B:V_B1B + 32, VECS, :], a["L1_ffn_b1"].rearrange("e (c p) -> (e c) p", p=P))
            load(wnat[V_FB1:V_FB1 + FC, VECS, :], a["L1_attn_b1"].rearrange("(c p) -> c p", p=P))
            load(wnat[V_BQ:V_BQ + 2, VECS, :], a["L1_attn_in_proj_b"][0:2 * D].rearrange("(c p) -> c p", p=P))
            for row, name in ((V_LN1, "L1_attn_ln1_w"), (V_LN2, "L1_attn_ln2_w"), (V_DECAY, "L1_attn_delta_decay")):
                load(wnat[row:row + 1, VECS, :], a[name].unsqueeze(0))
            load(gb[:, :], a["L1_attn_gate_b"][2 * NS:3 * NS].unsqueeze(1))
            load(c.rows[:, R_PROJ, :], a["L0_attn_bproj"].unsqueeze(0))
            load(c.rows[:, R_OUT, :], a["L1_attn_out_b"].unsqueeze(0))
            load(c.rows[:, R_V, :], a["L1_attn_in_proj_b"][2 * D:3 * D].unsqueeze(0))
            load(c.rows[:, R_FB2, :], a["L1_attn_b2"].unsqueeze(0))
            load(wg[:, :], a["L0_ffn_Wg"])
            load(sim[:, :], a["L1_ffn_sim_matrix"])
            load(phi[:, :], a["L1_attn_phi_res"])

        @block.scalar
        def _(act):
            act.dma_start(c.x[:, :].rearrange("p (t d) -> p t d", d=D),
                          a["L0_attn_x"].rearrange("b (h p) d -> p (b h) d", p=P)).then_inc(c.x_in, 16)
            act.dma_start(tempr[:, :], a["L1_ffn_temperature"].unsqueeze(0).to_broadcast([P, 1])).then_inc(c.w_in, 16)
            act.wait_ge(padded, 2)
            act.dma_start(c.rows_x[E * REGION:NROWS, :].rearrange("(e p) d -> p e d", p=P), spare[:, :, :]
                          ).then_inc(c.spare_out, 16)
            act.wait_ge(c.spare_out, 16)
            act.wait_ge(c.w_in, 16 * (NW + 1))
            nc.scalar.activation(simq[:, :], sim[:, :], ACT.Square, accum_out=nrm[:, 0:1]).then_inc(simn, 1)
            nc.scalar.activation(k0[:, :], phi[:, :], ACT.Exp).then_inc(expd, 1)
            act.wait_ge(kept, SLOTS // 4)
            nc.scalar.activation(edec[:, 0:1], c.wT[:, VECS, V_DECAY:V_DECAY + 1], ACT.Exp, scale=-1.0).then_inc(expd, 1)

        @block.gpsimd
        def _(pool):
            nc.gpsimd.memset(wnat[:, VECS:VECS + 2, :], 0.0).then_inc(zeroed, 1)
            nc.gpsimd.memset(c.ident[:, :], 0.0).then_inc(made, 1)
            nc.gpsimd.memset(esel[:, :, :], 1.0).then_inc(made, 1)
            nc.gpsimd.memset(dsel[:, :, :], 0.0).then_inc(made, 1)
            nc.gpsimd.memset(c.ones[:, :], 1.0).then_inc(consts, 1)
            nc.gpsimd.memset(c.neghalf[:, :], -0.5).then_inc(consts, 1)
            nc.gpsimd.memset(c.negone[:, :], -1.0).then_inc(consts, 1)
            nc.gpsimd.memset(c.onesc[:, :], 1.0).then_inc(consts, 1)
            nc.gpsimd.memset(c.euler[:, :], EULER).then_inc(consts, 1)
            nc.gpsimd.iota(c.iota8[:, :], [[1, E]], base=0, channel_multiplier=0,
                           allow_small_or_imprecise_dtypes=True).then_inc(consts, 1)
            nc.gpsimd.memset(c.onesb[:, :], 1.0).then_inc(consts, 1)
            nc.gpsimd.iota(c.region[:, :], [[REGION, E]], base=0, channel_multiplier=0,
                           allow_small_or_imprecise_dtypes=True).then_inc(consts, 1)
            nc.gpsimd.memset(c.before[:, :], 1.0).then_inc(zeroed, 1)
            for rows in (c.padrow, spare):
                nc.gpsimd.memset(rows[:, :, :], 0.0).then_inc(zeroed, 1)
            pool.wait_ge(zeroed, 4)
            nc.gpsimd.affine_select(out=c.before[:, :], in_=c.before[:, :], compare_op=ALU.is_gt, fill=0.0,
                                    base=0, pattern=[[1, P]], channel_multiplier=-1).then_inc(consts, 1)
            for n, rows in enumerate((c.padrow, spare)):
                nc.gpsimd.iota(rows[:, :, D].bitcast(U32), [[P, E]], base=TOPK * T * P + n * E * P,
                               channel_multiplier=1).then_inc(padded, 1)
            pool.wait_ge(made, 3)
            nc.gpsimd.affine_select(out=c.ident[:, :], in_=c.ident[:, :], compare_op=ALU.not_equal, fill=1.0,
                                    base=0, pattern=[[-1, P]], channel_multiplier=1).then_inc(made, 1)
            nc.gpsimd.affine_select(out=esel[:, :, :], in_=esel[:, :, :], compare_op=ALU.is_equal, fill=0.0,
                                    base=0, pattern=[[-1, NS], [0, SD]], channel_multiplier=1).then_inc(made, 1)
            nc.gpsimd.affine_select(out=dsel[:, :, :], in_=dsel[:, :, :], compare_op=ALU.not_equal, fill=1.0,
                                    base=0, pattern=[[0, NS], [-1, SD]], channel_multiplier=1).then_inc(made, 1)
            pool.wait_ge(made, 6)
            nc.gpsimd.tensor_copy(c.identb[:, :], c.ident[:, :]).then_inc(consts, 1)
            pool.wait_ge(simn, 1)
            pool.wait_ge(consts, 10)
            nc.gpsimd.tensor_scalar(nrm[:, 1:2], nrm[:, 0:1], L2_EPS * L2_EPS, None, ALU.max).then_inc(simn, 1)
            pool.wait_ge(simn, 2)
            nc.gpsimd.tensor_tensor(nrm[:, 2:3], nrm[:, 1:2], c.neghalf[0:E, 0:1], ALU.pow).then_inc(simn, 1)
            pool.wait_ge(simn, 3)
            nc.gpsimd.tensor_scalar(sn[:, :], sim[:, :], nrm[:, 2:3], None, ALU.mult).then_inc(simn, 1)

        @block.tensor
        def _(pe):
            pe.wait_ge(made, 6)
            pe.wait_ge(c.w_in, 16 * (NW + 1))
            for g in range(SLOTS // 4):
                if g >= 2:
                    pe.wait_ge(kept, g - 1)
                for k in range(4):
                    mm = nc.tensor.transpose(wps[g % 2][:, k * P:(k + 1) * P], wnat[:, 4 * g + k, :], c.ident[:, :])
                mm.then_inc(turned, 1)
            nc.tensor.transpose(sps[:, 0:E], wg[:, :], c.ident[0:E, 0:E])
            pe.wait_ge(simn, 4)
            nc.tensor.transpose(sps[:, E:2 * E], sn[:, :], c.ident[0:E, 0:E])
            pe.wait_ge(expd, 1)
            nc.tensor.transpose(sps[0:NS, 16:16 + NS], k0[:, :], c.ident[0:NS, 0:NS]).then_inc(s_small, 1)
            pe.wait_ge(small_kept, 2)
            with pe.Fori(0, SINKHORN) as i:
                pe.wait_ge(scaled, 2 * i + 1)
                apart(pe, i)
                nc.tensor.matmul(mps[0:NS, 0:1], k0T[:, :], rc[:, 1:2], start=True, stop=True).then_inc(matv, 1)
                pe.wait_ge(scaled, 2 * i + 2)
                apart(pe, i)
                nc.tensor.matmul(mps[0:NS, 0:1], k0[:, :], rc[:, 0:1], start=True, stop=True).then_inc(matv, 1)
            pe.wait_ge(built, 1)
            nc.tensor.transpose(sps[0:NS, 64:64 + NS], hr[:, :], c.ident[0:NS, 0:NS]).then_inc(s_small, 1)
            pe.wait_ge(built, 2)
            nc.tensor.matmul(mps[:, 0:P], esel[:, :, :].rearrange("n a b -> n (a b)"),
                             hTe[:, :, :].rearrange("n a b -> n (a b)"), start=True, stop=True).then_inc(s_small, 1)
            nc.tensor.matmul(wps[0][:, 0:P], dsel[:, :, :].rearrange("n a b -> n (a b)"),
                             dsel[:, :, :].rearrange("n a b -> n (a b)"), start=True, stop=True).then_inc(s_small, 1)
            nc.tensor.matmul(sps[:, 96:97], esel[:, :, :].rearrange("n a b -> n (a b)"), gb[:, :], start=True,
                             stop=True).then_inc(s_small, 1)

        @block.vector
        def _(dve):
            for g in range(SLOTS // 4):
                dve.wait_ge(turned, g + 1)
                nc.vector.tensor_copy(c.wT[:, 4 * g:4 * g + 4, :].rearrange("p s d -> p (s d)"),
                                      wps[g % 2][:, :]).then_inc(kept, 1)
            dve.wait_ge(s_small, 1)
            nc.vector.tensor_copy(c.wgT[:, :], sps[:, 0:E]).then_inc(small_kept, 1)
            nc.vector.tensor_copy(c.snT[:, :], sps[:, E:2 * E]).then_inc(consts, 1)
            nc.vector.tensor_copy(k0T[:, :], sps[0:NS, 16:16 + NS]).then_inc(small_kept, 1)
            nc.vector.memset(rc[:, 1:2], 1.0).then_inc(scaled, 1)
            with dve.Fori(0, SINKHORN) as i:
                dve.wait_ge(matv, 2 * i + 1)
                nc.vector.reciprocal(rc[:, 0:1], mps[0:NS, 0:1]).then_inc(scaled, 1)
                dve.wait_ge(matv, 2 * i + 2)
                nc.vector.reciprocal(rc[:, 1:2], mps[0:NS, 0:1]).then_inc(scaled, 1)
            dve.wait_ge(scaled, 2 * SINKHORN + 1)
            nc.vector.tensor_scalar(hr[:, :], k0[:, :], rc[:, 0:1], None, ALU.mult).then_inc(built, 1)
            dve.wait_ge(s_small, 2)
            nc.vector.tensor_scalar(hTe[:, :, :], sps[0:NS, 64:64 + NS].unsqueeze(2).to_broadcast([NS, NS, SD]),
                                    rc[:, 1:2], None, ALU.mult).then_inc(built, 1)
            dve.wait_ge(s_small, 4)
            nc.vector.tensor_copy(dmask[:, :], wps[0][:, 0:P]).then_inc(built, 1)
            dve.wait_ge(built, 3)
            nc.vector.tensor_tensor(c.hbig[:, :], mps[:, 0:P], dmask[:, :], ALU.mult).then_inc(consts, 1)
            nc.vector.reciprocal(c.itemp[:, :], tempr[:, :]).then_inc(consts, 1)
            dve.wait_ge(expd, 2)
            nc.vector.tensor_scalar(edec[:, 1:2], edec[:, 0:1], 1.0, None, ALU.add).then_inc(built, 1)
            dve.wait_ge(built, 4)
            nc.vector.reciprocal(c.beta[:, :], edec[:, 1:2]).then_inc(built, 1)
            dve.wait_ge(built, 5)
            nc.vector.tensor_scalar(c.omb[:, :], c.beta[:, :], -1.0, 1.0, ALU.mult, ALU.add).then_inc(consts, 1)
            dve.wait_ge(s_small, 5)
            nc.vector.tensor_scalar(c.ngb[:, :], sps[:, 96:97], -1.0, None,
                                    ALU.mult).then_inc(consts, 1)


class Router:

    def __init__(self, nc, c, name, similarity):
        self.nc, self.c, self.name, self.similarity = nc, c, name, similarity

    def open(self, nc, ctx, x_ready):
        name = self.name
        self.x_ready = x_ready
        named = ctx.enter_context(semaphores(nc))

        def pair(what, shape, dt=F32):
            return [ctx.enter_context(nc.sbuf_tensor(f"{name}_{what}{u}", shape, dt)) for u in range(2)]

        def sem(what):
            return named(f"{name}_{what}")

        self.st, self.mv, self.ve, self.rstd = (pair("st", [P, 6]), pair("mv", [P, 2]), pair("ve", [P, 1]),
                                                pair("rstd", [P, 1]))
        self.row = [pair("rowa", [P, ROW]), pair("rowb", [P, ROW])]
        self.rT = pair("rT", [P, P])
        self.m8, self.ix, self.ixf = pair("m8", [P, 8]), pair("ix", [P, 8], U32), pair("ixf", [P, 2])
        self.hot = [pair("hota", [P, E]), pair("hotb", [P, E])]
        self.mask, self.cum = pair("mask", [P, E], BF16), pair("cum", [P, E], BF16)
        self.lg = pair("lg", [P, E])
        self.pf, self.junk, self.pk, self.idx = (pair("pf", [P, E]), pair("junk", [P, TOPK * E]), pair("pk", [P, 2]),
                                                 pair("idx", [P, 2], U32))
        self.gd, self.g1, self.gs, self.gr = (pair("gd", [P, 1]), pair("g1", [P, 1]), pair("gs", [P, 1]),
                                              pair("gr", [P, 1]))
        self.ids = ctx.enter_context(nc.sbuf_tensor(f"{name}_ids", [P, 2], F32))
        self.ps_turn = ctx.enter_context(nc.psum_tensor(f"{name}_pt", [P, 512], F32))
        self.ps_log = ctx.enter_context(nc.psum_tensor(f"{name}_pl", [P, 512], F32))
        self.s = {s: sem(s) for s in ("bn", "stats", "ve", "rstd", "rows", "turned", "kept", "logit", "lgd", "top", "index", "indexf",
                  "hots", "masks", "cums", "pos", "pfd", "pkd", "idxd", "gdd", "g1d", "gsd", "grd", "gated", "idw",
                  "idn", "begun", "projd", "projk", "sqd", "ssd", "ssm", "rnd")}
        self.s["sent"] = nc.alloc_semaphore(name=f"{name}_sent")
        if self.similarity:
            self.pjT, self.sq = pair("pjT", [P, P]), pair("sq", [P, P])
            self.ssk, self.ssx, self.rn = pair("ssk", [P, 1]), pair("ssx", [P, 1]), pair("rn", [P, 1])

    def x_of(self, t):
        return self.c.x[:, bass.ds(t * D, D)]

    def statistics(self, dve):
        nc = self.nc

        def stage(t, u):
            after(dve, self.x_ready, t)
            apart(dve, t)
            nc.vector.bn_stats(self.st[u][:, :], self.x_of(t)).then_inc(self.s["bn"], 1)
            after(dve, self.s["bn"], t)
            after(dve, self.s["ve"], t, back=2)
            apart(dve, t)
            nc.vector.bn_aggr(self.mv[u][:, :], self.st[u][:, :]).then_inc(self.s["stats"], 1)
        return stage

    def normalise(self, dve):
        nc = self.nc

        def stage(t, u):
            after(dve, self.s["rstd"], t)
            after(dve, self.s["sent"], t, back=2, per=32)
            for k in range(TOPK):
                nc.vector.tensor_scalar(self.row[k][u][:, 0:D], self.x_of(t), self.mv[u][:, 0:1],
                                        self.rstd[u][:, 0:1], ALU.subtract, ALU.mult).then_inc(self.s["rows"], 1)
        return stage

    def select(self, dve):
        nc, c = self.nc, self.c

        def stage(t, u):
            after(dve, self.s["logit"], t)
            after(dve, self.s["gdd"], t, back=2)
            if self.similarity:
                after(dve, self.s["rnd"], t)
                nc.vector.tensor_scalar(self.lg[u][:, :], self.ps_log[:, 0:E], self.rn[u][:, 0:1], c.itemp[:, 0:1],
                                        ALU.mult, ALU.mult).then_inc(self.s["lgd"], 1)
            else:
                nc.vector.tensor_copy(self.lg[u][:, :], self.ps_log[:, 0:E]).then_inc(self.s["lgd"], 1)
            after(dve, self.s["lgd"], t)
            apart(dve, t)
            nc.vector.max(self.m8[u][:, :], self.lg[u][:, :]).then_inc(self.s["top"], 1)
            after(dve, self.s["top"], t)
            apart(dve, t)
            nc.vector.max_index(self.ix[u][:, :], self.m8[u][:, :], self.lg[u][:, :]).then_inc(self.s["index"], 1)
            after(dve, self.s["index"], t)
            nc.vector.tensor_copy(self.ixf[u][:, :], self.ix[u][:, 0:2]).then_inc(self.s["indexf"], 1)
            after(dve, self.s["indexf"], t)
            for k in range(TOPK):
                nc.vector.tensor_scalar(self.hot[k][u][:, :], c.iota8[:, :], self.ixf[u][:, k:k + 1], None,
                                        ALU.is_equal).then_inc(self.s["hots"], 1)
            after(dve, self.s["hots"], t, per=TOPK)
            after(dve, self.s["pos"], t, back=1)
            nc.vector.tensor_tensor(self.mask[u][:, :], self.hot[0][u][:, :], self.hot[1][u][:, :],
                                    ALU.add).then_inc(self.s["masks"], 1)
            after(dve, self.s["masks"], t)
            if isinstance(t, int) and t == 0:
                nc.vector.memset(self.cum[1][:, :], 0.0).then_inc(self.s["begun"], 1)
                dve.wait_ge(self.s["begun"], 1)
            else:
                after(dve, self.s["cums"], t, back=1)
            nc.vector.tensor_tensor(self.cum[u][:, :], self.cum[1 - u][:, :], self.mask[u][:, :],
                                    ALU.add).then_inc(self.s["cums"], 1)
        return stage

    def place(self, dve):
        nc, c = self.nc, self.c

        def stage(t, u):
            after(dve, self.s["pos"], t)
            nc.vector.tensor_tensor(self.pf[u][:, :], self.ps_log[:, 16:16 + E], c.region[:, :],
                                    ALU.add).then_inc(self.s["pfd"], 1)
            after(dve, self.s["pfd"], t)
            for k in range(TOPK):
                nc.vector.scalar_tensor_tensor(out=self.junk[u][:, k * E:(k + 1) * E], in0=self.hot[k][u][:, :], scalar=1.0,
                                               in1=self.pf[u][:, :], op0=ALU.mult, op1=ALU.mult,
                                               accum_out=self.pk[u][:, k:k + 1]).then_inc(self.s["pkd"], 1)
            after(dve, self.s["pkd"], t, per=TOPK)
            nc.vector.tensor_copy(self.idx[u][:, :], self.pk[u][:, :]).then_inc(self.s["idxd"], 1)
        return stage

    def root(self, pool):
        nc, c = self.nc, self.c

        def stage(t, u):
            after(pool, self.s["stats"], t)
            apart(pool, t)
            nc.gpsimd.tensor_scalar(self.ve[u][:, :], self.mv[u][:, 1:2], LN_EPS, None, ALU.add).then_inc(self.s["ve"], 1)
            after(pool, self.s["ve"], t)
            after(pool, self.s["rows"], t, back=2, per=TOPK)
            nc.gpsimd.tensor_tensor(self.rstd[u][:, :], self.ve[u][:, :], c.neghalf[:, 0:1],
                                    ALU.pow).then_inc(self.s["rstd"], 1)
        return stage

    def inverse_norm(self, pool):
        nc, c = self.nc, self.c

        def stage(t, u):
            after(pool, self.s["ssm"], t)
            apart(pool, t)
            nc.gpsimd.tensor_scalar(self.ssx[u][:, :], self.ssk[u][:, :], L2_EPS * L2_EPS, None,
                                    ALU.max).then_inc(self.s["ssd"], 1)
            after(pool, self.s["ssd"], t)
            after(pool, self.s["lgd"], t, back=2)
            nc.gpsimd.tensor_tensor(self.rn[u][:, :], self.ssx[u][:, :], c.neghalf[:, 0:1],
                                    ALU.pow).then_inc(self.s["rnd"], 1)
        return stage

    def gates(self, pool):
        nc, c = self.nc, self.c

        def stage(t, u):
            if isinstance(t, int) and t == 0:
                nc.gpsimd.iota(self.ids[:, :], [[T * P, TOPK]], base=0, channel_multiplier=1,
                               allow_small_or_imprecise_dtypes=True).then_inc(self.s["idn"], 1)
            after(pool, self.s["idn"], t)
            after(pool, self.s["rows"], t, per=TOPK)
            apart(pool, t)
            for k in range(TOPK):
                nc.gpsimd.tensor_copy(self.row[k][u][:, D:D + 1].bitcast(U32),
                                      self.ids[:, k:k + 1]).then_inc(self.s["idw"], 1)
            after(pool, self.s["idw"], t, per=TOPK)
            apart(pool, t)
            nc.gpsimd.tensor_scalar(self.ids[:, :], self.ids[:, :], float(P), None, ALU.add).then_inc(self.s["idn"], 1)
            after(pool, self.s["top"], t)
            nc.gpsimd.tensor_tensor(self.gd[u][:, :], self.m8[u][:, 1:2], self.m8[u][:, 0:1],
                                    ALU.subtract).then_inc(self.s["gdd"], 1)
            after(pool, self.s["gdd"], t)
            nc.gpsimd.tensor_tensor(self.g1[u][:, :], c.euler[:, 0:1], self.gd[u][:, :], ALU.pow).then_inc(self.s["g1d"], 1)
            after(pool, self.s["g1d"], t)
            apart(pool, t)
            nc.gpsimd.tensor_scalar(self.gs[u][:, :], self.g1[u][:, :], 1.0, None, ALU.add).then_inc(self.s["gsd"], 1)
            after(pool, self.s["gsd"], t)
            nc.gpsimd.tensor_tensor(self.row[0][u][:, D + 1:D + 2], self.gs[u][:, :], c.negone[:, 0:1],
                                    ALU.pow).then_inc(self.s["grd"], 1)
            after(pool, self.s["grd"], t)
            nc.gpsimd.tensor_tensor(self.row[1][u][:, D + 1:D + 2], self.g1[u][:, :], self.row[0][u][:, D + 1:D + 2],
                                    ALU.mult).then_inc(self.s["gated"], 1)
        return stage

    def send(self, pool):
        nc, c = self.nc, self.c

        def stage(t, u):
            after(pool, self.s["gated"], t)
            after(pool, self.s["idxd"], t)
            apart(pool, t)
            for k in range(TOPK):
                pool.indirect_dma_start(out=c.rows_x, out_offset=bass.IndirectOffsetOnAxis(
                    ap=self.idx[u][:, k:k + 1], axis=0), in_=self.row[k][u][:, :], in_offset=None
                ).then_inc(self.s["sent"], 16)
        return stage

    def sent_all(self, pool):
        pool.wait_ge(self.s["sent"], 32 * T)

    def keep_turned(self, act):
        nc = self.nc

        def stage(t, u):
            after(act, self.s["turned"], t)
            after(act, self.s["projd"] if self.similarity else self.s["logit"], t, back=2)
            nc.scalar.copy(self.rT[u][:, :], self.ps_turn[:, 0:P]).then_inc(self.s["kept"], 1)
        return stage

    def keep_projected(self, act):
        nc = self.nc

        def stage(t, u):
            after(act, self.s["projd"], t)
            after(act, self.s["logit"], t, back=2)
            nc.scalar.copy(self.pjT[u][:, :], self.ps_turn[:, P:2 * P]).then_inc(self.s["projk"], 1)
            nc.scalar.activation(self.sq[u][:, :], self.ps_turn[:, P:2 * P], ACT.Square).then_inc(self.s["sqd"], 1)
        return stage

    def keep_squares(self, act):
        nc = self.nc

        def stage(t, u):
            after(act, self.s["logit"], t)
            after(act, self.s["ssd"], t, back=2)
            nc.scalar.copy(self.ssk[u][:, :], self.ps_log[:, E:E + 1]).then_inc(self.s["ssm"], 1)
        return stage

    def turn(self, pe):
        nc, c = self.nc, self.c

        def stage(t, u):
            after(pe, self.s["rows"], t, per=TOPK)
            after(pe, self.s["kept"], t, back=1)
            if self.similarity:
                after(pe, self.s["sqd"], t, back=1)
            nc.tensor.transpose(self.ps_turn[:, 0:P], self.row[0][u][:, 0:D], c.ident[:, :]).then_inc(self.s["turned"], 1)
        return stage

    def project(self, pe):
        nc, c = self.nc, self.c

        def stage(t, u):
            after(pe, self.s["kept"], t)
            after(pe, self.s["sqd"], t, back=1)
            nc.tensor.matmul(self.ps_turn[:, P:2 * P], c.wT[:, WP1, :], self.rT[u][:, :], start=True,
                             stop=True).then_inc(self.s["projd"], 1)
        return stage

    def logits(self, pe):
        nc, c = self.nc, self.c

        def stage(t, u):
            after(pe, self.s["pfd"], t, back=1)
            if self.similarity:
                after(pe, self.s["sqd"], t)
                after(pe, self.s["ssm"], t, back=1)
                nc.tensor.matmul(self.ps_log[:, E:E + 1], self.sq[u][:, :], c.onesc[:, 0:1], start=True, stop=True)
                nc.tensor.matmul(self.ps_log[:, 0:E], self.pjT[u][:, :], c.snT[:, :], start=True,
                                 stop=True).then_inc(self.s["logit"], 1)
            else:
                after(pe, self.s["kept"], t)
                nc.tensor.matmul(self.ps_log[:, 0:E], self.rT[u][:, :], c.wgT[:, :], start=True,
                                 stop=True).then_inc(self.s["logit"], 1)
        return stage

    def positions(self, pe):
        nc, c = self.nc, self.c

        def stage(t, u):
            after(pe, self.s["cums"], t)
            after(pe, self.s["lgd"], t)
            if self.similarity:
                after(pe, self.s["ssm"], t)
            nc.tensor.matmul(self.ps_log[:, 16:16 + E], c.before[:, :], self.mask[u][:, :], start=True, stop=False)
            nc.tensor.matmul(self.ps_log[:, 16:16 + E], c.onesb[:, :], self.cum[1 - u][:, :], start=False,
                             stop=True).then_inc(self.s["pos"], 1)
        return stage

    def finish(self, nc, ctx):
        c, name = self.c, self.name
        named = ctx.enter_context(semaphores(nc))

        def sem(what):
            return named(f"{name}_{what}")

        counted, step, listed, pads = sem("counted"), sem("fstep"), sem("listed"), sem("pads")
        with ExitStack() as tmp:
            def tb(what, shape, dt=F32):
                return tmp.enter_context(nc.sbuf_tensor(f"{name}_{what}", shape, dt))

            cnt, part, nt, ct, one8 = (tb(w, [P, E]) for w in ("cnt", "part", "nt", "ct", "one8"))
            own, padf, padi = tb("own", [P, 1]), tb("padf", [P, E]), tb("padi", [P, E], U32)
            it, reached, starts = tb("it", [1, XT]), tb("reached", [1, XT, E]), tb("starts", [1, XT, E])
            ef, sf, df, rf = (tb(w, [1, XT]) for w in ("ef", "sf", "df", "rf"))
            block = tmp.enter_context(nc.Block())

            @block.tensor
            def _(pe):
                nc.tensor.matmul(self.ps_log[:, 0:E], c.onesb[:, :], self.cum[(T - 1) % 2][:, :], start=True,
                                 stop=True).then_inc(counted, 1)

            @block.vector
            def _(dve):
                n = [0]

                def then(ins):
                    ins.then_inc(step, 1)
                    n[0] += 1
                    dve.wait_ge(step, n[0])

                then(nc.vector.memset(one8[:, :], 1.0))
                dve.wait_ge(counted, 1)
                then(nc.vector.tensor_copy(cnt[:, :], self.ps_log[:, 0:E]))
                then(nc.vector.tensor_scalar(part[:, :], cnt[:, :], 1.0 / P, 63.5 / P, ALU.mult, ALU.add))
                then(nc.vector.tensor_scalar(nt[:, :], part[:, :], ROUND, None, ALU.add))
                then(nc.vector.tensor_scalar(part[:, :], nt[:, :], -ROUND, None, ALU.add))
                then(nc.vector.tensor_tensor_scan(ct[:, :], one8[:, :], part[:, :], 0.0, ALU.mult, ALU.add))
                dve.wait_ge(pads, 2)
                then(nc.vector.scalar_tensor_tensor(out=padf[:, :], in0=cnt[:, :], scalar=own[:, 0:1],
                                                    in1=c.region[:, :], op0=ALU.add, op1=ALU.add))
                nc.vector.tensor_copy(padi[:, :], padf[:, :]).then_inc(listed, 1)
                then(nc.vector.tensor_tensor(reached[:, :, :], it[:, :].unsqueeze(2).to_broadcast([1, XT, E]),
                                             ct[0:1, :].unsqueeze(1).to_broadcast([1, XT, E]), ALU.is_ge))
                then(nc.vector.tensor_tensor(starts[:, :, :], reached[:, :, :],
                                             part[0:1, :].unsqueeze(1).to_broadcast([1, XT, E]), ALU.mult))
                then(nc.vector.tensor_reduce(ef[:, :], reached[:, :, :], AX.X, ALU.add))
                then(nc.vector.tensor_reduce(sf[:, :], starts[:, :, :], AX.X, ALU.add))
                then(nc.vector.tensor_tensor(df[:, :], it[:, :], sf[:, :], ALU.subtract))
                then(nc.vector.scalar_tensor_tensor(out=rf[:, :], in0=ef[:, :], scalar=float(REGION // P),
                                                    in1=df[:, :], op0=ALU.mult, op1=ALU.add))
                nc.vector.tensor_scalar(c.tile_e[:, :], ef[:, :], float(E - 1), None, ALU.min).then_inc(listed, 1)
                nc.vector.tensor_copy(c.tile_r[:, :], rf[:, :]).then_inc(listed, 1)

            @block.gpsimd
            def _(pool):
                nc.gpsimd.iota(own[:, :], [[0, 1]], base=0, channel_multiplier=1,
                               allow_small_or_imprecise_dtypes=True).then_inc(pads, 1)
                nc.gpsimd.iota(it[:, :], [[1, XT]], base=0, channel_multiplier=0,
                               allow_small_or_imprecise_dtypes=True).then_inc(pads, 1)
                pool.wait_ge(listed, 1)
                for e in range(E):
                    pool.indirect_dma_start(out=c.rows_x, out_offset=bass.IndirectOffsetOnAxis(
                        ap=padi[:, e:e + 1], axis=0), in_=c.padrow[:, e, :], in_offset=None).then_inc(self.s["sent"], 16)
                pool.wait_ge(self.s["sent"], 32 * T + 16 * E)


def run_experts(nc, c, name):
    RING = 8
    AHEAD = 6
    with ExitStack() as ctx:
        named = ctx.enter_context(semaphores(nc))

        def ring(what, shape, dt=F32, n=RING):
            return [ctx.enter_context(nc.sbuf_tensor(f"{name}_{what}{u}", shape, dt)) for u in range(n)]

        def banks(what, n=2):
            return [ctx.enter_context(nc.psum_tensor(f"{name}_{what}{u}", [P, 512], F32)) for u in range(n)]

        def sem(what):
            return named(f"{name}_{what}")

        xr, xT, hb = ring("xr", [P, ROW]), ring("xT", [P, P], n=2), ring("hb", [P, F], n=2)
        hg, hT, yb, yo, di = (ring("hg", [P, F], n=2), ring("hT", [P, F], n=2), ring("yb", [P, D], n=2),
                              ring("yo", [P, D]), ring("di", [P, 1], U32))
        ps_x, ps_h, ps_t, ps_y = banks("px", 1), banks("ph"), banks("pt"), banks("py")
        loaded = [sem(f"loaded{u}") for u in range(RING)]
        xTd, xTk, hd, hbd, hgd, hTd, hTk, yd, ybd, yod, did = (
            sem(s) for s in ("xTd", "xTk", "hd", "hbd", "hgd", "hTd", "hTk", "yd", "ybd", "yod", "did"))
        sent = [nc.alloc_semaphore(name=f"{name}_sent{u}") for u in range(RING)]
        rows = c.rows_x.rearrange("(n p) d -> n p d", p=P)
        block = ctx.enter_context(nc.Block())

        def expert_of(eng, i):
            return eng.value_load(c.tile_e[0:1, bass.ds(i, 1)], min_val=0, max_val=E - 1)

        def of_ring(eng, sems, i, u, back=0):
            if not isinstance(i, int):
                eng.wait_ge(sems[u], (i - u) * (16 // RING) + 16 * (1 - back))
            elif i // RING + 1 - back > 0:
                eng.wait_ge(sems[u], 16 * (i // RING + 1 - back))

        @block.sync
        def _(sp):
            def load(i, u):
                after(sp, yod, i, back=RING)
                r = sp.value_load(c.tile_r[0:1, bass.ds(i, 1)], min_val=0, max_val=NROWS // P - 1)
                sp.dma_start(xr[u][:, :], rows[bass.ds(r, 1), :, :].rearrange("n p d -> (n p) d")
                             ).then_inc(loaded[u], 16)

            pipeline(sp, XT, [(load, 6)], AHEAD, start=RING, ring=RING)

        @block.tensor
        def _(pe):
            pe.wait_ge(c.e_in, 64)

            def turn(i, u):
                of_ring(pe, loaded, i, u)
                after(pe, xTk, i, back=1)
                nc.tensor.transpose(ps_x[0][:, 0:P], xr[u][:, 0:D], c.ident[:, :]).then_inc(xTd, 1)

            def up(i, u):
                e = expert_of(pe, i)
                after(pe, xTk, i)
                after(pe, hbd, i, back=2)
                nc.tensor.matmul(ps_h[u % 2][:, :], xT[u % 2][:, :], c.w1[:, bass.ds(e, 1), :], start=True,
                                 stop=True).then_inc(hd, 1)

            def turn_h(i, u):
                after(pe, hgd, i)
                after(pe, hTk, i, back=2)
                for k in range(FC):
                    mm = nc.tensor.transpose(ps_t[u % 2][:, k * P:(k + 1) * P], hg[u % 2][:, k * P:(k + 1) * P],
                                             c.ident[:, :])
                mm.then_inc(hTd, 1)

            def down(i, u):
                e = expert_of(pe, i)
                after(pe, hTk, i)
                after(pe, ybd, i, back=2)
                for k in range(FC):
                    mm = nc.tensor.matmul(ps_y[u % 2][:, 0:D], hT[u % 2][:, k * P:(k + 1) * P],
                                          c.w2[:, bass.ds(e * FC + k, 1), :], start=(k == 0), stop=(k == FC - 1))
                mm.then_inc(yd, 1)

            pipeline(pe, XT, [(up, 2), (down, 0), (turn, 3), (turn_h, 1)], AHEAD, start=RING, ring=RING)

        @block.scalar
        def _(act):
            def keep_x(i, u):
                after(act, xTd, i)
                after(act, hd, i, back=2)
                nc.scalar.copy(xT[u % 2][:, :], ps_x[0][:, 0:P]).then_inc(xTk, 1)

            def gelu(i, u):
                after(act, hbd, i)
                after(act, hTd, i, back=2)
                nc.scalar.activation(hg[u % 2][:, :], hb[u % 2][:, :], ACT.Gelu).then_inc(hgd, 1)

            pipeline(act, XT, [(keep_x, 3), (gelu, 2)], AHEAD, start=RING, ring=RING)

        @block.vector
        def _(dve):
            dve.wait_ge(c.e_in, 64)

            def bias(i, u):
                e = expert_of(dve, i)
                after(dve, hd, i)
                after(dve, hgd, i, back=2)
                nc.vector.tensor_tensor(hb[u % 2][:, :], ps_h[u % 2][:, :], c.b1bc[:, bass.ds(e * F, F)],
                                        ALU.add).then_inc(hbd, 1)

            def keep_h(i, u):
                after(dve, hTd, i)
                after(dve, yd, i, back=2)
                nc.vector.tensor_copy(hT[u % 2][:, :], ps_t[u % 2][:, :]).then_inc(hTk, 1)

            def bias_y(i, u):
                e = expert_of(dve, i)
                after(dve, yd, i)
                after(dve, yod, i, back=2)
                nc.vector.tensor_tensor(yb[u % 2][:, :], ps_y[u % 2][:, 0:D], c.b2bc[:, bass.ds(e * D, D)],
                                        ALU.add).then_inc(ybd, 1)

            pipeline(dve, XT, [(bias, 2), (keep_h, 1), (bias_y, 0)], AHEAD, start=RING, ring=RING)

        @block.gpsimd
        def _(pool):
            def send(i, u):
                of_ring(pool, sent, i, u, back=1)
                of_ring(pool, loaded, i, u)
                apart(pool, i)
                nc.gpsimd.tensor_copy(di[u][:, :], xr[u][:, D:D + 1].bitcast(U32)).then_inc(did, 1)
                after(pool, ybd, i)
                apart(pool, i)
                nc.gpsimd.tensor_scalar(yo[u][:, :], yb[u % 2][:, :], xr[u][:, D + 1:D + 2], None,
                                        ALU.mult).then_inc(yod, 1)
                after(pool, did, i)
                after(pool, yod, i)
                apart(pool, i)
                pool.indirect_dma_start(out=c.res, out_offset=bass.IndirectOffsetOnAxis(ap=di[u][:, 0:1], axis=0),
                                        in_=yo[u][:, :], in_offset=None).then_inc(sent[u], 16)

            pipeline(pool, XT, [(send, 0)], AHEAD, start=RING, ring=RING)
            for u in range(RING):
                pool.wait_ge(sent[u], 16 * XT // RING)


def head_attention(nc, outer, c, r):
    HH, W = H * H, 3 * H * DH
    AHEAD = 4
    x1 = outer.enter_context(semaphores(nc))("a_x1")
    r.open(nc, outer, x1)
    with ExitStack() as ctx:
        def pair(name, shape, dt=F32):
            return [ctx.enter_context(nc.sbuf_tensor(f"a_{name}{u}", shape, dt)) for u in range(2)]

        def banks(name):
            return [ctx.enter_context(nc.psum_tensor(f"a_{name}{u}", [P, 512], F32)) for u in range(2)]

        named = ctx.enter_context(semaphores(nc))

        def sem(name):
            return named("a_" + name)

        st, mv, ve, rstd = pair("st", [P, 6]), pair("mv", [P, 2]), pair("ve", [P, 1]), pair("rstd", [P, 1])
        xn, xnT, qkv = pair("xn", [P, D]), pair("xnT", [P, P]), pair("qkv", [P, W])
        prod = ctx.enter_context(nc.sbuf_tensor("a_prod", [P, HH * DH], F32))
        sc, mx, ss, ex = pair("sc", [P, HH]), pair("mx", [P, H]), pair("ss", [P, HH]), pair("ex", [P, HH])
        sm, rs, pr = pair("sm", [P, H]), pair("rs", [P, H]), pair("pr", [P, HH])
        pv, oT = pair("pv", [P, H, H * DH]), pair("oT", [P, P])
        ps_t1, ps_qkv, ps_o1, ps_p = (ctx.enter_context(nc.psum_tensor("a_t", [P, 512], F32)), banks("q"),
                                      ctx.enter_context(nc.psum_tensor("a_o", [P, 512], F32)), banks("p"))
        ps_t, ps_o = [ps_t1, ps_t1], [ps_o1, ps_o1]
        bn, stats, ved, rstdd, xnd = sem("bn"), sem("stats"), sem("ve"), sem("rstd"), sem("xn")
        xT, xTk, qk, qkk = sem("xT"), sem("xTk"), sem("qk"), sem("qkk")
        prodd, scd, mxd, ssd, exd = sem("prod"), sem("sc"), sem("mx"), sem("ss"), sem("ex")
        smd, rsd, prd, pvd, od, ok, pj = (sem("sm"), sem("rs"), sem("pr"), sem("pv"), sem("o"), sem("ok"),
                                          sem("pj"))
        wqkvT = c.wT[:, QKV0:QKV0 + 3, :].rearrange("p s f -> p (s f)")
        wprojT = c.wT[:, PROJ0, :]
        block = ctx.enter_context(nc.Block())

        def x_of(t):
            return c.x[:, bass.ds(t * D, D)]

        @block.vector
        def _(dve):
            dve.wait_ge(c.x_in, 16)

            def scores(t, u):
                after(dve, qkk, t)
                hd = qkv[u][:, :].rearrange("p (h k) -> p h k", h=H)
                q = hd[:, :, 0:DH].unsqueeze(2).to_broadcast([P, H, H, DH])
                k = hd[:, :, DH:2 * DH].unsqueeze(1).to_broadcast([P, H, H, DH])
                nc.vector.tensor_tensor(prod[:, :].rearrange("p (h g d) -> p h g d", h=H, g=H), q, k,
                                        ALU.mult).then_inc(prodd, 1)
                after(dve, prodd, t)
                nc.vector.tensor_reduce(sc[u][:, :], prod[:, :].rearrange("p (a d) -> p a d", d=DH), AX.X,
                                        ALU.add).then_inc(scd, 1)
                after(dve, scd, t)
                nc.vector.tensor_reduce(mx[u][:, :], sc[u][:, :].rearrange("p (h g) -> p h g", h=H), AX.X,
                                        ALU.max).then_inc(mxd, 1)
                after(dve, mxd, t)
                after(dve, exd, t, back=2)
                nc.vector.tensor_tensor(ss[u][:, :].rearrange("p (h g) -> p h g", h=H),
                                        sc[u][:, :].rearrange("p (h g) -> p h g", h=H),
                                        mx[u][:, :].unsqueeze(2).to_broadcast([P, H, H]),
                                        ALU.subtract).then_inc(ssd, 1)

            def statistics(t, u):
                nc.vector.bn_stats(st[u][:, :], x_of(t)).then_inc(bn, 1)
                after(dve, bn, t)
                after(dve, ved, t, back=2)
                apart(dve, t)
                nc.vector.bn_aggr(mv[u][:, :], st[u][:, :]).then_inc(stats, 1)

            def probabilities(t, u):
                after(dve, exd, t)
                nc.vector.tensor_reduce(sm[u][:, :], ex[u][:, :].rearrange("p (h g) -> p h g", h=H), AX.X,
                                        ALU.add).then_inc(smd, 1)
                after(dve, smd, t)
                nc.vector.reciprocal(rs[u][:, :], sm[u][:, :]).then_inc(rsd, 1)
                after(dve, rsd, t)
                after(dve, pvd, t, back=2)
                nc.vector.tensor_tensor(pr[u][:, :].rearrange("p (h g) -> p h g", h=H),
                                        ex[u][:, :].rearrange("p (h g) -> p h g", h=H),
                                        rs[u][:, :].unsqueeze(2).to_broadcast([P, H, H]),
                                        ALU.mult).then_inc(prd, 1)

            def normalise(t, u):
                after(dve, stats, t)
                after(dve, rstdd, t)
                after(dve, xT, t, back=2)
                nc.vector.tensor_scalar(xn[u][:, :], x_of(t), mv[u][:, 0:1], rstd[u][:, 0:1], ALU.subtract,
                                        ALU.mult).then_inc(xnd, 1)

            def residual(t, u):
                after(dve, pj, t)
                nc.vector.tensor_tensor(x_of(t), ps_p[u][:, 0:D], x_of(t), ALU.add).then_inc(x1, 1)

            pipeline(dve, T, [(scores, 3), (statistics, 4), (r.statistics(dve), 1), (probabilities, 3), (normalise, 4),
                             (r.normalise(dve), 1), (r.select(dve), 0), (residual, 2), (r.place(dve), 0)], AHEAD)

        @block.gpsimd
        def _(pool):
            def weigh(t, u):
                after(pool, prd, t)
                after(pool, qkk, t)
                after(pool, od, t, back=2)
                p_ = pr[u][:, :].rearrange("p (h g) -> p g h", h=H).unsqueeze(3).to_broadcast([P, H, H, DH])
                v = qkv[u][:, :].rearrange("p (g k) -> p g k", g=H)[:, :, 2 * DH:3 * DH]
                v = v.unsqueeze(2).to_broadcast([P, H, H, DH])
                nc.gpsimd.tensor_tensor(pv[u][:, :, :].rearrange("p g (h d) -> p g h d", h=H), p_, v,
                                        ALU.mult).then_inc(pvd, 1)

            def root(t, u):
                after(pool, stats, t)
                apart(pool, t)
                nc.gpsimd.tensor_scalar(ve[u][:, :], mv[u][:, 1:2], LN_EPS, None, ALU.add).then_inc(ved, 1)
                after(pool, ved, t)
                after(pool, xnd, t, back=2)
                nc.gpsimd.tensor_tensor(rstd[u][:, :], ve[u][:, :], c.neghalf[:, 0:1], ALU.pow).then_inc(rstdd, 1)

            pipeline(pool, T, [(weigh, 2), (root, 4), (r.root(pool), 1), (r.gates(pool), 0), (r.send(pool), 0)], AHEAD)
            r.sent_all(pool)

        @block.scalar
        def _(act):
            def expo(t, u):
                after(act, ssd, t)
                after(act, prd, t, back=2)
                nc.scalar.activation(ex[u][:, :], ss[u][:, :], ACT.Exp, scale=0.125).then_inc(exd, 1)

            def keep_out(t, u):
                after(act, od, t)
                after(act, pj, t, back=2)
                nc.scalar.copy(oT[u][:, :], ps_o[u][:, 0:P]).then_inc(ok, 1)

            def keep_turned(t, u):
                after(act, xT, t)
                after(act, qk, t, back=2)
                nc.scalar.copy(xnT[u][:, :], ps_t[u][:, 0:P]).then_inc(xTk, 1)

            def keep_qkv(t, u):
                after(act, qk, t)
                after(act, pvd, t, back=2)
                nc.scalar.copy(qkv[u][:, :], ps_qkv[u][:, 0:W]).then_inc(qkk, 1)

            pipeline(act, T, [(expo, 3), (keep_out, 2), (keep_turned, 4), (keep_qkv, 4), (r.keep_turned(act), 1)], AHEAD)

        @block.tensor
        def _(pe):
            def sum_out(t, u):
                after(pe, pvd, t)
                after(pe, ok, t, back=1)
                for g in range(H):
                    mm = nc.tensor.matmul(ps_o[u][:, 0:P], pv[u][:, g, :], c.ident[:, :], start=(g == 0),
                                          stop=(g == H - 1))
                mm.then_inc(od, 1)

            def project(t, u):
                after(pe, ok, t)
                after(pe, x1, t, back=2)
                nc.tensor.matmul(ps_p[u][:, 0:D], oT[u][:, :], wprojT, start=True, stop=False)
                nc.tensor.matmul(ps_p[u][:, 0:D], c.ones[:, :], c.rows[:, R_PROJ, :], start=False,
                                 stop=True).then_inc(pj, 1)

            def turn(t, u):
                after(pe, xnd, t)
                after(pe, xTk, t, back=1)
                nc.tensor.transpose(ps_t[u][:, 0:P], xn[u][:, :], c.ident[:, :]).then_inc(xT, 1)

            def make_qkv(t, u):
                after(pe, xTk, t)
                after(pe, qkk, t, back=2)
                nc.tensor.matmul(ps_qkv[u][:, 0:W], xnT[u][:, :], wqkvT, start=True, stop=True).then_inc(qk, 1)

            pipeline(pe, T, [(sum_out, 2), (project, 2), (r.positions(pe), 0), (turn, 4), (make_qkv, 4),
                            (r.turn(pe), 1), (r.logits(pe), 1)], AHEAD)


def causal_attention(nc, c):
    R, AHEAD, KP, FILLS = 4, 4, 96, 12
    TB = S // P
    SCALE = float(DH) ** -0.5
    with ExitStack() as ctx:
        named = ctx.enter_context(semaphores(nc))

        def ring(name, shape, dt=F32, n=R):
            return [ctx.enter_context(nc.sbuf_tensor(f"c_{name}{u}", shape, dt)) for u in range(n)]

        def one(name, shape, dt=F32):
            return ctx.enter_context(nc.sbuf_tensor(f"c_{name}", shape, dt))

        def bank(name):
            return ctx.enter_context(nc.psum_tensor(f"c_{name}", [P, 512], F32))

        def sem(name):
            return named("c_" + name)

        y = ring("y", [P, TOPK, TB, D])
        st, mv, ve, rstd = ring("st", [P, TB, 6]), ring("mv", [P, TB, 2]), ring("ve", [P, TB]), ring("rstd", [P, TB])
        z, uu, state, xdT = ring("z", [P, TB, D], n=1), ring("uu", [P, S], n=1), ring("state", [P, 1 + S], n=1), \
            ring("xdT", [P, S], n=1)
        xs, eg, gd, gr, mb = ring("xs", [P, 1]), ring("eg", [P, 1]), ring("gd", [P, 1]), ring("gr", [P, 1]), \
            ring("mb", [P, P], n=1)
        junk, ss, se, rs = one("junk", [P, TB, D]), ring("ss", [P, TB]), ring("se", [P, TB]), ring("rs", [P, TB])
        nd, ndT = ring("nd", [P, TB, D], n=1), ring("ndT", [P, S], n=1)
        qk, left1, left2 = ring("qk", [P, 2, S], n=1), one("left1", [P, 2, S]), one("left2", [P, 2, S])
        part = [ring(f"part{k}", [P, 2, S], BF16, n=1) for k in range(3)]
        qs, ks = ring("qs", [KP, H // 2, S], BF16), ring("ks", [KP, H, S], BF16)
        va = ring("va", [P, TB, H, 32])
        mx, nm, m1, m2 = ring("mx", [P, TB, H]), ring("nm", [P, TB, H], n=1), ring("m1", [P, TB, H], n=1), \
            ring("m2", [P, TB, H], n=1)
        mp, mT = ring("mp", [P, TB, 3, 32], BF16, n=1), ring("mT", [KP, S], BF16)
        pt = ring("pt", [P, 512], n=4)
        oTs, on, oT, rd = ring("oTs", [P, 4, S], n=1), ring("on", [P, TB, D], n=1), ring("oT", [P, S], n=1), \
            ring("rd", [P, TB, H], n=1)
        pick = one("pick", [KP, H, P], BF16)
        mask_q = [one(f"mask_q{j}", [P, 512], BF16) for j in range(2)]
        mask_k = [one(f"mask_k{j}", [P, 512], BF16) for j in range(2)]
        ps_c2, ps_c3 = [bank("s0"), bank("s1")], [bank("e0"), bank("e1")]
        ps_pv, ps_t, ps_q, ps_o = bank("pv"), bank("t"), bank("q"), bank("o")
        ps_tb = ps_t[:, :].bitcast(BF16)

        names = ("preset preset2 comb1 comb bn stats ve rstd zd zT uud scan xd xsd gate egd gdd grd mbd mh mhx xdr sq xdk se rs "
                 "ndd ndTd ndTk qkd qkk vd vk p0 l1 p1 l2 p2 s2 mxd nmd a1 b1 a2 b2 a3 mTd mTk s3 exd pvd otk on0 rd0 "
                 "nrm0 on1 rd1 nrm1 oT2 oT2k ao rr rx").split()
        s = {n: sem(n) for n in names}
        ydma = [sem(f"y{u}") for u in range(R)]
        parts, stack = [sem(f"parts{u}") for u in range(R)], [sem(f"stack{u}") for u in range(R)]
        spread = [nc.dram_tensor(f"spread{u}", (2, 3, DH, H, S), BF16, kind="Internal").ap() for u in range(R)]
        c.c_done = s["rx"]
        wq, wk, wv = (c.wT[:, IN1 + k, :] for k in range(3))
        wo = c.wT[:, OUT1, :]
        block = ctx.enter_context(nc.Block())

        def xb(b):
            return c.x[:, bass.ds(b * (TB * D), TB * D)]

        def rb(b):
            return c.r[:, bass.ds(b * (TB * D), TB * D)]

        def nth(eng, sm, b, k=0, per=1, back=0):
            n = b * per + (k + 1 - back)
            if isinstance(n, int):
                n = min(n, B * per)
                if n <= 0:
                    return
            eng.wait_ge(sm, n)

        def of_ring(eng, sems, b, u, each, back=0):
            if isinstance(b, int):
                if b // R + 1 - back > 0:
                    eng.wait_ge(sems[u], each * (b // R + 1 - back))
            else:
                eng.wait_ge(sems[u], (b - u) * (each // R) + each * (1 - back))

        def heads2(k):
            return (0, range(4 * k, 4 * k + 4)) if k < 4 else (1, range(2 * (k - 4), 2 * (k - 4) + 2))

        def heads3(k):
            g, i = divmod(k, 3)
            return (0, range(4 * g + 2 * i, 4 * g + 2 * i + 2)) if i < 2 else (1, range(4 * g, 4 * g + 4))

        NSTACK, NPARTS, NY = 12 * 16, 6 * 16, 3 * 16

        @block.sync
        def _(sp):
            def results(b, u):
                nth(sp, s["comb"], b, back=R)
                src = c.res[0:TOPK * T * P, :].rearrange("(k t p) d -> k p t d", k=TOPK, p=P)
                sp.dma_start(y[u][:, 0, :, :], src[0, :, bass.ds(b * TB, TB), :]).then_inc(ydma[u], 16)
                for j in range(TB):
                    sp.dma_start(y[u][:, 1, j:j + 1, :], src[1, :, bass.ds(b * TB + j, 1), :]).then_inc(ydma[u], 16)

            def stacks(b, u):
                of_ring(sp, stack, b, u, NSTACK, back=1)
                apart(sp, b)
                nth(sp, s["p2"], b)
                for k in range(3):
                    for side in range(2):
                        sp.dma_start(spread[u][side, k].rearrange("d h q -> h d q"),
                                     part[k][0][:, side, :]).then_inc(parts[u], 16)
                nth(sp, s["s3"], b, k=FILLS - 1, per=FILLS, back=R * FILLS)
                of_ring(sp, parts, b, u, NPARTS)
                for par in range(2):
                    row = 48 * par
                    for first, n in ((0, 3), (1, 2), (2, 1)):
                        rows = slice(row, row + 8 * n)
                        half = slice(par * H // 2, (par + 1) * H // 2)
                        sp.dma_start(qs[u][rows, :, :], spread[u][0, first:first + 1, :, half, :]
                                     .to_broadcast([n, DH, H // 2, S])).then_inc(stack[u], 16)
                        sp.dma_start(ks[u][rows, half, :], spread[u][1, 0:n, :, half, :]).then_inc(stack[u], 16)
                        row += 8 * n

            pipeline(sp, B, [(results, AHEAD), (stacks, AHEAD)], AHEAD, start=2, ring=R)

        @block.gpsimd
        def _(pool):
            for u in range(R):
                nc.gpsimd.memset(ks[u][:, :, :], 0.0).then_inc(s["preset"], 1)
                nc.gpsimd.memset(va[u][:, :, :, :], 0.0).then_inc(s["preset2"], 1)
            nc.gpsimd.memset(mp[0][:, :, :, :], 0.0).then_inc(s["preset"], 1)
            nc.gpsimd.memset(pick[:, :, :], 0.0).then_inc(s["preset"], 1)
            for m in mask_q + mask_k:
                nc.gpsimd.memset(m[:, :], 0.0).then_inc(s["preset"], 1)
            nc.gpsimd.memset(state[0][:, 0:1], 0.0).then_inc(s["preset"], 1)
            n = R + 7
            pool.wait_ge(s["preset2"], R)
            for u in range(R):
                nc.gpsimd.memset(va[u][:, :, :, DH:DH + 1], 1.0).then_inc(s["preset2"], 1)
            pool.wait_ge(s["preset"], n)
            for k in range(3):
                nc.gpsimd.affine_select(out=pick[:, :, :], in_=pick[:, :, :], compare_op=ALU.not_equal, fill=1.0,
                                        base=-32 * k, pattern=[[-1, H], [0, P]],
                                        channel_multiplier=1).then_inc(s["preset"], 1)
                pool.wait_ge(s["preset"], n + k + 1)
            n += 3
            NEG = -1e9
            for m, heads, width, at, sign in ((mask_q[0], 4, P, 0, 1), (mask_q[1], 2, S, P, 1),
                                              (mask_k[0], 2, S, 0, -1), (mask_k[1], 4, P, 0, -1)):
                v = m[:, :].rearrange("p (h w) -> p h w", h=heads)[:, :, at:at + P]
                nc.gpsimd.affine_select(out=v, in_=v, compare_op=ALU.is_ge, fill=NEG, base=0,
                                        pattern=[[0, heads], [-sign, P]], channel_multiplier=sign
                                        ).then_inc(s["preset"], 1)
            c.c_preset = n + 4

            def root(b, u):
                after(pool, s["stats"], b)
                apart(pool, b)
                nc.gpsimd.tensor_scalar(ve[u][:, :], mv[u][:, :, 1], LN_EPS, None, ALU.add).then_inc(s["ve"], 1)
                after(pool, s["ve"], b)
                nc.gpsimd.tensor_tensor(rstd[u][:, :], ve[u][:, :], c.neghalf[:, 0:TB], ALU.pow).then_inc(s["rstd"], 1)

            def root2(b, u):
                nth(pool, s["sq"], b, k=1, per=2)
                apart(pool, b)
                nc.gpsimd.tensor_scalar(se[u][:, :], ss[u][:, :], 1.0 / D, RMS_EPS, ALU.mult, ALU.add).then_inc(s["se"], 1)
                after(pool, s["se"], b)
                nc.gpsimd.tensor_tensor(rs[u][:, :], se[u][:, :], c.neghalf[:, 0:TB], ALU.pow).then_inc(s["rs"], 1)

            def split(b, u):
                nth(pool, s["qkk"], b, k=1, per=2)
                of_ring(pool, parts, b - 1, (u - 1) % R, NPARTS)
                apart(pool, b)
                nc.gpsimd.tensor_copy(part[0][0][:, :, :], qk[0][:, :, :]).then_inc(s["p0"], 1)
                after(pool, s["p0"], b)
                nc.gpsimd.tensor_tensor(left1[:, :, :], qk[0][:, :, :], part[0][0][:, :, :],
                                        ALU.subtract).then_inc(s["l1"], 1)
                after(pool, s["l1"], b)
                apart(pool, b)
                nc.gpsimd.tensor_copy(part[1][0][:, :, :], left1[:, :, :]).then_inc(s["p1"], 1)
                after(pool, s["p1"], b)
                nc.gpsimd.tensor_tensor(part[2][0][:, :, :], left1[:, :, :], part[1][0][:, :, :],
                                        ALU.subtract).then_inc(s["p2"], 1)

            def split_max(b, u):
                nth(pool, s["mxd"], b, k=FILLS - 1, per=FILLS)
                after(pool, s["mTd"], b, back=1)
                apart(pool, b)
                nc.gpsimd.tensor_scalar(nm[0][:, :, :], mx[u][:, :, :], -1.0, None, ALU.mult).then_inc(s["nmd"], 1)
                after(pool, s["nmd"], b)
                apart(pool, b)
                nc.gpsimd.tensor_copy(mp[0][:, :, 0, 0:H], nm[0][:, :, :]).then_inc(s["a1"], 1)
                after(pool, s["a1"], b)
                nc.gpsimd.tensor_tensor(m1[0][:, :, :], nm[0][:, :, :], mp[0][:, :, 0, 0:H],
                                        ALU.subtract).then_inc(s["b1"], 1)
                after(pool, s["b1"], b)
                apart(pool, b)
                nc.gpsimd.tensor_copy(mp[0][:, :, 1, 0:H], m1[0][:, :, :]).then_inc(s["a2"], 1)
                after(pool, s["a2"], b)
                nc.gpsimd.tensor_tensor(mp[0][:, :, 2, 0:H], m1[0][:, :, :], mp[0][:, :, 1, 0:H],
                                        ALU.subtract).then_inc(s["a3"], 1)

            pipeline(pool, B, [(root, AHEAD), (root2, AHEAD), (split_max, 2), (split, AHEAD)], AHEAD, start=2, ring=R)

        @block.vector
        def _(dve):
            dve.wait_ge(s["preset"], c.c_preset)

            def combine(b, u):
                of_ring(dve, ydma, b, u, NY)
                nc.vector.tensor_tensor(xb(b), xb(b), y[u][:, 0, :, :].rearrange("p t d -> p (t d)"),
                                        ALU.add).then_inc(s["comb1"], 1)
                after(dve, s["comb1"], b)
                nc.vector.tensor_tensor(xb(b), xb(b), y[u][:, 1, :, :].rearrange("p t d -> p (t d)"),
                                        ALU.add).then_inc(s["comb"], 1)

            def statistics(b, u):
                after(dve, s["comb"], b)
                apart(dve, b)
                for j in range(TB):
                    nc.vector.bn_stats(st[u][:, j, :], c.x[:, bass.ds(b * (TB * D) + j * D, D)]).then_inc(s["bn"], 1)
                after(dve, s["bn"], b, per=TB)
                apart(dve, b)
                for j in range(TB):
                    ins = nc.vector.bn_aggr(mv[u][:, j, :], st[u][:, j, :])
                ins.then_inc(s["stats"], 1)

            def normalise(b, u):
                after(dve, s["rstd"], b)
                after(dve, s["zT"], b, back=1)
                for j in range(TB):
                    ins = nc.vector.tensor_scalar(z[0][:, j, :], c.x[:, bass.ds(b * (TB * D) + j * D, D)],
                                                  mv[u][:, j, 0:1], rstd[u][:, j:j + 1], ALU.subtract, ALU.mult)
                ins.then_inc(s["zd"], 1)

            def delta(b, u):
                after(dve, s["uud"], b)
                after(dve, s["xd"], b, back=1)
                nc.vector.tensor_tensor_scan(state[0][:, 1:1 + S], c.beta[:, 0:1].to_broadcast([P, S]), uu[0][:, :],
                                             0.0, ALU.mult, ALU.add).then_inc(s["scan"], 1)
                after(dve, s["scan"], b)
                after(dve, s["mh"], b, back=1)
                nc.vector.tensor_tensor(xdT[0][:, :], ps_t[:, 0:S], state[0][:, 0:S], ALU.subtract).then_inc(s["xd"], 1)
                after(dve, s["xd"], b)
                nc.vector.tensor_reduce(xs[u][:, :], xdT[0][:, :], AX.X, ALU.add).then_inc(s["xsd"], 1)

            def mixing(b, u):
                after(dve, s["egd"], b)
                nc.vector.tensor_scalar(gd[u][:, :], eg[u][:, :], 1.0, None, ALU.add).then_inc(s["gdd"], 1)
                after(dve, s["gdd"], b)
                nc.vector.reciprocal(gr[u][:, :], gd[u][:, :]).then_inc(s["grd"], 1)
                after(dve, s["grd"], b)
                nc.vector.tensor_scalar(mb[0][:, :], c.hbig[:, :], gr[u][:, 0:1], None, ALU.mult).then_inc(s["mbd"], 1)

            def add_mixed(b, u):
                after(dve, s["mh"], b)
                nc.vector.tensor_tensor(xb(b), ps_q[:, 256:512], xb(b), ALU.add).then_inc(s["mhx"], 1)

            def maxima(k):
                def stage(b, u):
                    j, hs = heads2(k)
                    nth(dve, s["s2"], b, k, FILLS)
                    n = len(hs)
                    nc.vector.tensor_reduce(mx[u][:, j, hs[0]:hs[0] + n],
                                            ps_c2[k % 2][:, :].rearrange("p (h w) -> p h w", h=n), AX.X,
                                            ALU.max).then_inc(s["mxd"], 1)
                return stage

            def divide(j):
                def stage(b, u):
                    after(dve, s[f"on{j}"], b)
                    v = ps_o[:, :].rearrange("p (h w) -> p h w", h=H)
                    nc.vector.reciprocal(rd[0][:, j, :], v[:, :, DH]).then_inc(s[f"rd{j}"], 1)
                    after(dve, s[f"rd{j}"], b)
                    after(dve, s["oT2"], b, back=1)
                    nc.vector.tensor_tensor(on[0][:, j, :].rearrange("p (h w) -> p h w", h=H), v[:, :, 0:DH],
                                            rd[0][:, j, :].unsqueeze(2).to_broadcast([P, H, DH]),
                                            ALU.mult).then_inc(s[f"nrm{j}"], 1)
                return stage

            def join(b, u):
                after(dve, s["ao"], b)
                after(dve, s["xdk"], b)
                nc.vector.tensor_tensor(rb(b), ps_o[:, 0:S], rb(b), ALU.add).then_inc(s["rr"], 1)
                after(dve, s["rr"], b)
                after(dve, s["mhx"], b)
                nc.vector.tensor_tensor(xb(b), xb(b), rb(b), ALU.add).then_inc(s["rx"], 1)

            m = [(maxima(k), 2) for k in range(FILLS)]
            pipeline(dve, B, [(combine, AHEAD), (statistics, AHEAD), (divide(0), 0), *m[0:2], (normalise, AHEAD), (divide(1), 0),
                              *m[2:4], (delta, AHEAD), *m[4:6], (join, 0), *m[6:8], (mixing, AHEAD), *m[8:10], (add_mixed, AHEAD),
                              *m[10:12]], AHEAD, start=2, ring=R)

        @block.scalar
        def _(act):
            act.wait_ge(s["preset"], c.c_preset)
            act.wait_ge(s["preset2"], 2 * R)

            def blend(b, u):
                after(act, s["zT"], b)
                after(act, s["scan"], b, back=1)
                nc.scalar.activation(uu[0][:, :], ps_t[:, 0:S], ACT.Copy, scale=c.omb[:, 0:1]).then_inc(s["uud"], 1)

            def rows(b, u):
                after(act, s["xdr"], b)
                for j in range(TB):
                    nc.scalar.activation(junk[:, j, :], ps_t[:, 256 + j * D:256 + (j + 1) * D], ACT.Square,
                                         accum_out=ss[u][:, j:j + 1]).then_inc(s["sq"], 1)
                nc.scalar.copy(rb(b), ps_t[:, 256:512]).then_inc(s["xdk"], 1)

            def gate(b, u):
                after(act, s["gate"], b)
                nc.scalar.activation(eg[u][:, :], ps_q[:, 0:1], ACT.Exp, bias=c.ngb[:, 0:1],
                                     scale=-1.0 / S).then_inc(s["egd"], 1)

            def scale_rows(b, u):
                after(act, s["ndTd"], b, back=1)
                after(act, s["xdk"], b)
                after(act, s["rs"], b)
                apart(act, b)
                for j in range(TB):
                    ins = nc.scalar.activation(nd[0][:, j, :], c.r[:, bass.ds(b * (TB * D) + j * D, D)], ACT.Copy,
                                               scale=rs[u][:, j:j + 1])
                ins.then_inc(s["ndd"], 1)

            def keep_turned(b, u):
                after(act, s["ndTd"], b)
                after(act, s["vd"], b, back=1)
                nc.scalar.activation(ndT[0][:, :], ps_t[:, 0:S], ACT.Copy,
                                     scale=c.wT[:, VECS, V_LN1:V_LN1 + 1]).then_inc(s["ndTk"], 1)

            def keep_qkv(b, u):
                after(act, s["qkd"], b)
                after(act, s["p2"], b, back=1)
                for k, row in ((0, V_BQ), (1, V_BK)):
                    nc.scalar.activation(qk[0][:, k, :], ps_q[:, k * S:(k + 1) * S], ACT.Identity,
                                         bias=c.wT[:, VECS, row:row + 1]).then_inc(s["qkk"], 1)

            def keep_v(b, u):
                after(act, s["vd"], b)
                nth(act, s["pvd"], b, k=0, per=FILLS, back=1 + (R - 1) * FILLS)
                nc.scalar.copy(va[u][:, :, :, 0:DH],
                               ps_t[:, 256:512].rearrange("p (t h w) -> p t h w", t=TB, h=H)).then_inc(s["vk"], 1)

            def keep_max(b, u):
                after(act, s["mTd"], b)
                nth(act, s["s3"], b, k=0, per=FILLS, back=1 + (R - 1) * FILLS)
                nc.scalar.copy(mT[u][:, :], ps_tb[0:KP, 0:S]).then_inc(s["mTk"], 1)

            def expo(k):
                def stage(b, u):
                    nth(act, s["s3"], b, k, FILLS)
                    nth(act, s["pvd"], b, k, FILLS, back=4)
                    nc.scalar.activation(pt[k % 4][:, :], ps_c3[k % 2][:, :], ACT.Exp, scale=SCALE).then_inc(s["exd"], 1)
                return stage

            def keep_out(half):
                def stage(b, u):
                    nth(act, s["pvd"], b, 6 * half + 5, FILLS)
                    if half == 0:
                        after(act, s["on1"], b, back=1)
                    nc.scalar.copy(oTs[0][:, 2 * half:2 * half + 2, :].rearrange("p g q -> p (g q)"),
                                   ps_pv[:, :]).then_inc(s["otk"], 1)
                return stage

            def keep_o(b, u):
                after(act, s["oT2"], b)
                after(act, s["ao"], b, back=1)
                nc.scalar.copy(oT[0][:, :], ps_t[:, 0:S]).then_inc(s["oT2k"], 1)

            e = [(expo(k), 1) for k in range(FILLS)]
            pipeline(act, B, [*e[0:2], (blend, AHEAD), *e[2:3], (keep_o, 0), *e[3:4], (rows, AHEAD), (gate, AHEAD), *e[4:5],
                              (scale_rows, AHEAD), *e[5:6], (keep_turned, AHEAD), *e[6:7], (keep_out(0), 1), *e[7:8],
                              (keep_qkv, AHEAD), (keep_v, AHEAD), *e[8:10], (keep_max, 2), *e[10:12], (keep_out(1), 1)],
                     AHEAD, start=2, ring=R)

        @block.tensor
        def _(pe):
            pe.wait_ge(s["preset"], c.c_preset)

            def turn_z(b, u):
                after(pe, s["zd"], b)
                after(pe, s["vk"], b, back=1)
                after(pe, s["mTk"], b, back=AHEAD - 1)
                for j in range(TB):
                    mm = nc.tensor.transpose(ps_t[:, j * P:(j + 1) * P], z[0][:, j, :], c.ident[:, :])
                mm.then_inc(s["zT"], 1)

            def turn_delta(b, u):
                after(pe, s["xd"], b)
                nth(pe, s["oT2k"], b, back=AHEAD)
                for j in range(TB):
                    mm = nc.tensor.transpose(ps_t[:, 256 + j * P:256 + (j + 1) * P], xdT[0][:, :][:, j * P:(j + 1) * P],
                                             c.ident[:, :])
                mm.then_inc(s["xdr"], 1)
                after(pe, s["xsd"], b)
                nth(pe, s["qkk"], b, k=1, per=2, back=2)
                nc.tensor.matmul(ps_q[:, 0:1], c.wT[:, GATE1, :], xs[u][:, :], start=True, stop=True).then_inc(s["gate"], 1)

            def mix(b, u):
                after(pe, s["mbd"], b)
                after(pe, s["egd"], b)
                for j in range(TB):
                    mm = nc.tensor.matmul(ps_q[:, 256 + j * P:256 + (j + 1) * P], xdT[0][:, :][:, j * P:(j + 1) * P],
                                          mb[0][:, :], start=True, stop=True)
                mm.then_inc(s["mh"], 1)

            def turn_normed(b, u):
                after(pe, s["ndd"], b)
                after(pe, s["xdk"], b)
                nth(pe, s["sq"], b, k=1, per=2)
                for j in range(TB):
                    mm = nc.tensor.transpose(ps_t[:, j * P:(j + 1) * P], nd[0][:, j, :], c.ident[:, :])
                mm.then_inc(s["ndTd"], 1)

            def project(b, u):
                after(pe, s["ndTk"], b)
                after(pe, s["mhx"], b)
                nc.tensor.matmul(ps_q[:, 0:S], wq, ndT[0][:, :], start=True, stop=True)
                nc.tensor.matmul(ps_q[:, S:2 * S], wk, ndT[0][:, :], start=True, stop=True).then_inc(s["qkd"], 1)
                for j in range(TB):
                    o = ps_t[:, 256 + j * P:256 + (j + 1) * P]
                    nc.tensor.matmul(o, ndT[0][:, j * P:(j + 1) * P], wv, start=True, stop=False)
                    mm = nc.tensor.matmul(o, c.ones[:, :], c.rows[:, R_V, :], start=False, stop=True)
                mm.then_inc(s["vd"], 1)

            def turn_max(b, u):
                after(pe, s["a3"], b)
                nth(pe, s["vk"], b, back=2 - AHEAD)
                after(pe, s["oT2k"], b, back=2)
                for j in range(TB):
                    mm = nc.tensor.transpose(ps_tb[0:KP, j * P:(j + 1) * P],
                                             mp[0][:, j, :, :].rearrange("p a b -> p (a b)"), c.identb[:, :])
                mm.then_inc(s["mTd"], 1)

            def scores(k):
                def stage(b, u):
                    j, hs = heads2(k)
                    if k == 0:
                        of_ring(pe, stack, b, u, NSTACK)
                    nth(pe, s["mxd"], b, k, FILLS, back=2)
                    w = (j + 1) * P
                    nc.tensor.matmul(ps_c2[k % 2][:, :], c.identb[:, :], mask_q[j][:, :], start=True, stop=False)
                    for n, h in enumerate(hs):
                        mm = nc.tensor.matmul(ps_c2[k % 2][:, n * w:(n + 1) * w], qs[u][:, h % (H // 2), j * P:(j + 1) * P],
                                              ks[u][:, h, 0:w], start=False, stop=(n == len(hs) - 1))
                    mm.then_inc(s["s2"], 1)
                return stage

            def scores_t(k):
                def stage(b, u):
                    j, hs = heads3(k)
                    if k == 0:
                        after(pe, s["mTk"], b)
                    nth(pe, s["exd"], b, k, FILLS, back=2)
                    w = S - j * P
                    nc.tensor.matmul(ps_c3[k % 2][:, :], c.identb[:, :], mask_k[j][:, :], start=True, stop=False)
                    for n, h in enumerate(hs):
                        o = ps_c3[k % 2][:, n * w:(n + 1) * w]
                        nc.tensor.matmul(o, ks[u][:, h, j * P:(j + 1) * P], qs[u][:, h % (H // 2), j * P:S], start=False,
                                         stop=False)
                        mm = nc.tensor.matmul(o, pick[:, h, :], mT[u][:, j * P:S], start=False,
                                              stop=(n == len(hs) - 1))
                    mm.then_inc(s["s3"], 1)
                return stage

            def weigh(k):
                def stage(b, u):
                    j, hs = heads3(k)
                    nth(pe, s["exd"], b, k, FILLS)
                    if k == 0:
                        after(pe, s["vk"], b)
                        nth(pe, s["otk"], b, k=0, per=2, back=1)
                    if k == 6:
                        nth(pe, s["otk"], b, k=0, per=2)
                    w = S - j * P
                    for n, h in enumerate(hs):
                        q, at = 32 * (h % 4), (h // 4 % 2) * S
                        mm = nc.tensor.matmul(ps_pv[q:q + 32, at + j * P:at + S], va[u][:, j, h, :],
                                              pt[k % 4][:, n * w:(n + 1) * w], start=(j == 0), stop=(j == 1),
                                              skip_group_check=True)
                    mm.then_inc(s["pvd"], 1)
                return stage

            def turn_out(j):
                def stage(b, u):
                    if j == 0:
                        nth(pe, s["otk"], b, k=1, per=2)
                        after(pe, s["rr"], b, back=1)
                    else:
                        after(pe, s["nrm0"], b)
                    for g in range(4):
                        mm = nc.tensor.transpose(ps_o[:, g * P:(g + 1) * P], oTs[0][:, g, j * P:(j + 1) * P],
                                                 c.ident[:, :])
                    mm.then_inc(s[f"on{j}"], 1)
                return stage

            def turn_o(b, u):
                after(pe, s["nrm1"], b)
                nth(pe, s["xd"], b, back=-AHEAD)
                nth(pe, s["mTk"], b, back=-1)
                for j in range(TB):
                    mm = nc.tensor.transpose(ps_t[:, j * P:(j + 1) * P], on[0][:, j, :], c.ident[:, :])
                mm.then_inc(s["oT2"], 1)

            def project_out(b, u):
                after(pe, s["oT2k"], b)
                for j in range(TB):
                    o = ps_o[:, j * P:(j + 1) * P]
                    nc.tensor.matmul(o, oT[0][:, j * P:(j + 1) * P], wo, start=True, stop=False)
                    mm = nc.tensor.matmul(o, c.ones[:, :], c.rows[:, R_OUT, :], start=False, stop=True)
                mm.then_inc(s["ao"], 1)

            s2 = [(scores(k), 2) for k in range(FILLS)]
            s3 = [(scores_t(k), 1) for k in range(FILLS)]
            pv = [(weigh(k), 1) for k in range(FILLS)]
            pipeline(pe, B, [(turn_out(0), 0), s3[0], *s2[0:2], (turn_out(1), 0), s3[1], (turn_z, AHEAD), *s2[2:4], pv[0],
                             s3[2], (turn_o, 0), *s2[4:6], pv[1], s3[3], (turn_delta, AHEAD), *s2[6:8], pv[2], s3[4],
                             (project_out, 0), *s2[8:10], pv[3], s3[5], (turn_normed, AHEAD), (mix, AHEAD), *s2[10:12], pv[4],
                             s3[6], pv[5], s3[7], (project, AHEAD), pv[6], s3[8], pv[7], s3[9], (turn_max, 2), pv[8],
                             s3[10], pv[9], s3[11], pv[10], pv[11]], AHEAD, start=2, ring=R)


def feed_forward(nc, outer, c, router):
    AHEAD = 4
    x3 = outer.enter_context(semaphores(nc))("d_x3")
    router.open(nc, outer, x3)
    with ExitStack() as ctx:
        named = ctx.enter_context(semaphores(nc))

        def pair(name, shape, dt=F32):
            return [ctx.enter_context(nc.sbuf_tensor(f"d_{name}{u}", shape, dt)) for u in range(2)]

        def banks(name, n=2):
            return [ctx.enter_context(nc.psum_tensor(f"d_{name}{u}", [P, 512], F32)) for u in range(n)]

        junk, ss, se, rs = pair("junk", [P, D]), pair("ss", [P, 1]), pair("se", [P, 1]), pair("rs", [P, 1])
        nd, ndT, hT = pair("nd", [P, D]), pair("ndT", [P, P]), pair("hT", [P, F])
        ps_n, ps_h, ps_y = banks("n", 1)[0], banks("h"), banks("y")
        sq, sed, rsd, ndd, ndTd, ndTk, hd, hTd, yd = (
            named("d_" + n) for n in ("sq", "se", "rs", "nd", "ndT", "ndTk", "h", "hT", "y"))
        block = ctx.enter_context(nc.Block())

        def r_of(t):
            return c.r[:, bass.ds(t * D, D)]

        @block.scalar
        def _(act):
            def squares(t, u):
                after(act, sed, t, back=2)
                after(act, sq, t, back=2)
                nc.scalar.activation(junk[u][:, :], r_of(t), ACT.Square, accum_out=ss[u][:, :]).then_inc(sq, 1)

            def keep_turned(t, u):
                after(act, ndTd, t)
                after(act, hd, t, back=2)
                nc.scalar.activation(ndT[u][:, :], ps_n[:, 0:P], ACT.Copy,
                                     scale=c.wT[:, VECS, V_LN2:V_LN2 + 1]).then_inc(ndTk, 1)

            def gelu(t, u):
                after(act, hd, t)
                after(act, yd, t, back=2)
                for k in range(FC):
                    ins = nc.scalar.activation(hT[u][:, k * P:(k + 1) * P], ps_h[u][:, k * P:(k + 1) * P], ACT.Gelu,
                                               bias=c.wT[:, VECS, V_FB1 + k:V_FB1 + k + 1])
                ins.then_inc(hTd, 1)

            pipeline(act, T, [(squares, 4), (keep_turned, 3), (router.keep_turned(act), 1), (gelu, 3),
                              (router.keep_projected(act), 1), (router.keep_squares(act), 1)], AHEAD)

        @block.gpsimd
        def _(pool):
            def root(t, u):
                after(pool, sq, t)
                apart(pool, t)
                nc.gpsimd.tensor_scalar(se[u][:, :], ss[u][:, :], 1.0 / D, RMS_EPS, ALU.mult, ALU.add).then_inc(sed, 1)
                after(pool, sed, t)
                after(pool, ndd, t, back=2)
                nc.gpsimd.tensor_tensor(rs[u][:, :], se[u][:, :], c.neghalf[:, 0:1], ALU.pow).then_inc(rsd, 1)

            pipeline(pool, T, [(root, 4), (router.root(pool), 1), (router.gates(pool), 0), (router.send(pool), 0),
                               (router.inverse_norm(pool), 1)], AHEAD)
            router.sent_all(pool)

        @block.vector
        def _(dve):
            def scale_rows(t, u):
                after(dve, rsd, t)
                after(dve, ndTd, t, back=2)
                nc.vector.tensor_scalar(nd[u][:, :], r_of(t), rs[u][:, 0:1], None, ALU.mult).then_inc(ndd, 1)

            def residual(t, u):
                after(dve, yd, t)
                x = c.x[:, bass.ds(t * D, D)]
                nc.vector.tensor_tensor(x, ps_y[u][:, 0:D], x, ALU.add).then_inc(x3, 1)

            pipeline(dve, T, [(router.statistics(dve), 1), (router.select(dve), 0), (scale_rows, 4),
                              (router.normalise(dve), 1), (router.place(dve), 0), (residual, 2)], AHEAD)

        @block.tensor
        def _(pe):
            def turn(t, u):
                after(pe, ndd, t)
                after(pe, ndTk, t, back=1)
                nc.tensor.transpose(ps_n[:, 0:P], nd[u][:, :], c.ident[:, :]).then_inc(ndTd, 1)

            def up(t, u):
                after(pe, ndTk, t)
                after(pe, hTd, t, back=2)
                for k in range(FC):
                    mm = nc.tensor.matmul(ps_h[u][:, k * P:(k + 1) * P], c.wT[:, FF1 + k, :], ndT[u][:, :], start=True,
                                          stop=True)
                mm.then_inc(hd, 1)

            def down(t, u):
                after(pe, hTd, t)
                after(pe, x3, t, back=2)
                for k in range(FC):
                    nc.tensor.matmul(ps_y[u][:, 0:D], hT[u][:, k * P:(k + 1) * P], c.wT[:, FF2 + k, :], start=(k == 0),
                                     stop=False)
                nc.tensor.matmul(ps_y[u][:, 0:D], c.ones[:, :], c.rows[:, R_FB2, :], start=False,
                                 stop=True).then_inc(yd, 1)

            pipeline(pe, T, [(router.positions(pe), 0), (turn, 3), (down, 2), (router.turn(pe), 1), (up, 3),
                             (router.project(pe), 1), (router.logits(pe), 1)], AHEAD)


@contextmanager
def expert_weights(nc, c, a, layer):
    names = ("L0_ffn_", "L1_ffn_")[layer]
    with ExitStack() as ctx:
        def sb(name, shape):
            return ctx.enter_context(nc.sbuf_tensor(f"{name}_{layer}", shape, F32))

        c.w1, c.w2 = sb("w1", [P, E, F]), sb("w2", [P, E * FC, D])
        c.b1bc, c.b2bc = sb("b1bc", [P, E * F]), sb("b2bc", [P, E * D])
        c.e_in = ctx.enter_context(semaphores(nc))(f"e_in{layer}")
        with nc.Block() as block:
            @block.scalar
            def _(act):
                act.dma_start(c.b1bc[:, :], a[names + "b1"].rearrange("e f -> (e f)").unsqueeze(0)
                              .to_broadcast([P, E * F])).then_inc(c.e_in, 16)
                act.dma_start(c.b2bc[:, :], a[names + "b2"].rearrange("e d -> (e d)").unsqueeze(0)
                              .to_broadcast([P, E * D])).then_inc(c.e_in, 16)
                act.dma_start(c.w1[:, :, :], a[names + "W1"].rearrange("e d f -> d e f")).then_inc(c.e_in, 16)
                act.dma_start(c.w2[:, :, :], a[names + "W2"].rearrange("e (c p) d -> p (e c) d", p=P)
                              ).then_inc(c.e_in, 16)
        yield


def combine_and_store(nc, ctx, c, out):
    G = 4
    parts = T // G
    added, stored = (ctx.enter_context(nc.semaphore(s)) for s in ("added", "stored"))
    fetched = [ctx.enter_context(nc.semaphore(f"fetched{g}")) for g in range(parts)]
    res = c.res[0:TOPK * T * P, :].rearrange("(k t p) d -> k p t d", k=TOPK, p=P)
    outv = out.rearrange("b (h p) d -> p (b h) d", p=P)
    with ExitStack() as tmp:
        y = tmp.enter_context(nc.sbuf_tensor("y", [P, TOPK, T, D], F32))
        block = tmp.enter_context(nc.Block())

        @block.scalar
        def _(act):
            for g in range(parts):
                act.dma_start(y[:, 1, g * G:(g + 1) * G, :], res[1, :, g * G:(g + 1) * G, :]).then_inc(fetched[g], 16)

        @block.sync
        def _(sp):
            for g in range(parts):
                sp.dma_start(y[:, 0, g * G:(g + 1) * G, :], res[0, :, g * G:(g + 1) * G, :]).then_inc(fetched[g], 16)
            for g in range(parts):
                sp.wait_ge(added, 2 * g + 2)
                sp.dma_start(outv[:, g * G:(g + 1) * G, :],
                             c.x[:, g * G * D:(g + 1) * G * D].rearrange("p (t d) -> p t d", d=D)).then_inc(stored, 16)
            sp.wait_ge(stored, 16 * parts)

        @block.vector
        def _(dve):
            for g in range(parts):
                dve.wait_ge(fetched[g], 32)
                xs = c.x[:, g * G * D:(g + 1) * G * D]
                for k in range(TOPK):
                    nc.vector.tensor_tensor(xs, xs, y[:, k, g * G:(g + 1) * G, :].rearrange("p t d -> p (t d)"),
                                            ALU.add).then_inc(added, 1)
                    dve.wait_ge(added, TOPK * g + k + 1)


def transformer(nc, a, out, stage=9):
    with ExitStack() as ctx:
        c = Core()
        c.tile_e = ctx.enter_context(nc.sbuf_tensor("tile_e", [1, XT], U32))
        c.tile_r = ctx.enter_context(nc.sbuf_tensor("tile_r", [1, XT], U32))
        load_and_prepare(nc, ctx, c, a)
        with expert_weights(nc, c, a, 0):
            with ExitStack() as routed:
                first = Router(nc, c, "r0", False)
                head_attention(nc, routed, c, first)
                first.finish(nc, routed)
            run_experts(nc, c, "x0")
        with ExitStack() as layer1:
            c.r = layer1.enter_context(nc.sbuf_tensor("r", [P, T * D], F32))
            causal_attention(nc, c)
            with expert_weights(nc, c, a, 1):
                with ExitStack() as routed:
                    second = Router(nc, c, "r1", True)
                    feed_forward(nc, routed, c, second)
                    second.finish(nc, routed)
                run_experts(nc, c, "x1")
        combine_and_store(nc, ctx, c, out)


def kernel(**inputs):
    import numpy as _np
    import concourse.bacc as _bacc
    from concourse import mybir as _mybir
    from concourse.bass_utils import run_bass_kernel_spmd as _run

    nc = _bacc.Bacc("TRN2", target_bir_lowering=False, num_devices=1)
    arrays, args = {}, {}
    for name, value in inputs.items():
        array = _np.ascontiguousarray(value)
        arrays[f"in_{name}_dram"] = array
        args[name] = nc.dram_tensor(f"in_{name}_dram", array.shape, _mybir.dt.from_np(array.dtype),
                                    kind="ExternalInput").ap()
    out = nc.dram_tensor("out_0_dram", (B, S, D), _mybir.dt.float32, kind="ExternalOutput").ap()
    transformer(nc, args, out)
    result = _run(nc, [arrays], core_ids=[0])
    return result.results[0]["out_0_dram"]
```

```python
from contextlib import ExitStack, contextmanager

import concourse.bass as bass
from concourse import mybir

P = 128
ALU = mybir.AluOpType
ACT = mybir.ActivationFunctionType
AX = mybir.AxisListType
F32 = mybir.dt.float32
BF16 = mybir.dt.bfloat16
U32 = mybir.dt.uint32

B, S, D = 16, 256, 128
T = B * S // P
H, DH = 16, 8
E, F = 8, 512
FC = F // P
NS, SD = 8, 16
LN_EPS, RMS_EPS, L2_EPS = 1e-5, 1e-6, 1e-12
SINKHORN = 15
EULER = 2.718281828459045

QKV0, PROJ0, IN1, OUT1, FF1, WP1, FF2, GATE1, VECS = 0, 3, 4, 7, 8, 12, 13, 17, 18
SLOTS = 20
V_B1A, V_B1B, V_FB1, V_LN1, V_LN2, V_DECAY, V_BQ, V_BK, NVEC = 0, 32, 64, 68, 69, 70, 71, 72, 73
R_PROJ, R_OUT, R_V, R_FB2 = range(4)

PADS = P
REGION = T * P + PADS
TOPK = 2
XT = T * TOPK + E
ROW = D + 1
NROWS = E * REGION + E * P
NRES = TOPK * T * P + 2 * E * P
E_LOADS = 3 * 16
KP = 96
ROUND = 8388608.0


def after(eng, sem, t, back=0, per=1):
    n = (t + 1 - back) * per
    if isinstance(n, int) and n <= 0:
        return
    eng.wait_ge(sem, n)


def apart(eng, t):
    if not isinstance(t, int):
        eng.nop(nofuse=True)


def pipeline(eng, tiles, stages, most, start=2, ring=2):

    def step(s, par):
        for f, a in stages:
            if isinstance(s, int) and not 0 <= s + a < tiles:
                continue
            f(s + a, (par + a) % ring)

    for s in range(-most, start):
        step(s, s % ring)
    bodies = (tiles - most - start) // ring
    with eng.Fori(0, bodies) as i:
        for k in range(ring):
            step(i * ring + (start + k), (start + k) % ring)
    end = start + ring * bodies
    for s in range(end, tiles):
        step(s, s % ring)


@contextmanager
def semaphores(nc):
    used = []

    def sem(name):
        used.append(nc.alloc_semaphore(name=name))
        return used[-1]

    yield sem
    with nc.Block() as block:
        @block.gpsimd
        def _(pool):
            numbers = sorted(handle.num for handle in used)
            first = 0
            for i in range(1, len(numbers) + 1):
                if i == len(numbers) or numbers[i] != numbers[i - 1] + 1:
                    pool.sem_clear(range(numbers[first], numbers[i - 1] + 1))
                    first = i
    for handle in used:
        nc.release_semaphore(handle)


class Core:
    pass


def load_and_prepare(nc, ctx, c, a):
    def sb(name, shape, dt=F32):
        return ctx.enter_context(nc.sbuf_tensor(name, shape, dt))

    keep = ctx.enter_context(semaphores(nc))

    c.x = sb("x", [P, T * D])
    c.wT = sb("wT", [P, SLOTS, P])
    c.rows = sb("rows", [1, 4, D])
    c.ones = sb("ones", [1, P])
    c.ident = sb("ident", [P, P])
    c.identb = sb("identb", [P, P], BF16)
    c.neghalf = sb("neghalf", [P, T])
    c.onesc = sb("onesc", [P, 2])
    c.iota8 = sb("iota8", [P, E])
    c.wgT = sb("wgT", [P, E])
    c.snT = sb("snT", [P, E])
    c.itemp = sb("itemp", [P, 1])
    c.omb = sb("omb", [P, 1])
    c.beta = sb("beta", [P, 1])
    c.ngb = sb("ngb", [P, 1])
    c.hbig = sb("hbig", [P, P])
    c.k0, c.k0T = sb("k0", [NS, NS]), sb("k0T", [NS, NS])
    c.rc = sb("rc", [NS, 2])
    c.esel = sb("esel", [NS, NS, SD])
    c.dmask = sb("dmask", [P, P])
    c.pick = sb("pick", [KP, H, P], BF16)
    c.mask_q = sb("mask_q", [P, 4 * P], BF16)
    c.mask_k = sb("mask_k", [P, 4 * P], BF16)
    c.w_in = keep("w_in")
    c.x_in = keep("x_in")

    c.before = sb("before", [P, P], BF16)
    c.onesb = sb("onesb", [P, P], BF16)
    c.gap = sb("gap", [P, T])
    c.gate = sb("gate", [P, TOPK, T])
    c.squares = sb("squares", [P, T])
    c.region = sb("region", [P, E])
    c.padrow = sb("padrow", [P, E, ROW])
    c.rows_x = nc.dram_tensor("rows_x", (NROWS, ROW), F32, kind="Internal").ap()
    c.res = nc.dram_tensor("res", (NRES, D), F32, kind="Internal").ap()
    c.spare_out = keep("spare_out")

    with ExitStack() as tmp:
        sem = tmp.enter_context(semaphores(nc))

        def tb(name, shape, dt=F32):
            return tmp.enter_context(nc.sbuf_tensor(name, shape, dt))

        wnat = tb("wnat", [P, SLOTS, P])
        wg = tb("wg", [E, D])
        sim = tb("sim", [E, D])
        simq = tb("simq", [E, D])
        sn = tb("sn", [E, D])
        nrm = tb("nrm", [E, 4])
        gb = tb("gb", [NS, 1])
        phi = tb("phi", [NS, NS])
        dsel = tb("dsel", [SD, NS, SD])
        edec = tb("edec", [P, 2])
        tempr = tb("tempr", [P, 1])
        spare = tb("spare", [P, E, ROW])
        padded = sem("padded")
        wps = [tmp.enter_context(nc.psum_tensor(f"wps{i}", [P, 512], F32)) for i in range(2)]
        sps = tmp.enter_context(nc.psum_tensor("sps", [P, 512], F32))
        mps = tmp.enter_context(nc.psum_tensor("mps", [P, 512], F32))
        zeroed, made, consts = sem("zeroed"), sem("made"), sem("consts")
        turned, kept = sem("turned"), sem("kept")
        s_small, small_kept = sem("s_small"), sem("small_kept")
        simn, expd, built = sem("simn"), sem("expd"), sem("built")
        NW = 23
        block = tmp.enter_context(nc.Block())

        @block.sync
        def _(sp):
            sp.wait_ge(zeroed, 1)
            def load(dst, src):
                sp.dma_start(dst, src).then_inc(c.w_in, 16)
            load(wnat[:, QKV0:QKV0 + 3, :], a["L0_attn_Wqkv"].rearrange("(s p) d -> p s d", p=P))
            load(wnat[:, PROJ0, :], a["L0_attn_Wproj"])
            load(wnat[:, IN1:IN1 + 3, :], a["L1_attn_in_proj_w"].rearrange("(s p) d -> p s d", p=P))
            load(wnat[:, OUT1, :], a["L1_attn_out_w"])
            load(wnat[:, FF1:FF1 + FC, :], a["L1_attn_w1"].rearrange("(s p) d -> p s d", p=P))
            load(wnat[:, WP1, :], a["L1_ffn_Wp"])
            load(wnat[:, FF2:FF2 + FC, :].rearrange("p s d -> p (s d)"), a["L1_attn_w2"])
            load(wnat[:, GATE1, :], a["L1_attn_gate_w"][2 * NS:3 * NS, :].unsqueeze(1).to_broadcast([NS, SD, D]))
            load(wnat[V_B1A:V_B1A + 32, VECS, :], a["L0_ffn_b1"].rearrange("e (c p) -> (e c) p", p=P))
            load(wnat[V_B1B:V_B1B + 32, VECS, :], a["L1_ffn_b1"].rearrange("e (c p) -> (e c) p", p=P))
            load(wnat[V_FB1:V_FB1 + FC, VECS, :], a["L1_attn_b1"].rearrange("(c p) -> c p", p=P))
            load(wnat[V_BQ:V_BQ + 2, VECS, :], a["L1_attn_in_proj_b"][0:2 * D].rearrange("(c p) -> c p", p=P))
            for row, name in ((V_LN1, "L1_attn_ln1_w"), (V_LN2, "L1_attn_ln2_w"), (V_DECAY, "L1_attn_delta_decay")):
                load(wnat[row:row + 1, VECS, :], a[name].unsqueeze(0))
            load(gb[:, :], a["L1_attn_gate_b"][2 * NS:3 * NS].unsqueeze(1))
            load(c.rows[:, R_PROJ, :], a["L0_attn_bproj"].unsqueeze(0))
            load(c.rows[:, R_OUT, :], a["L1_attn_out_b"].unsqueeze(0))
            load(c.rows[:, R_V, :], a["L1_attn_in_proj_b"][2 * D:3 * D].unsqueeze(0))
            load(c.rows[:, R_FB2, :], a["L1_attn_b2"].unsqueeze(0))
            load(wg[:, :], a["L0_ffn_Wg"])
            load(sim[:, :], a["L1_ffn_sim_matrix"])
            load(phi[:, :], a["L1_attn_phi_res"])

        @block.scalar
        def _(act):
            act.dma_start(c.x[:, :].rearrange("p (t d) -> p t d", d=D),
                          a["L0_attn_x"].rearrange("b (h p) d -> p (b h) d", p=P)).then_inc(c.x_in, 16)
            act.dma_start(tempr[:, :], a["L1_ffn_temperature"].unsqueeze(0).to_broadcast([P, 1])).then_inc(c.w_in, 16)
            act.wait_ge(padded, 2)
            act.dma_start(c.rows_x[E * REGION:NROWS, :].rearrange("(e p) d -> p e d", p=P), spare[:, :, :]
                          ).then_inc(c.spare_out, 16)
            act.wait_ge(c.spare_out, 16)
            act.wait_ge(c.w_in, 16 * (NW + 1))
            nc.scalar.activation(simq[:, :], sim[:, :], ACT.Square, accum_out=nrm[:, 0:1]).then_inc(simn, 1)
            nc.scalar.activation(c.k0[:, :], phi[:, :], ACT.Exp).then_inc(expd, 1)
            act.wait_ge(kept, SLOTS // 4)
            nc.scalar.activation(edec[:, 0:1], c.wT[:, VECS, V_DECAY:V_DECAY + 1], ACT.Exp, scale=-1.0).then_inc(expd, 1)

        @block.gpsimd
        def _(pool):
            nc.gpsimd.memset(wnat[:, VECS:VECS + 2, :], 0.0).then_inc(zeroed, 1)
            nc.gpsimd.memset(c.ident[:, :], 0.0).then_inc(made, 1)
            nc.gpsimd.memset(c.esel[:, :, :], 1.0).then_inc(made, 1)
            nc.gpsimd.memset(dsel[:, :, :], 0.0).then_inc(made, 1)
            nc.gpsimd.memset(c.ones[:, :], 1.0).then_inc(consts, 1)
            nc.gpsimd.memset(c.neghalf[:, :], -0.5).then_inc(consts, 1)
            nc.gpsimd.memset(c.onesc[:, :], 1.0).then_inc(consts, 1)
            nc.gpsimd.iota(c.iota8[:, :], [[1, E]], base=0, channel_multiplier=0,
                           allow_small_or_imprecise_dtypes=True).then_inc(consts, 1)
            nc.gpsimd.memset(c.onesb[:, :], 1.0).then_inc(consts, 1)
            nc.gpsimd.iota(c.region[:, :], [[REGION, E]], base=0, channel_multiplier=0,
                           allow_small_or_imprecise_dtypes=True).then_inc(consts, 1)
            nc.gpsimd.memset(c.before[:, :], 1.0).then_inc(zeroed, 1)
            for rows in (c.padrow, spare):
                nc.gpsimd.memset(rows[:, :, :], 0.0).then_inc(zeroed, 1)
            pool.wait_ge(zeroed, 4)
            nc.gpsimd.affine_select(out=c.before[:, :], in_=c.before[:, :], compare_op=ALU.is_gt, fill=0.0,
                                    base=0, pattern=[[1, P]], channel_multiplier=-1).then_inc(consts, 1)
            for n, rows in enumerate((c.padrow, spare)):
                nc.gpsimd.iota(rows[:, :, D].bitcast(U32), [[P, E]], base=TOPK * T * P + n * E * P,
                               channel_multiplier=1).then_inc(padded, 1)
            pool.wait_ge(made, 3)
            nc.gpsimd.affine_select(out=c.ident[:, :], in_=c.ident[:, :], compare_op=ALU.not_equal, fill=1.0,
                                    base=0, pattern=[[-1, P]], channel_multiplier=1).then_inc(made, 1)
            nc.gpsimd.affine_select(out=c.esel[:, :, :], in_=c.esel[:, :, :], compare_op=ALU.is_equal, fill=0.0,
                                    base=0, pattern=[[-1, NS], [0, SD]], channel_multiplier=1).then_inc(made, 1)
            nc.gpsimd.affine_select(out=dsel[:, :, :], in_=dsel[:, :, :], compare_op=ALU.not_equal, fill=1.0,
                                    base=0, pattern=[[0, NS], [-1, SD]], channel_multiplier=1).then_inc(made, 1)
            pool.wait_ge(made, 6)
            nc.gpsimd.tensor_copy(c.identb[:, :], c.ident[:, :]).then_inc(consts, 1)
            pool.wait_ge(simn, 1)
            pool.wait_ge(consts, 8)
            nc.gpsimd.tensor_scalar(nrm[:, 1:2], nrm[:, 0:1], L2_EPS * L2_EPS, None, ALU.max).then_inc(simn, 1)
            pool.wait_ge(simn, 2)
            nc.gpsimd.tensor_tensor(nrm[:, 2:3], nrm[:, 1:2], c.neghalf[0:E, 0:1], ALU.pow).then_inc(simn, 1)
            pool.wait_ge(simn, 3)
            nc.gpsimd.tensor_scalar(sn[:, :], sim[:, :], nrm[:, 2:3], None, ALU.mult).then_inc(simn, 1)

        @block.tensor
        def _(pe):
            pe.wait_ge(made, 6)
            pe.wait_ge(c.w_in, 16 * (NW + 1))
            for g in range(SLOTS // 4):
                if g >= 2:
                    pe.wait_ge(kept, g - 1)
                for k in range(4):
                    mm = nc.tensor.transpose(wps[g % 2][:, k * P:(k + 1) * P], wnat[:, 4 * g + k, :], c.ident[:, :])
                mm.then_inc(turned, 1)
            nc.tensor.transpose(sps[:, 0:E], wg[:, :], c.ident[0:E, 0:E])
            pe.wait_ge(simn, 4)
            nc.tensor.transpose(sps[:, E:2 * E], sn[:, :], c.ident[0:E, 0:E])
            pe.wait_ge(expd, 1)
            nc.tensor.transpose(sps[0:NS, 16:16 + NS], c.k0[:, :], c.ident[0:NS, 0:NS]).then_inc(s_small, 1)
            nc.tensor.matmul(mps[:, 0:P], dsel[:, :, :].rearrange("n a b -> n (a b)"),
                             dsel[:, :, :].rearrange("n a b -> n (a b)"), start=True, stop=True)
            nc.tensor.matmul(mps[:, P:P + 1], c.esel[:, :, :].rearrange("n a b -> n (a b)"), gb[:, :], start=True,
                             stop=True).then_inc(s_small, 1)

        @block.vector
        def _(dve):
            for g in range(SLOTS // 4):
                dve.wait_ge(turned, g + 1)
                nc.vector.tensor_copy(c.wT[:, 4 * g:4 * g + 4, :].rearrange("p s d -> p (s d)"),
                                      wps[g % 2][:, :]).then_inc(kept, 1)
            dve.wait_ge(s_small, 1)
            nc.vector.tensor_copy(c.wgT[:, :], sps[:, 0:E]).then_inc(small_kept, 1)
            nc.vector.tensor_copy(c.snT[:, :], sps[:, E:2 * E]).then_inc(consts, 1)
            nc.vector.tensor_copy(c.k0T[:, :], sps[0:NS, 16:16 + NS]).then_inc(small_kept, 1)
            nc.vector.memset(c.rc[:, 1:2], 1.0).then_inc(consts, 1)
            dve.wait_ge(s_small, 2)
            nc.vector.tensor_copy(c.dmask[:, :], mps[:, 0:P]).then_inc(consts, 1)
            nc.vector.reciprocal(c.itemp[:, :], tempr[:, :]).then_inc(consts, 1)
            dve.wait_ge(expd, 2)
            nc.vector.tensor_scalar(edec[:, 1:2], edec[:, 0:1], 1.0, None, ALU.add).then_inc(built, 1)
            dve.wait_ge(built, 1)
            nc.vector.reciprocal(c.beta[:, :], edec[:, 1:2]).then_inc(built, 1)
            dve.wait_ge(built, 2)
            nc.vector.tensor_scalar(c.omb[:, :], c.beta[:, :], -1.0, 1.0, ALU.mult, ALU.add).then_inc(consts, 1)
            dve.wait_ge(s_small, 2)
            nc.vector.tensor_scalar(c.ngb[:, :], mps[:, P:P + 1], -1.0, None,
                                    ALU.mult).then_inc(consts, 1)


class Router:

    def __init__(self, nc, c, name, similarity):
        self.nc, self.c, self.name, self.similarity = nc, c, name, similarity

    def open(self, nc, ctx, x_ready):
        name = self.name
        self.x_ready = x_ready
        named = ctx.enter_context(semaphores(nc))

        def pair(what, shape, dt=F32):
            return [ctx.enter_context(nc.sbuf_tensor(f"{name}_{what}{u}", shape, dt)) for u in range(2)]

        def sem(what):
            return named(f"{name}_{what}")

        self.st, self.mv, self.ve, self.rstd = (pair("st", [P, 6]), pair("mv", [P, 2]), pair("ve", [P, 1]),
                                                pair("rstd", [P, 1]))
        self.row = [[ctx.enter_context(nc.sbuf_tensor(f"{name}_row{k}{u}", [P, ROW], F32)) for u in range(4)]
                    for k in range(TOPK)]
        self.rT = pair("rT", [P, P])
        self.m8, self.ix, self.ixf = pair("m8", [P, 8]), pair("ix", [P, 8], U32), pair("ixf", [P, 2])
        self.hot = [pair("hota", [P, E]), pair("hotb", [P, E])]
        self.mask, self.cum = pair("mask", [P, E], BF16), pair("cum", [P, E], BF16)
        self.lg = pair("lg", [P, E])
        self.pf, self.junk, self.pk = pair("pf", [P, E]), pair("junk", [P, TOPK * E]), pair("pk", [P, 2])
        self.idx = [ctx.enter_context(nc.sbuf_tensor(f"{name}_idx{u}", [P, 2], U32)) for u in range(4)]
        self.ids = ctx.enter_context(nc.sbuf_tensor(f"{name}_ids", [P, 2], F32))
        self.ps_turn = ctx.enter_context(nc.psum_tensor(f"{name}_pt", [P, 512], F32))
        self.ps_log = ctx.enter_context(nc.psum_tensor(f"{name}_pl", [P, 512], F32))
        self.ps_pos = ctx.enter_context(nc.psum_tensor(f"{name}_pp", [P, 512], F32))
        self.s = {what: sem(what) for what in (
            "bn", "stats", "ve", "rstd", "rows", "copied", "turned", "kept", "logit", "lgd", "top", "gap", "index",
            "indexf", "hots", "masks", "cums", "pos", "pfd", "pkd", "idxd", "idw", "idn", "begun", "projd", "projk",
            "sqd", "ssm")}
        self.sent = [nc.alloc_semaphore(name=f"{name}_sent{u}") for u in range(4)]
        if self.similarity:
            self.pjT, self.sq = pair("pjT", [P, P]), pair("sq", [P, P])

    def x_of(self, t):
        return self.c.x[:, bass.ds(t * D, D)]

    def row_sent(self, eng, t, u):
        if not isinstance(t, int):
            eng.wait_ge(self.sent[u], (t - u) * (32 // 4))
        elif t >= 4:
            eng.wait_ge(self.sent[u], t // 4 * 32)

    def statistics(self, dve):
        nc = self.nc

        def sums(t, u):
            after(dve, self.x_ready, t)
            after(dve, self.s["stats"], t, back=2)
            apart(dve, t)
            nc.vector.bn_stats(self.st[u % 2][:, :], self.x_of(t)).then_inc(self.s["bn"], 1)

        def moments(t, u):
            after(dve, self.s["bn"], t)
            after(dve, self.s["ve"], t, back=2)
            apart(dve, t)
            nc.vector.bn_aggr(self.mv[u % 2][:, :], self.st[u % 2][:, :]).then_inc(self.s["stats"], 1)
        return sums, moments

    def normalise(self, dve):
        nc = self.nc

        def stage(t, u):
            after(dve, self.s["rstd"], t)
            self.row_sent(dve, t, u)
            nc.vector.tensor_scalar(self.row[0][u][:, 0:D], self.x_of(t), self.mv[u % 2][:, 0:1],
                                    self.rstd[u % 2][:, 0:1], ALU.subtract, ALU.mult).then_inc(self.s["rows"], 1)
        return stage

    def select(self, dve):
        nc, c = self.nc, self.c

        def keep(t, u):
            after(dve, self.s["logit"], t)
            if self.similarity:
                nc.vector.tensor_copy(c.squares[:, bass.ds(t, 1)], self.ps_log[:, E:E + 1]).then_inc(self.s["ssm"], 1)
                nc.vector.tensor_scalar(self.lg[u % 2][:, :], self.ps_log[:, 0:E], c.itemp[:, 0:1], None,
                                        ALU.mult).then_inc(self.s["lgd"], 1)
            else:
                nc.vector.tensor_copy(self.lg[u % 2][:, :], self.ps_log[:, 0:E]).then_inc(self.s["lgd"], 1)

        def best(t, u):
            after(dve, self.s["lgd"], t)
            apart(dve, t)
            nc.vector.max(self.m8[u % 2][:, :], self.lg[u % 2][:, :]).then_inc(self.s["top"], 1)

        def find(t, u):
            after(dve, self.s["top"], t)
            nc.vector.tensor_tensor(c.gap[:, bass.ds(t, 1)], self.m8[u % 2][:, 1:2], self.m8[u % 2][:, 0:1],
                                    ALU.subtract).then_inc(self.s["gap"], 1)
            nc.vector.max_index(self.ix[u % 2][:, :], self.m8[u % 2][:, :],
                                self.lg[u % 2][:, :]).then_inc(self.s["index"], 1)

        def as_float(t, u):
            after(dve, self.s["index"], t)
            nc.vector.tensor_copy(self.ixf[u % 2][:, :], self.ix[u % 2][:, 0:2]).then_inc(self.s["indexf"], 1)

        def one_hot(t, u):
            after(dve, self.s["indexf"], t)
            for k in range(TOPK):
                nc.vector.tensor_scalar(self.hot[k][u % 2][:, :], c.iota8[:, :], self.ixf[u % 2][:, k:k + 1], None,
                                        ALU.is_equal).then_inc(self.s["hots"], 1)

        def both(t, u):
            after(dve, self.s["hots"], t, per=TOPK)
            after(dve, self.s["pos"], t, back=1)
            nc.vector.tensor_tensor(self.mask[u % 2][:, :], self.hot[0][u % 2][:, :], self.hot[1][u % 2][:, :],
                                    ALU.add).then_inc(self.s["masks"], 1)

        def count(t, u):
            after(dve, self.s["masks"], t)
            if isinstance(t, int) and t == 0:
                nc.vector.memset(self.cum[1][:, :], 0.0).then_inc(self.s["begun"], 1)
                dve.wait_ge(self.s["begun"], 1)
            else:
                after(dve, self.s["cums"], t, back=1)
            nc.vector.tensor_tensor(self.cum[u % 2][:, :], self.cum[1 - u % 2][:, :], self.mask[u % 2][:, :],
                                    ALU.add).then_inc(self.s["cums"], 1)
        return keep, best, find, as_float, one_hot, both, count

    def place(self, dve):
        nc, c = self.nc, self.c

        def add_region(t, u):
            after(dve, self.s["pos"], t)
            nc.vector.tensor_tensor(self.pf[u % 2][:, :], self.ps_pos[:, 0:E], c.region[:, :],
                                    ALU.add).then_inc(self.s["pfd"], 1)

        def pick(t, u):
            after(dve, self.s["pfd"], t)
            for k in range(TOPK):
                nc.vector.scalar_tensor_tensor(out=self.junk[u % 2][:, k * E:(k + 1) * E], in0=self.hot[k][u % 2][:, :],
                                               scalar=1.0, in1=self.pf[u % 2][:, :], op0=ALU.mult, op1=ALU.mult,
                                               accum_out=self.pk[u % 2][:, k:k + 1]).then_inc(self.s["pkd"], 1)

        def as_row(t, u):
            after(dve, self.s["pkd"], t, per=TOPK)
            self.row_sent(dve, t, u)
            nc.vector.tensor_copy(self.idx[u][:, :], self.pk[u % 2][:, :]).then_inc(self.s["idxd"], 1)
        return add_region, pick, as_row

    def root(self, pool):
        nc, c = self.nc, self.c

        def stage(t, u):
            after(pool, self.s["stats"], t)
            apart(pool, t)
            nc.gpsimd.tensor_scalar(self.ve[u % 2][:, :], self.mv[u % 2][:, 1:2], LN_EPS, None, ALU.add).then_inc(self.s["ve"], 1)
            after(pool, self.s["ve"], t)
            after(pool, self.s["rows"], t, back=2)
            nc.gpsimd.tensor_tensor(self.rstd[u % 2][:, :], self.ve[u % 2][:, :], c.neghalf[:, 0:1],
                                    ALU.pow).then_inc(self.s["rstd"], 1)
        return stage

    def stamp(self, pool):
        nc = self.nc

        def stage(t, u):
            if isinstance(t, int) and t == 0:
                nc.gpsimd.iota(self.ids[:, :], [[T * P, TOPK]], base=0, channel_multiplier=1,
                               allow_small_or_imprecise_dtypes=True).then_inc(self.s["idn"], 1)
            after(pool, self.s["idn"], t)
            self.row_sent(pool, t, u)
            apart(pool, t)
            for k in range(TOPK):
                nc.gpsimd.tensor_copy(self.row[k][u][:, D:D + 1].bitcast(U32),
                                      self.ids[:, k:k + 1]).then_inc(self.s["idw"], 1)
            after(pool, self.s["idw"], t, per=TOPK)
            apart(pool, t)
            nc.gpsimd.tensor_scalar(self.ids[:, :], self.ids[:, :], float(P), None, ALU.add).then_inc(self.s["idn"], 1)
        return stage

    def send(self, pool):
        nc, c = self.nc, self.c

        def stage(t, u):
            after(pool, self.s["idw"], t, per=TOPK)
            after(pool, self.s["copied"], t)
            after(pool, self.s["idxd"], t)
            apart(pool, t)
            for k in range(TOPK):
                pool.indirect_dma_start(out=c.rows_x, out_offset=bass.IndirectOffsetOnAxis(
                    ap=self.idx[u][:, k:k + 1], axis=0), in_=self.row[k][u][:, :], in_offset=None
                ).then_inc(self.sent[u], 16)
        return stage

    def sent_all(self, pool):
        for u in range(4):
            pool.wait_ge(self.sent[u], 32 * T // 4)

    def copy_row(self, act):
        nc = self.nc

        def stage(t, u):
            after(act, self.s["rows"], t)
            nc.scalar.copy(self.row[1][u][:, 0:D], self.row[0][u][:, 0:D]).then_inc(self.s["copied"], 1)
        return stage

    def keep_turned(self, act):
        nc = self.nc

        def stage(t, u):
            after(act, self.s["turned"], t)
            after(act, self.s["projd"] if self.similarity else self.s["logit"], t, back=2)
            nc.scalar.copy(self.rT[u % 2][:, :], self.ps_turn[:, 0:P]).then_inc(self.s["kept"], 1)
        return stage

    def keep_projected(self, act):
        nc = self.nc

        def stage(t, u):
            after(act, self.s["projd"], t)
            after(act, self.s["logit"], t, back=2)
            nc.scalar.copy(self.pjT[u % 2][:, :], self.ps_turn[:, P:2 * P]).then_inc(self.s["projk"], 1)
            nc.scalar.activation(self.sq[u % 2][:, :], self.ps_turn[:, P:2 * P], ACT.Square).then_inc(self.s["sqd"], 1)
        return stage

    def turn(self, pe):
        nc, c = self.nc, self.c

        def stage(t, u):
            after(pe, self.s["rows"], t)
            after(pe, self.s["kept"], t, back=1)
            if self.similarity:
                after(pe, self.s["sqd"], t, back=1)
            nc.tensor.transpose(self.ps_turn[:, 0:P], self.row[0][u][:, 0:D], c.ident[:, :]).then_inc(self.s["turned"], 1)
        return stage

    def project(self, pe):
        nc, c = self.nc, self.c

        def stage(t, u):
            after(pe, self.s["kept"], t)
            after(pe, self.s["sqd"], t, back=1)
            nc.tensor.matmul(self.ps_turn[:, P:2 * P], c.wT[:, WP1, :], self.rT[u % 2][:, :], start=True,
                             stop=True).then_inc(self.s["projd"], 1)
        return stage

    def logits(self, pe):
        nc, c = self.nc, self.c

        def stage(t, u):
            after(pe, self.s["lgd"], t, back=1)
            if self.similarity:
                after(pe, self.s["sqd"], t)
                after(pe, self.s["ssm"], t, back=1)
                nc.tensor.matmul(self.ps_log[:, E:E + 1], self.sq[u % 2][:, :], c.onesc[:, 0:1], start=True, stop=True)
                nc.tensor.matmul(self.ps_log[:, 0:E], self.pjT[u % 2][:, :], c.snT[:, :], start=True,
                                 stop=True).then_inc(self.s["logit"], 1)
            else:
                after(pe, self.s["kept"], t)
                nc.tensor.matmul(self.ps_log[:, 0:E], self.rT[u % 2][:, :], c.wgT[:, :], start=True,
                                 stop=True).then_inc(self.s["logit"], 1)
        return stage

    def positions(self, pe):
        nc, c = self.nc, self.c

        def stage(t, u):
            after(pe, self.s["cums"], t)
            after(pe, self.s["pfd"], t, back=1)
            nc.tensor.matmul(self.ps_pos[:, 0:E], c.before[:, :], self.mask[u % 2][:, :], start=True, stop=False)
            nc.tensor.matmul(self.ps_pos[:, 0:E], c.onesb[:, :], self.cum[1 - u % 2][:, :], start=False,
                             stop=True).then_inc(self.s["pos"], 1)
        return stage

    def finish(self, nc, ctx):
        c, name = self.c, self.name
        named = ctx.enter_context(semaphores(nc))

        def sem(what):
            return named(f"{name}_{what}")

        counted, step, listed, pads = sem("counted"), sem("fstep"), sem("listed"), sem("pads")
        normed, gap_ready, powered, shared, gated = (
            sem(what) for what in ("normed", "gap_ready", "powered", "shared", "gated"))
        with ExitStack() as tmp:
            def tb(what, shape, dt=F32):
                return tmp.enter_context(nc.sbuf_tensor(f"{name}_{what}", shape, dt))

            cnt, part, nt, ct, one8 = (tb(w, [P, E]) for w in ("cnt", "part", "nt", "ct", "one8"))
            own, padf, padi = tb("own", [P, 1]), tb("padf", [P, E]), tb("padi", [P, E], U32)
            it, reached, starts = tb("it", [1, XT]), tb("reached", [1, XT, E]), tb("starts", [1, XT, E])
            sq, rn, eg, sg = (tb(w, [P, T]) for w in ("sq", "rn", "eg", "sg"))
            ef, sf, df, rf = (tb(w, [1, XT]) for w in ("ef", "sf", "df", "rf"))
            block = tmp.enter_context(nc.Block())

            @block.tensor
            def _(pe):
                nc.tensor.matmul(self.ps_pos[:, 0:E], c.onesb[:, :], self.cum[(T - 1) % 2][:, :], start=True,
                                 stop=True).then_inc(counted, 1)

            @block.vector
            def _(dve):
                n = [0]

                def then(ins):
                    ins.then_inc(step, 1)
                    n[0] += 1
                    dve.wait_ge(step, n[0])

                then(nc.vector.memset(one8[:, :], 1.0))
                dve.wait_ge(counted, 1)
                then(nc.vector.tensor_copy(cnt[:, :], self.ps_pos[:, 0:E]))
                then(nc.vector.tensor_scalar(part[:, :], cnt[:, :], 1.0 / P, 63.5 / P, ALU.mult, ALU.add))
                then(nc.vector.tensor_scalar(nt[:, :], part[:, :], ROUND, None, ALU.add))
                then(nc.vector.tensor_scalar(part[:, :], nt[:, :], -ROUND, None, ALU.add))
                then(nc.vector.tensor_tensor_scan(ct[:, :], one8[:, :], part[:, :], 0.0, ALU.mult, ALU.add))
                dve.wait_ge(pads, 2)
                then(nc.vector.scalar_tensor_tensor(out=padf[:, :], in0=cnt[:, :], scalar=own[:, 0:1],
                                                    in1=c.region[:, :], op0=ALU.add, op1=ALU.add))
                nc.vector.tensor_copy(padi[:, :], padf[:, :]).then_inc(listed, 1)
                then(nc.vector.tensor_tensor(reached[:, :, :], it[:, :].unsqueeze(2).to_broadcast([1, XT, E]),
                                             ct[0:1, :].unsqueeze(1).to_broadcast([1, XT, E]), ALU.is_ge))
                then(nc.vector.tensor_tensor(starts[:, :, :], reached[:, :, :],
                                             part[0:1, :].unsqueeze(1).to_broadcast([1, XT, E]), ALU.mult))
                then(nc.vector.tensor_reduce(ef[:, :], reached[:, :, :], AX.X, ALU.add))
                then(nc.vector.tensor_reduce(sf[:, :], starts[:, :, :], AX.X, ALU.add))
                then(nc.vector.tensor_tensor(df[:, :], it[:, :], sf[:, :], ALU.subtract))
                then(nc.vector.scalar_tensor_tensor(out=rf[:, :], in0=ef[:, :], scalar=float(REGION // P),
                                                    in1=df[:, :], op0=ALU.mult, op1=ALU.add))
                nc.vector.tensor_scalar(c.tile_e[:, :], ef[:, :], float(E - 1), None, ALU.min).then_inc(listed, 1)
                nc.vector.tensor_copy(c.tile_r[:, :], rf[:, :]).then_inc(listed, 1)
                if self.similarity:
                    dve.wait_ge(normed, 2)
                    nc.vector.tensor_tensor(c.gap[:, :], c.gap[:, :], rn[:, :], ALU.mult).then_inc(gap_ready, 1)
                dve.wait_ge(powered, 1)
                nc.vector.tensor_scalar(sg[:, :], eg[:, :], 1.0, None, ALU.add).then_inc(shared, 1)
                dve.wait_ge(shared, 1)
                nc.vector.reciprocal(c.gate[:, 0, :], sg[:, :]).then_inc(gated, 1)
                dve.wait_ge(gated, 1)
                nc.vector.tensor_tensor(c.gate[:, 1, :], eg[:, :], c.gate[:, 0, :], ALU.mult).then_inc(gated, 1)

            @block.scalar
            def _(act):
                if self.similarity:
                    act.wait_ge(gap_ready, 1)
                nc.scalar.activation(eg[:, :], c.gap[:, :], ACT.Exp).then_inc(powered, 1)

            @block.gpsimd
            def _(pool):
                nc.gpsimd.iota(own[:, :], [[0, 1]], base=0, channel_multiplier=1,
                               allow_small_or_imprecise_dtypes=True).then_inc(pads, 1)
                nc.gpsimd.iota(it[:, :], [[1, XT]], base=0, channel_multiplier=0,
                               allow_small_or_imprecise_dtypes=True).then_inc(pads, 1)
                if self.similarity:
                    nc.gpsimd.tensor_scalar(sq[:, :], c.squares[:, :], L2_EPS * L2_EPS, None, ALU.max).then_inc(normed, 1)
                    pool.wait_ge(normed, 1)
                    nc.gpsimd.tensor_tensor(rn[:, :], sq[:, :], c.neghalf[:, :], ALU.pow).then_inc(normed, 1)
                pool.wait_ge(listed, 1)
                for e in range(E):
                    pool.indirect_dma_start(out=c.rows_x, out_offset=bass.IndirectOffsetOnAxis(
                        ap=padi[:, e:e + 1], axis=0), in_=c.padrow[:, e, :], in_offset=None).then_inc(self.sent[0], 16)
                pool.wait_ge(self.sent[0], 32 * T // 4 + 16 * E)


def make_masks(nc, c, picked):
    pool = nc.gpsimd
    pool.memset(c.pick[:, :, :], 0.0).then_inc(picked, 1)
    for m in (c.mask_q, c.mask_k):
        pool.memset(m[:, :], 0.0).then_inc(picked, 1)
    for k in range(3):
        pool.wait_ge(picked, k + 3)
        pool.affine_select(out=c.pick[:, :, :], in_=c.pick[:, :, :], compare_op=ALU.not_equal, fill=1.0, base=-32 * k,
                           pattern=[[-1, H], [0, P]], channel_multiplier=1).then_inc(picked, 1)
    for m, sign in ((c.mask_q, 1), (c.mask_k, -1)):
        pool.affine_select(out=m[:, :], in_=m[:, :], compare_op=ALU.is_ge, fill=-1e9, base=0,
                           pattern=[[0, 4], [-sign, P]], channel_multiplier=sign).then_inc(picked, 1)


def run_experts(nc, c, name, b1_column, with_masks=False):
    RING = 8
    AHEAD = 7
    with ExitStack() as ctx:
        named = ctx.enter_context(semaphores(nc))

        def ring(what, shape, dt=F32, n=RING):
            return [ctx.enter_context(nc.sbuf_tensor(f"{name}_{what}{u}", shape, dt)) for u in range(n)]

        def banks(what, n=2):
            return [ctx.enter_context(nc.psum_tensor(f"{name}_{what}{u}", [P, 512], F32)) for u in range(n)]

        def sem(what):
            return named(f"{name}_{what}")

        xr, xT, w1s = ring("xr", [P, ROW]), ring("xT", [P, P], n=4), ring("w1s", [P, F], n=2)
        b1s, hT, yb = ring("b1s", [P, FC], n=4), ring("hT", [P, F], n=4), ring("yb", [P, D])
        di = ring("di", [P, 1], U32)
        ps_x, ps_h, ps_y = banks("px", 1), banks("ph"), banks("py")
        loaded = [sem(f"loaded{u}") for u in range(RING)]
        did, xTd, xTk, w1k, b1k, hd, hTk, yd, ybd = (
            sem(s) for s in ("did", "xTd", "xTk", "w1k", "b1k", "hd", "hTk", "yd", "ybd"))
        sent = [nc.alloc_semaphore(name=f"{name}_sent{u}") for u in range(RING)]
        rows = c.rows_x.rearrange("(n p) d -> n p d", p=P)
        block = ctx.enter_context(nc.Block())

        def expert_of(eng, held):
            def stage(i, u):
                held[:] = [eng.value_load(c.tile_e[0:1, bass.ds(i, 1)], min_val=0, max_val=E - 1)]
            return stage

        def of_ring(eng, sems, i, u, back=0):
            if not isinstance(i, int):
                eng.wait_ge(sems[u], (i - u) * (16 // RING) + 16 * (1 - back))
            elif i // RING + 1 - back > 0:
                eng.wait_ge(sems[u], 16 * (i // RING + 1 - back))

        @block.sync
        def _(sp):
            def load(i, u):
                after(sp, xTd, i, back=RING)
                after(sp, did, i, back=RING)
                apart(sp, i)
                r = sp.value_load(c.tile_r[0:1, bass.ds(i, 1)], min_val=0, max_val=NROWS // P - 1)
                sp.dma_start(xr[u][:, :], rows[bass.ds(r, 1), :, :].rearrange("n p d -> (n p) d")
                             ).then_inc(loaded[u], 16)

            pipeline(sp, XT, [(load, AHEAD)], AHEAD, start=RING, ring=RING)

        @block.tensor
        def _(pe):
            pe.wait_ge(c.e_in, E_LOADS)
            expert = []

            def turn(i, u):
                of_ring(pe, loaded, i, u)
                after(pe, xTk, i, back=1)
                nc.tensor.transpose(ps_x[0][:, 0:P], xr[u][:, 0:D], c.ident[:, :]).then_inc(xTd, 1)

            def up(i, u):
                after(pe, xTk, i)
                after(pe, w1k, i)
                after(pe, hTk, i, back=2)
                for k in range(FC):
                    mm = nc.tensor.matmul(ps_h[u % 2][:, k * P:(k + 1) * P], w1s[u % 2][:, k * P:(k + 1) * P],
                                          xT[u % 4][:, :], start=True, stop=True)
                mm.then_inc(hd, 1)

            def down(i, u):
                after(pe, hTk, i)
                after(pe, ybd, i, back=2)
                for k in range(FC):
                    mm = nc.tensor.matmul(ps_y[u % 2][:, 0:D], hT[u % 4][:, k * P:(k + 1) * P],
                                          c.w2[:, bass.ds(expert[0] * FC + k, 1), :], start=(k == 0),
                                          stop=(k == FC - 1))
                mm.then_inc(yd, 1)

            pipeline(pe, XT, [(turn, 4), (up, 3), (expert_of(pe, expert), 1), (down, 1)], AHEAD, start=RING, ring=RING)

        @block.scalar
        def _(act):
            def keep_x(i, u):
                after(act, xTd, i)
                after(act, hd, i, back=4)
                nc.scalar.copy(xT[u % 4][:, :], ps_x[0][:, 0:P]).then_inc(xTk, 1)

            def gelu(i, u):
                after(act, hd, i)
                after(act, b1k, i)
                after(act, yd, i, back=4)
                for k in range(FC):
                    ins = nc.scalar.activation(hT[u % 4][:, k * P:(k + 1) * P], ps_h[u % 2][:, k * P:(k + 1) * P],
                                               ACT.Gelu, bias=b1s[u % 4][:, k:k + 1])
                ins.then_inc(hTk, 1)

            pipeline(act, XT, [(keep_x, 4), (gelu, 3)], AHEAD, start=RING, ring=RING)

        @block.vector
        def _(dve):
            dve.wait_ge(c.e_in, E_LOADS)
            for_w1, for_y = [], []

            def take_w1(i, u):
                after(dve, hd, i, back=2)
                nc.vector.tensor_copy(w1s[u % 2][:, :], c.w1[:, bass.ds(for_w1[0], 1), :].rearrange(
                    "p e f -> p (e f)")).then_inc(w1k, 1)
                after(dve, hTk, i, back=4)
                nc.vector.tensor_copy(b1s[u % 4][:, :], c.wT[:, VECS, bass.ds(for_w1[0] * FC + b1_column, FC)]
                                      ).then_inc(b1k, 1)

            def bias_y(i, u):
                after(dve, yd, i)
                of_ring(dve, sent, i, u, back=1)
                nc.vector.tensor_tensor(yb[u][:, :], ps_y[u % 2][:, 0:D], c.b2bc[:, bass.ds(for_y[0] * D, D)],
                                        ALU.add).then_inc(ybd, 1)

            pipeline(dve, XT, [(expert_of(dve, for_w1), 4), (take_w1, 4), (expert_of(dve, for_y), 1), (bias_y, 1)],
                     AHEAD, start=RING, ring=RING)

        @block.gpsimd
        def _(pool):
            if with_masks:
                make_masks(nc, c, sem("picked"))

            def note(i, u):
                of_ring(pool, loaded, i, u)
                of_ring(pool, sent, i, u, back=1)
                apart(pool, i)
                nc.gpsimd.tensor_copy(di[u][:, :], xr[u][:, D:D + 1].bitcast(U32)).then_inc(did, 1)

            def send(i, u):
                after(pool, did, i)
                after(pool, ybd, i)
                apart(pool, i)
                pool.indirect_dma_start(out=c.res, out_offset=bass.IndirectOffsetOnAxis(
                    ap=di[u][:, 0:1], axis=0), in_=yb[u][:, :], in_offset=None
                ).then_inc(sent[u], 16)

            pipeline(pool, XT, [(send, 0), (note, 4)], AHEAD, start=RING, ring=RING)
            for u in range(RING):
                pool.wait_ge(sent[u], 16 * XT // RING)


def head_attention(nc, outer, c, r):
    HH, W = H * H, 3 * H * DH
    AHEAD = 6
    x1 = outer.enter_context(semaphores(nc))("a_x1")
    r.open(nc, outer, x1)
    with ExitStack() as ctx:
        def pair(name, shape, dt=F32):
            return [ctx.enter_context(nc.sbuf_tensor(f"a_{name}{u}", shape, dt)) for u in range(2)]

        def banks(name):
            return [ctx.enter_context(nc.psum_tensor(f"a_{name}{u}", [P, 512], F32)) for u in range(2)]

        named = ctx.enter_context(semaphores(nc))

        def sem(name):
            return named("a_" + name)

        st, mv, ve, rstd = pair("st", [P, 6]), pair("mv", [P, 2]), pair("ve", [P, 1]), pair("rstd", [P, 1])
        nmr = pair("nmr", [P, 1])
        xn, xnT, qkv = pair("xn", [P, D]), pair("xnT", [P, P]), pair("qkv", [P, W])
        prod = ctx.enter_context(nc.sbuf_tensor("a_prod", [P, HH * DH], F32))
        sc, mx, ss, ex = pair("sc", [P, HH]), pair("mx", [P, H]), pair("ss", [P, HH]), pair("ex", [P, HH])
        sm, rs, pr = pair("sm", [P, H]), pair("rs", [P, H]), pair("pr", [P, HH])
        pv, oT = pair("pv", [P, H, H * DH]), pair("oT", [P, P])
        ps_t1, ps_qkv, ps_o1, ps_p = (ctx.enter_context(nc.psum_tensor("a_t", [P, 512], F32)), banks("q"),
                                      ctx.enter_context(nc.psum_tensor("a_o", [P, 512], F32)),
                                      ctx.enter_context(nc.psum_tensor("a_p", [P, 512], F32)))
        ps_t, ps_o = [ps_t1, ps_t1], [ps_o1, ps_o1]
        nmrd = sem("nmr")
        bn, stats, ved, rstdd, xnd = sem("bn"), sem("stats"), sem("ve"), sem("rstd"), sem("xn")
        xT, xTk, qk, qkk = sem("xT"), sem("xTk"), sem("qk"), sem("qkk")
        prodd, scd, mxd, ssd, exd = sem("prod"), sem("sc"), sem("mx"), sem("ss"), sem("ex")
        smd, rsd, prd, pvd, od, ok, pj = (sem("sm"), sem("rs"), sem("pr"), sem("pv"), sem("o"), sem("ok"),
                                          sem("pj"))
        wqkvT = c.wT[:, QKV0:QKV0 + 3, :].rearrange("p s f -> p (s f)")
        wprojT = c.wT[:, PROJ0, :]
        HALVES = 2 * SINKHORN
        summed, scaled = sem("summed"), sem("scaled")
        block = ctx.enter_context(nc.Block())

        def x_of(t):
            return c.x[:, bass.ds(t * D, D)]

        @block.vector
        def _(dve):
            dve.wait_ge(c.x_in, 16)

            def products(t, u):
                after(dve, qkk, t)
                after(dve, scd, t, back=1)
                hd = qkv[u % 2][:, :].rearrange("p (h k) -> p h k", h=H)
                q = hd[:, :, 0:DH].unsqueeze(2).to_broadcast([P, H, H, DH])
                k = hd[:, :, DH:2 * DH].unsqueeze(1).to_broadcast([P, H, H, DH])
                nc.vector.tensor_tensor(prod[:, :].rearrange("p (h g d) -> p h g d", h=H, g=H), q, k,
                                        ALU.mult).then_inc(prodd, 1)

            def scores(t, u):
                after(dve, prodd, t)
                nc.vector.tensor_reduce(sc[u % 2][:, :], prod[:, :].rearrange("p (a d) -> p a d", d=DH), AX.X,
                                        ALU.add).then_inc(scd, 1)

            def maxima(t, u):
                after(dve, scd, t)
                nc.vector.tensor_reduce(mx[u % 2][:, :], sc[u % 2][:, :].rearrange("p (h g) -> p h g", h=H), AX.X,
                                        ALU.max).then_inc(mxd, 1)

            def less_max(t, u):
                after(dve, mxd, t)
                after(dve, exd, t, back=2)
                nc.vector.tensor_tensor(ss[u % 2][:, :].rearrange("p (h g) -> p h g", h=H),
                                        sc[u % 2][:, :].rearrange("p (h g) -> p h g", h=H),
                                        mx[u % 2][:, :].unsqueeze(2).to_broadcast([P, H, H]),
                                        ALU.subtract).then_inc(ssd, 1)

            def moments_1(t, u):
                after(dve, stats, t, back=2)
                nc.vector.bn_stats(st[u % 2][:, :], x_of(t)).then_inc(bn, 1)

            def moments_2(t, u):
                after(dve, bn, t)
                after(dve, nmrd, t, back=2)
                apart(dve, t)
                nc.vector.bn_aggr(mv[u % 2][:, :], st[u % 2][:, :]).then_inc(stats, 1)

            def sums(t, u):
                after(dve, exd, t)
                nc.vector.tensor_reduce(sm[u % 2][:, :], ex[u % 2][:, :].rearrange("p (h g) -> p h g", h=H), AX.X,
                                        ALU.add).then_inc(smd, 1)

            def inverses(t, u):
                after(dve, smd, t)
                nc.vector.reciprocal(rs[u % 2][:, :], sm[u % 2][:, :]).then_inc(rsd, 1)

            def probabilities(t, u):
                after(dve, rsd, t)
                after(dve, pvd, t, back=2)
                nc.vector.tensor_tensor(pr[u % 2][:, :].rearrange("p (h g) -> p h g", h=H),
                                        ex[u % 2][:, :].rearrange("p (h g) -> p h g", h=H),
                                        rs[u % 2][:, :].unsqueeze(2).to_broadcast([P, H, H]),
                                        ALU.mult).then_inc(prd, 1)

            def residual(t, u):
                after(dve, pj, t)
                nc.vector.tensor_tensor(x_of(t), ps_p[:, 0:D], x_of(t), ALU.add).then_inc(x1, 1)

            def balance(t, u):
                if isinstance(t, int) and t >= HALVES:
                    return
                after(dve, summed, t)
                nc.vector.reciprocal(c.rc[:, u % 2:u % 2 + 1], ps_p[0:NS, 2 * P:2 * P + 1]).then_inc(scaled, 1)

            add_region, pick, as_row = r.place(dve)
            r_sums, r_moments = r.statistics(dve)
            keep, best, find, as_float, one_hot, both, count = r.select(dve)
            pipeline(dve, T, [(moments_1, 6), (r_sums, 2), (moments_2, 6), (r_moments, 2), (products, 5), (keep, 1),
                              (scores, 5), (best, 1), (add_region, 0), (maxima, 5), (pick, 0), (find, 1), (less_max, 5),
                              (as_row, 0), (as_float, 1), (one_hot, 1), (r.normalise(dve), 2), (both, 1),
                              (residual, 3), (balance, 0), (sums, 5), (count, 1), (inverses, 5), (probabilities, 5)], AHEAD, start=4,
                     ring=4)

        @block.gpsimd
        def _(pool):
            def weigh(t, u):
                after(pool, prd, t)
                after(pool, qkk, t)
                after(pool, od, t, back=2)
                p_ = pr[u % 2][:, :].rearrange("p (h g) -> p g h", h=H).unsqueeze(3).to_broadcast([P, H, H, DH])
                v = qkv[u % 2][:, :].rearrange("p (g k) -> p g k", g=H)[:, :, 2 * DH:3 * DH]
                v = v.unsqueeze(2).to_broadcast([P, H, H, DH])
                nc.gpsimd.tensor_tensor(pv[u % 2][:, :, :].rearrange("p g (h d) -> p g h d", h=H), p_, v,
                                        ALU.mult).then_inc(pvd, 1)

            def root(t, u):
                after(pool, stats, t)
                apart(pool, t)
                nc.gpsimd.tensor_scalar(ve[u % 2][:, :], mv[u % 2][:, 1:2], LN_EPS, None, ALU.add).then_inc(ved, 1)
                after(pool, ved, t)
                after(pool, xnd, t, back=2)
                nc.gpsimd.tensor_tensor(rstd[u % 2][:, :], ve[u % 2][:, :], c.neghalf[:, 0:1], ALU.pow).then_inc(rstdd, 1)
                after(pool, rstdd, t)
                apart(pool, t)
                nc.gpsimd.tensor_scalar(nmr[u % 2][:, :], mv[u % 2][:, 0:1], rstd[u % 2][:, 0:1], -1.0, ALU.mult,
                                        ALU.mult).then_inc(nmrd, 1)

            pipeline(pool, T, [(root, 6), (r.root(pool), 2), (r.stamp(pool), 2), (weigh, 4), (r.send(pool), 0)], AHEAD,
                     start=4, ring=4)
            r.sent_all(pool)

        @block.scalar
        def _(act):
            act.wait_ge(c.x_in, 16)

            def expo(t, u):
                after(act, ssd, t)
                after(act, prd, t, back=2)
                nc.scalar.activation(ex[u % 2][:, :], ss[u % 2][:, :], ACT.Exp, scale=0.125).then_inc(exd, 1)

            def normalise(t, u):
                after(act, xT, t, back=2)
                after(act, nmrd, t)
                apart(act, t)
                nc.scalar.activation(xn[u % 2][:, :], x_of(t), ACT.Identity, bias=nmr[u % 2][:, 0:1],
                                     scale=rstd[u % 2][:, 0:1]).then_inc(xnd, 1)

            def keep_out(t, u):
                after(act, od, t)
                after(act, pj, t, back=2)
                nc.scalar.copy(oT[u % 2][:, :], ps_o[u % 2][:, 0:P]).then_inc(ok, 1)

            def keep_turned(t, u):
                after(act, xT, t)
                after(act, qk, t, back=2)
                nc.scalar.copy(xnT[u % 2][:, :], ps_t[u % 2][:, 0:P]).then_inc(xTk, 1)

            def keep_qkv(t, u):
                after(act, qk, t)
                after(act, pvd, t, back=2)
                nc.scalar.copy(qkv[u % 2][:, :], ps_qkv[u % 2][:, 0:W]).then_inc(qkk, 1)

            pipeline(act, T, [(normalise, 6), (keep_out, 3), (expo, 5), (keep_turned, 6), (r.copy_row(act), 2), (keep_qkv, 6),
                             (r.keep_turned(act), 2)], AHEAD, start=4, ring=4)

        @block.tensor
        def _(pe):
            def sum_out(t, u):
                after(pe, pvd, t)
                after(pe, ok, t, back=1)
                for g in range(H):
                    mm = nc.tensor.matmul(ps_o[u % 2][:, 0:P], pv[u % 2][:, g, :], c.ident[:, :], start=(g == 0),
                                          stop=(g == H - 1))
                mm.then_inc(od, 1)

            def project(t, u):
                after(pe, ok, t)
                after(pe, x1, t, back=1)
                nc.tensor.matmul(ps_p[:, 0:D], oT[u % 2][:, :], wprojT, start=True, stop=False)
                nc.tensor.matmul(ps_p[:, 0:D], c.ones[:, :], c.rows[:, R_PROJ, :], start=False,
                                 stop=True).then_inc(pj, 1)

            def balance_sums(t, u):
                if isinstance(t, int) and t >= HALVES:
                    return
                after(pe, scaled, t, back=1)
                after(pe, x1, t, back=-2)
                apart(pe, t)
                nc.tensor.matmul(ps_p[0:NS, 2 * P:2 * P + 1], (c.k0T, c.k0)[u % 2][:, :],
                                 c.rc[:, 1 - u % 2:2 - u % 2], start=True, stop=True).then_inc(summed, 1)

            def turn(t, u):
                after(pe, xnd, t)
                after(pe, xTk, t, back=1)
                nc.tensor.transpose(ps_t[u % 2][:, 0:P], xn[u % 2][:, :], c.ident[:, :]).then_inc(xT, 1)

            def make_qkv(t, u):
                after(pe, xTk, t)
                after(pe, qkk, t, back=2)
                nc.tensor.matmul(ps_qkv[u % 2][:, 0:W], xnT[u % 2][:, :], wqkvT, start=True, stop=True).then_inc(qk, 1)

            pipeline(pe, T, [(r.positions(pe), 0), (sum_out, 3), (balance_sums, 0), (project, 3), (turn, 6), (make_qkv, 6), (r.turn(pe), 2),
                            (r.logits(pe), 2)], AHEAD, start=4, ring=4)


def causal_attention(nc, c):
    R, AHEAD, FILLS = 4, 4, 12
    TB = S // P
    SCALE = float(DH) ** -0.5
    with ExitStack() as ctx:
        named = ctx.enter_context(semaphores(nc))

        def ring(name, shape, dt=F32, n=R):
            return [ctx.enter_context(nc.sbuf_tensor(f"c_{name}{u}", shape, dt)) for u in range(n)]

        def one(name, shape, dt=F32):
            return ctx.enter_context(nc.sbuf_tensor(f"c_{name}", shape, dt))

        def bank(name):
            return ctx.enter_context(nc.psum_tensor(f"c_{name}", [P, 512], F32))

        def sem(name):
            return named("c_" + name)

        y = ring("y", [P, TOPK, TB, D])
        st, mv, ve, rstd = ring("st", [P, TB, 6]), ring("mv", [P, TB, 2]), ring("ve", [P, TB]), ring("rstd", [P, TB])
        z, uu, state, xdT = ring("z", [P, TB, D], n=1), ring("uu", [P, S], n=1), ring("state", [P, 1 + S], n=1), \
            ring("xdT", [P, S], n=1)
        xs, eg, gd, gr, mb = ring("xs", [P, 1]), ring("eg", [P, 1]), ring("gd", [P, 1]), ring("gr", [P, 1]), \
            ring("mb", [P, P], n=1)
        junk, ss, se, rs = one("junk", [P, TB, D]), ring("ss", [P, TB]), ring("se", [P, TB]), ring("rs", [P, TB])
        nd, ndT = ring("nd", [P, TB, D], n=1), ring("ndT", [P, S], n=1)
        qk, left1, left2 = ring("qk", [P, 2, S], n=1), one("left1", [P, 2, S]), one("left2", [P, 2, S])
        part = [ring(f"part{k}", [P, 2, S], BF16, n=1) for k in range(3)]
        qs, ks = ring("qs", [KP, H // 2, S], BF16), ring("ks", [KP, H, S], BF16)
        va = ring("va", [P, TB, H, 32])
        mx, nm, m1, m2 = ring("mx", [P, TB, H]), ring("nm", [P, TB, H], n=1), ring("m1", [P, TB, H], n=1), \
            ring("m2", [P, TB, H], n=1)
        mp, mT = ring("mp", [P, TB, 3, 32], BF16, n=1), ring("mT", [KP, S], BF16)
        pt = ring("pt", [P, 512], n=4)
        oTs, on, oT, rd = ring("oTs", [P, 4, S], n=1), ring("on", [P, TB, D], n=1), ring("oT", [P, S], n=1), \
            ring("rd", [P, TB, H], n=1)
        hr, hTe = one("hr", [NS, NS]), one("hTe", [NS, NS, SD])
        ps_c2, ps_c3 = [bank("s0"), bank("s1")], [bank("e0"), bank("e1")]
        ps_pv, ps_t, ps_q, ps_o = bank("pv"), bank("t"), bank("q"), bank("o")
        ps_tb = ps_t[:, :].bitcast(BF16)

        names = ("preset preset2 zeroed built hT comb1 comb bn stats ve rstd zd zT uud scan xd xsd gate egd gdd grd mbd mh mhx xdr sq xdk se rs "
                 "ndd ndTd ndTk qkd qkk vd vk p0 l1 p1 l2 p2 s2 mxd nmd a1 b1 a2 b2 a3 mTd mTk s3 exd pvd otk on0 rd0 "
                 "nrm0 on1 rd1 nrm1 oT2 oT2k ao rr rx").split()
        s = {n: sem(n) for n in names}
        ydma = [sem(f"y{u}") for u in range(R)]
        parts, stack = [sem(f"parts{u}") for u in range(R)], [sem(f"stack{u}") for u in range(R)]
        spread = [nc.dram_tensor(f"spread{u}", (2, 3, DH, H, S), BF16, kind="Internal").ap() for u in range(R)]
        c.c_done = s["rx"]
        wq, wk, wv = (c.wT[:, IN1 + k, :] for k in range(3))
        wo = c.wT[:, OUT1, :]
        block = ctx.enter_context(nc.Block())

        def xb(b):
            return c.x[:, bass.ds(b * (TB * D), TB * D)]

        def rb(b):
            return c.r[:, bass.ds(b * (TB * D), TB * D)]

        def nth(eng, sm, b, k=0, per=1, back=0):
            n = b * per + (k + 1 - back)
            if isinstance(n, int):
                n = min(n, B * per)
                if n <= 0:
                    return
            eng.wait_ge(sm, n)

        def of_ring(eng, sems, b, u, each, back=0):
            if isinstance(b, int):
                if b // R + 1 - back > 0:
                    eng.wait_ge(sems[u], each * (b // R + 1 - back))
            else:
                eng.wait_ge(sems[u], (b - u) * (each // R) + each * (1 - back))

        def heads2(k):
            return (0, range(4 * k, 4 * k + 4)) if k < 4 else (1, range(2 * (k - 4), 2 * (k - 4) + 2))

        def heads3(k):
            g, i = divmod(k, 3)
            return (0, range(4 * g + 2 * i, 4 * g + 2 * i + 2)) if i < 2 else (1, range(4 * g, 4 * g + 4))

        NSTACK, NPARTS, NY = 12 * 16, 6 * 16, 3 * 16

        @block.sync
        def _(sp):
            def results(b, u):
                nth(sp, s["comb"], b, back=R)
                src = c.res[0:TOPK * T * P, :].rearrange("(k t p) d -> k p t d", k=TOPK, p=P)
                sp.dma_start(y[u][:, 0, :, :], src[0, :, bass.ds(b * TB, TB), :]).then_inc(ydma[u], 16)
                for j in range(TB):
                    sp.dma_start(y[u][:, 1, j:j + 1, :], src[1, :, bass.ds(b * TB + j, 1), :]).then_inc(ydma[u], 16)

            def stacks(b, u):
                of_ring(sp, stack, b, u, NSTACK, back=1)
                apart(sp, b)
                nth(sp, s["p2"], b)
                for k in range(3):
                    for side in range(2):
                        sp.dma_start(spread[u][side, k].rearrange("d h q -> h d q"),
                                     part[k][0][:, side, :]).then_inc(parts[u], 16)
                nth(sp, s["s3"], b, k=FILLS - 1, per=FILLS, back=R * FILLS)
                of_ring(sp, parts, b, u, NPARTS)
                if isinstance(b, int) and b < R:
                    sp.wait_ge(s["zeroed"], b + 1)
                for par in range(2):
                    row = 48 * par
                    for first, n in ((0, 3), (1, 2), (2, 1)):
                        rows = slice(row, row + 8 * n)
                        half = slice(par * H // 2, (par + 1) * H // 2)
                        sp.dma_start(qs[u][rows, :, :], spread[u][0, first:first + 1, :, half, :]
                                     .to_broadcast([n, DH, H // 2, S])).then_inc(stack[u], 16)
                        sp.dma_start(ks[u][rows, half, :], spread[u][1, 0:n, :, half, :]).then_inc(stack[u], 16)
                        row += 8 * n

            pipeline(sp, B, [(results, AHEAD + 1), (stacks, 3)], AHEAD + 1, start=2, ring=R)

        @block.gpsimd
        def _(pool):
            nc.gpsimd.memset(state[0][:, 0:1], 0.0).then_inc(s["preset"], 1)
            nc.gpsimd.memset(mp[0][:, :, :, :], 0.0).then_inc(s["preset"], 1)

            def ones_of(b, u):
                if isinstance(b, int) and b < R:
                    nc.gpsimd.memset(va[u][:, :, :, :], 0.0).then_inc(s["preset2"], 1)
                    pool.wait_ge(s["preset2"], 2 * b + 1)
                    nc.gpsimd.memset(va[u][:, :, :, DH:DH + 1], 1.0).then_inc(s["preset2"], 1)

            def root(b, u):
                after(pool, s["stats"], b)
                apart(pool, b)
                nc.gpsimd.tensor_scalar(ve[u][:, :], mv[u][:, :, 1], LN_EPS, None, ALU.add).then_inc(s["ve"], 1)
                after(pool, s["ve"], b)
                nc.gpsimd.tensor_tensor(rstd[u][:, :], ve[u][:, :], c.neghalf[:, 0:TB], ALU.pow).then_inc(s["rstd"], 1)

            def root2(b, u):
                nth(pool, s["sq"], b, k=1, per=2)
                apart(pool, b)
                nc.gpsimd.tensor_scalar(se[u][:, :], ss[u][:, :], 1.0 / D, RMS_EPS, ALU.mult, ALU.add).then_inc(s["se"], 1)
                after(pool, s["se"], b)
                nc.gpsimd.tensor_tensor(rs[u][:, :], se[u][:, :], c.neghalf[:, 0:TB], ALU.pow).then_inc(s["rs"], 1)

            def split(b, u):
                nth(pool, s["qkk"], b, k=1, per=2)
                of_ring(pool, parts, b - 1, (u - 1) % R, NPARTS)
                apart(pool, b)
                nc.gpsimd.tensor_copy(part[0][0][:, :, :], qk[0][:, :, :]).then_inc(s["p0"], 1)
                after(pool, s["p0"], b)
                nc.gpsimd.tensor_tensor(left1[:, :, :], qk[0][:, :, :], part[0][0][:, :, :],
                                        ALU.subtract).then_inc(s["l1"], 1)
                after(pool, s["l1"], b)
                apart(pool, b)
                nc.gpsimd.tensor_copy(part[1][0][:, :, :], left1[:, :, :]).then_inc(s["p1"], 1)
                after(pool, s["p1"], b)
                nc.gpsimd.tensor_tensor(part[2][0][:, :, :], left1[:, :, :], part[1][0][:, :, :],
                                        ALU.subtract).then_inc(s["p2"], 1)

            def split_max(b, u):
                nth(pool, s["mxd"], b, k=FILLS - 1, per=FILLS)
                after(pool, s["mTd"], b, back=1)
                if isinstance(b, int) and b == 0:
                    pool.wait_ge(s["preset"], 2)
                apart(pool, b)
                nc.gpsimd.tensor_scalar(nm[0][:, :, :], mx[u][:, :, :], -1.0, None, ALU.mult).then_inc(s["nmd"], 1)
                after(pool, s["nmd"], b)
                apart(pool, b)
                nc.gpsimd.tensor_copy(mp[0][:, :, 0, 0:H], nm[0][:, :, :]).then_inc(s["a1"], 1)
                after(pool, s["a1"], b)
                nc.gpsimd.tensor_tensor(m1[0][:, :, :], nm[0][:, :, :], mp[0][:, :, 0, 0:H],
                                        ALU.subtract).then_inc(s["b1"], 1)
                after(pool, s["b1"], b)
                apart(pool, b)
                nc.gpsimd.tensor_copy(mp[0][:, :, 1, 0:H], m1[0][:, :, :]).then_inc(s["a2"], 1)
                after(pool, s["a2"], b)
                nc.gpsimd.tensor_tensor(mp[0][:, :, 2, 0:H], m1[0][:, :, :], mp[0][:, :, 1, 0:H],
                                        ALU.subtract).then_inc(s["a3"], 1)

            pipeline(pool, B, [(root, AHEAD), (ones_of, AHEAD), (split, 3), (root2, AHEAD), (split_max, 2)], AHEAD, start=2, ring=R)

        @block.vector
        def _(dve):
            dve.wait_ge(s["preset"], 2)
            nc.vector.tensor_scalar(hr[:, :], c.k0[:, :], c.rc[:, 0:1], None, ALU.mult).then_inc(s["built"], 1)
            dve.wait_ge(s["hT"], 1)
            nc.vector.tensor_scalar(hTe[:, :, :], ps_o[0:NS, 0:NS].unsqueeze(2).to_broadcast([NS, NS, SD]),
                                    c.rc[:, 1:2], None, ALU.mult).then_inc(s["built"], 1)
            dve.wait_ge(s["hT"], 2)
            nc.vector.tensor_tensor(c.hbig[:, :], ps_o[:, P:2 * P], c.dmask[:, :], ALU.mult).then_inc(s["built"], 1)
            dve.wait_ge(s["built"], 3)

            def combine(b, u):
                of_ring(dve, ydma, b, u, NY)
                for k, done in ((0, "comb1"), (1, "comb")):
                    for j in range(TB):
                        v = c.x[:, bass.ds(b * (TB * D) + j * D, D)]
                        ins = nc.vector.scalar_tensor_tensor(out=v, in0=y[u][:, k, j, :],
                                                             scalar=c.gate[:, k, bass.ds(b * TB + j, 1)], in1=v,
                                                             op0=ALU.mult, op1=ALU.add)
                    ins.then_inc(s[done], 1)
                    if k == 0:
                        after(dve, s["comb1"], b)

            def statistics(b, u):
                after(dve, s["comb"], b)
                apart(dve, b)
                for j in range(TB):
                    nc.vector.bn_stats(st[u][:, j, :], c.x[:, bass.ds(b * (TB * D) + j * D, D)]).then_inc(s["bn"], 1)
                after(dve, s["bn"], b, per=TB)
                apart(dve, b)
                for j in range(TB):
                    ins = nc.vector.bn_aggr(mv[u][:, j, :], st[u][:, j, :])
                ins.then_inc(s["stats"], 1)

            def normalise(b, u):
                after(dve, s["rstd"], b)
                after(dve, s["zT"], b, back=1)
                for j in range(TB):
                    ins = nc.vector.tensor_scalar(z[0][:, j, :], c.x[:, bass.ds(b * (TB * D) + j * D, D)],
                                                  mv[u][:, j, 0:1], rstd[u][:, j:j + 1], ALU.subtract, ALU.mult)
                ins.then_inc(s["zd"], 1)

            def delta(b, u):
                after(dve, s["uud"], b)
                after(dve, s["xd"], b, back=1)
                nc.vector.tensor_tensor_scan(state[0][:, 1:1 + S], c.beta[:, 0:1].to_broadcast([P, S]), uu[0][:, :],
                                             0.0, ALU.mult, ALU.add).then_inc(s["scan"], 1)
                after(dve, s["scan"], b)
                after(dve, s["mh"], b, back=1)
                nc.vector.tensor_tensor(xdT[0][:, :], ps_t[:, 0:S], state[0][:, 0:S], ALU.subtract).then_inc(s["xd"], 1)
                after(dve, s["xd"], b)
                nc.vector.tensor_reduce(xs[u][:, :], xdT[0][:, :], AX.X, ALU.add).then_inc(s["xsd"], 1)

            def mixing(b, u):
                after(dve, s["egd"], b)
                nc.vector.tensor_scalar(gd[u][:, :], eg[u][:, :], 1.0, None, ALU.add).then_inc(s["gdd"], 1)
                after(dve, s["gdd"], b)
                nc.vector.reciprocal(gr[u][:, :], gd[u][:, :]).then_inc(s["grd"], 1)
                after(dve, s["grd"], b)
                nc.vector.tensor_scalar(mb[0][:, :], c.hbig[:, :], gr[u][:, 0:1], None, ALU.mult).then_inc(s["mbd"], 1)

            def zeros_of(b, u):
                if isinstance(b, int) and b < R:
                    nc.vector.memset(ks[u][:, :, :], 0.0).then_inc(s["zeroed"], 1)

            def add_mixed(b, u):
                after(dve, s["mh"], b)
                nc.vector.tensor_tensor(xb(b), ps_q[:, 256:512], xb(b), ALU.add).then_inc(s["mhx"], 1)

            def maxima(k):
                def stage(b, u):
                    j, hs = heads2(k)
                    nth(dve, s["s2"], b, k, FILLS)
                    n = len(hs)
                    nc.vector.tensor_reduce(mx[u][:, j, hs[0]:hs[0] + n],
                                            ps_c2[k % 2][:, :].rearrange("p (h w) -> p h w", h=n), AX.X,
                                            ALU.max).then_inc(s["mxd"], 1)
                return stage

            def divide(j):
                def stage(b, u):
                    after(dve, s[f"on{j}"], b)
                    v = ps_o[:, :].rearrange("p (h w) -> p h w", h=H)
                    nc.vector.reciprocal(rd[0][:, j, :], v[:, :, DH]).then_inc(s[f"rd{j}"], 1)
                    after(dve, s[f"rd{j}"], b)
                    after(dve, s["oT2"], b, back=1)
                    nc.vector.tensor_tensor(on[0][:, j, :].rearrange("p (h w) -> p h w", h=H), v[:, :, 0:DH],
                                            rd[0][:, j, :].unsqueeze(2).to_broadcast([P, H, DH]),
                                            ALU.mult).then_inc(s[f"nrm{j}"], 1)
                return stage

            def join(b, u):
                after(dve, s["ao"], b)
                after(dve, s["xdk"], b)
                nc.vector.tensor_tensor(rb(b), ps_o[:, 0:S], rb(b), ALU.add).then_inc(s["rr"], 1)
                after(dve, s["rr"], b)
                after(dve, s["mhx"], b)
                nc.vector.tensor_tensor(xb(b), xb(b), rb(b), ALU.add).then_inc(s["rx"], 1)

            m = [(maxima(k), 2) for k in range(FILLS)]
            pipeline(dve, B, [(combine, AHEAD), (statistics, AHEAD), *m[0:2], (normalise, AHEAD), *m[2:4], (divide(0), 0),
                              m[4], (delta, AHEAD), m[5], (divide(1), 0), *m[6:8], (mixing, AHEAD), *m[8:10],
                              (add_mixed, AHEAD), (zeros_of, AHEAD), m[10], (join, 0), m[11]], AHEAD, start=2, ring=R)

        @block.scalar
        def _(act):
            def blend(b, u):
                after(act, s["zT"], b)
                after(act, s["scan"], b, back=1)
                nc.scalar.activation(uu[0][:, :], ps_t[:, 0:S], ACT.Copy, scale=c.omb[:, 0:1]).then_inc(s["uud"], 1)

            def rows(b, u):
                after(act, s["xdr"], b)
                for j in range(TB):
                    nc.scalar.activation(junk[:, j, :], ps_t[:, 256 + j * D:256 + (j + 1) * D], ACT.Square,
                                         accum_out=ss[u][:, j:j + 1]).then_inc(s["sq"], 1)
                nc.scalar.copy(rb(b), ps_t[:, 256:512]).then_inc(s["xdk"], 1)

            def gate(b, u):
                after(act, s["gate"], b)
                nc.scalar.activation(eg[u][:, :], ps_q[:, 0:1], ACT.Exp, bias=c.ngb[:, 0:1],
                                     scale=-1.0 / S).then_inc(s["egd"], 1)

            def scale_rows(b, u):
                after(act, s["ndTd"], b, back=1)
                after(act, s["xdk"], b)
                after(act, s["rs"], b)
                apart(act, b)
                for j in range(TB):
                    ins = nc.scalar.activation(nd[0][:, j, :], c.r[:, bass.ds(b * (TB * D) + j * D, D)], ACT.Copy,
                                               scale=rs[u][:, j:j + 1])
                ins.then_inc(s["ndd"], 1)

            def keep_turned(b, u):
                after(act, s["ndTd"], b)
                after(act, s["vd"], b, back=1)
                nc.scalar.activation(ndT[0][:, :], ps_t[:, 0:S], ACT.Copy,
                                     scale=c.wT[:, VECS, V_LN1:V_LN1 + 1]).then_inc(s["ndTk"], 1)

            def keep_qkv(b, u):
                after(act, s["qkd"], b)
                after(act, s["p2"], b, back=1)
                for k, row in ((0, V_BQ), (1, V_BK)):
                    nc.scalar.activation(qk[0][:, k, :], ps_q[:, k * S:(k + 1) * S], ACT.Identity,
                                         bias=c.wT[:, VECS, row:row + 1]).then_inc(s["qkk"], 1)

            def keep_v(b, u):
                after(act, s["vd"], b)
                if isinstance(b, int) and b < R:
                    act.wait_ge(s["preset2"], 2 * b + 2)
                nth(act, s["pvd"], b, k=0, per=FILLS, back=1 + (R - 1) * FILLS)
                nc.scalar.copy(va[u][:, :, :, 0:DH],
                               ps_t[:, 256:512].rearrange("p (t h w) -> p t h w", t=TB, h=H)).then_inc(s["vk"], 1)

            def keep_max(b, u):
                after(act, s["mTd"], b)
                nth(act, s["s3"], b, k=0, per=FILLS, back=1 + (R - 1) * FILLS)
                nc.scalar.copy(mT[u][:, :], ps_tb[0:KP, 0:S]).then_inc(s["mTk"], 1)

            def expo(k):
                def stage(b, u):
                    nth(act, s["s3"], b, k, FILLS)
                    nth(act, s["pvd"], b, k, FILLS, back=4)
                    nc.scalar.activation(pt[k % 4][:, :], ps_c3[k % 2][:, :], ACT.Exp, scale=SCALE).then_inc(s["exd"], 1)
                return stage

            def keep_out(half):
                def stage(b, u):
                    nth(act, s["pvd"], b, 6 * half + 5, FILLS)
                    if half == 0:
                        after(act, s["on1"], b, back=1)
                    nc.scalar.copy(oTs[0][:, 2 * half:2 * half + 2, :].rearrange("p g q -> p (g q)"),
                                   ps_pv[:, :]).then_inc(s["otk"], 1)
                return stage

            def keep_o(b, u):
                after(act, s["oT2"], b)
                after(act, s["ao"], b, back=1)
                nc.scalar.copy(oT[0][:, :], ps_t[:, 0:S]).then_inc(s["oT2k"], 1)

            e = [(expo(k), 1) for k in range(FILLS)]
            pipeline(act, B, [e[0], (keep_out(1), 0), *e[1:3], (blend, AHEAD), *e[3:6], (keep_o, 0), e[6], (rows, AHEAD),
                              (gate, AHEAD), (keep_out(0), 1), e[7], (scale_rows, AHEAD), e[8], (keep_turned, AHEAD),
                              (keep_v, AHEAD), e[9], (keep_qkv, AHEAD), e[10], (keep_max, 2), e[11]],
                     AHEAD, start=2, ring=R)

        @block.tensor
        def _(pe):
            pe.wait_ge(s["built"], 1)
            nc.tensor.transpose(ps_o[0:NS, 0:NS], hr[:, :], c.ident[0:NS, 0:NS]).then_inc(s["hT"], 1)
            pe.wait_ge(s["built"], 2)
            nc.tensor.matmul(ps_o[:, P:2 * P], c.esel[:, :, :].rearrange("n a b -> n (a b)"),
                             hTe[:, :, :].rearrange("n a b -> n (a b)"), start=True, stop=True).then_inc(s["hT"], 1)
            pe.wait_ge(s["built"], 3)

            def turn_z(b, u):
                after(pe, s["zd"], b)
                after(pe, s["vk"], b, back=1)
                after(pe, s["mTk"], b, back=AHEAD - 1)
                for j in range(TB):
                    mm = nc.tensor.transpose(ps_t[:, j * P:(j + 1) * P], z[0][:, j, :], c.ident[:, :])
                mm.then_inc(s["zT"], 1)

            def turn_delta(b, u):
                after(pe, s["xd"], b)
                nth(pe, s["oT2k"], b, back=AHEAD)
                for j in range(TB):
                    mm = nc.tensor.transpose(ps_t[:, 256 + j * P:256 + (j + 1) * P], xdT[0][:, :][:, j * P:(j + 1) * P],
                                             c.ident[:, :])
                mm.then_inc(s["xdr"], 1)
                after(pe, s["xsd"], b)
                nth(pe, s["qkk"], b, k=1, per=2, back=2)
                nc.tensor.matmul(ps_q[:, 0:1], c.wT[:, GATE1, :], xs[u][:, :], start=True, stop=True).then_inc(s["gate"], 1)

            def mix(b, u):
                after(pe, s["mbd"], b)
                after(pe, s["egd"], b)
                for j in range(TB):
                    mm = nc.tensor.matmul(ps_q[:, 256 + j * P:256 + (j + 1) * P], xdT[0][:, :][:, j * P:(j + 1) * P],
                                          mb[0][:, :], start=True, stop=True)
                mm.then_inc(s["mh"], 1)

            def turn_normed(b, u):
                after(pe, s["ndd"], b)
                after(pe, s["xdk"], b)
                nth(pe, s["sq"], b, k=1, per=2)
                for j in range(TB):
                    mm = nc.tensor.transpose(ps_t[:, j * P:(j + 1) * P], nd[0][:, j, :], c.ident[:, :])
                mm.then_inc(s["ndTd"], 1)

            def project(b, u):
                after(pe, s["ndTk"], b)
                after(pe, s["mhx"], b)
                nc.tensor.matmul(ps_q[:, 0:S], wq, ndT[0][:, :], start=True, stop=True)
                nc.tensor.matmul(ps_q[:, S:2 * S], wk, ndT[0][:, :], start=True, stop=True).then_inc(s["qkd"], 1)
                for j in range(TB):
                    o = ps_t[:, 256 + j * P:256 + (j + 1) * P]
                    nc.tensor.matmul(o, ndT[0][:, j * P:(j + 1) * P], wv, start=True, stop=False)
                    mm = nc.tensor.matmul(o, c.ones[:, :], c.rows[:, R_V, :], start=False, stop=True)
                mm.then_inc(s["vd"], 1)

            def turn_max(b, u):
                after(pe, s["a3"], b)
                nth(pe, s["vk"], b, back=2 - AHEAD)
                after(pe, s["oT2k"], b, back=2)
                for j in range(TB):
                    mm = nc.tensor.transpose(ps_tb[0:KP, j * P:(j + 1) * P],
                                             mp[0][:, j, :, :].rearrange("p a b -> p (a b)"), c.identb[:, :])
                mm.then_inc(s["mTd"], 1)

            def scores(k):
                def stage(b, u):
                    j, hs = heads2(k)
                    if k == 0:
                        of_ring(pe, stack, b, u, NSTACK)
                    nth(pe, s["mxd"], b, k, FILLS, back=2)
                    w = (j + 1) * P
                    out = ps_c2[k % 2][:, :].rearrange("p (h w) -> p h w", w=w)
                    nc.tensor.matmul(out[:, :, j * P:w], c.identb[:, :], c.mask_q[:, 0:len(hs) * P], start=True, stop=False,
                                     skip_group_check=True)
                    for n, h in enumerate(hs):
                        for i in range(j + 1):
                            mm = nc.tensor.matmul(out[:, n, i * P:(i + 1) * P], qs[u][:, h % (H // 2), j * P:(j + 1) * P],
                                                  ks[u][:, h, i * P:(i + 1) * P], start=False, stop=True,
                                                  skip_group_check=True)
                    mm.then_inc(s["s2"], 1)
                return stage

            def scores_t(k):
                def stage(b, u):
                    j, hs = heads3(k)
                    if k == 0:
                        after(pe, s["mTk"], b)
                    nth(pe, s["exd"], b, k, FILLS, back=2)
                    w = S - j * P
                    out = ps_c3[k % 2][:, :].rearrange("p (h w) -> p h w", w=w)
                    nc.tensor.matmul(out[:, :, 0:P], c.identb[:, :], c.mask_k[:, 0:len(hs) * P], start=True, stop=False,
                                     skip_group_check=True)
                    for n, h in enumerate(hs):
                        for i in range(TB - j):
                            nc.tensor.matmul(out[:, n, i * P:(i + 1) * P], ks[u][:, h, j * P:(j + 1) * P],
                                             qs[u][:, h % (H // 2), (j + i) * P:(j + i + 1) * P], start=False,
                                             stop=False, skip_group_check=True)
                        mm = nc.tensor.matmul(out[:, n, :], c.pick[:, h, :], mT[u][:, j * P:S], start=False, stop=True,
                                              skip_group_check=True)
                    mm.then_inc(s["s3"], 1)
                return stage

            def weigh(k):
                def stage(b, u):
                    j, hs = heads3(k)
                    nth(pe, s["exd"], b, k, FILLS)
                    if k == 0:
                        after(pe, s["vk"], b)
                        nth(pe, s["otk"], b, k=0, per=2, back=1)
                    if k == 6:
                        nth(pe, s["otk"], b, k=0, per=2)
                    w = S - j * P
                    for n, h in enumerate(hs):
                        q, at = 32 * (h % 4), (h // 4 % 2) * S
                        mm = nc.tensor.matmul(ps_pv[q:q + 32, at + j * P:at + S], va[u][:, j, h, :],
                                              pt[k % 4][:, n * w:(n + 1) * w], start=(j == 0), stop=(j == 1),
                                              skip_group_check=True)
                    mm.then_inc(s["pvd"], 1)
                return stage

            def turn_out(j):
                def stage(b, u):
                    if j == 0:
                        nth(pe, s["otk"], b, k=1, per=2)
                        after(pe, s["rr"], b, back=1)
                    else:
                        after(pe, s["nrm0"], b)
                    for g in range(4):
                        mm = nc.tensor.transpose(ps_o[:, g * P:(g + 1) * P], oTs[0][:, g, j * P:(j + 1) * P],
                                                 c.ident[:, :])
                    mm.then_inc(s[f"on{j}"], 1)
                return stage

            def turn_o(b, u):
                after(pe, s["nrm1"], b)
                nth(pe, s["xd"], b, back=-AHEAD)
                nth(pe, s["mTk"], b, back=-1)
                for j in range(TB):
                    mm = nc.tensor.transpose(ps_t[:, j * P:(j + 1) * P], on[0][:, j, :], c.ident[:, :])
                mm.then_inc(s["oT2"], 1)

            def project_out(b, u):
                after(pe, s["oT2k"], b)
                for j in range(TB):
                    o = ps_o[:, j * P:(j + 1) * P]
                    nc.tensor.matmul(o, oT[0][:, j * P:(j + 1) * P], wo, start=True, stop=False)
                    mm = nc.tensor.matmul(o, c.ones[:, :], c.rows[:, R_OUT, :], start=False, stop=True)
                mm.then_inc(s["ao"], 1)

            s2 = [(scores(k), 2) for k in range(FILLS)]
            s3 = [(scores_t(k), 1) for k in range(FILLS)]
            pv = [(weigh(k), 1 if k < 10 else 0) for k in range(FILLS)]
            pipeline(pe, B, [s3[0], *s2[0:2], *pv[10:12], s3[1], s2[2], pv[0], (turn_out(0), 0), s3[2], s2[3], pv[1],
                             (turn_z, AHEAD), s3[3], s2[4], pv[2], (turn_out(1), 0), s3[4], s2[5], pv[3], s2[6], s3[5],
                             pv[4], (turn_o, 0), s2[7], s3[6], (turn_delta, AHEAD), pv[5], s2[8], s3[7], pv[6],
                             (project_out, 0), (mix, AHEAD), (turn_normed, AHEAD), s2[9], s3[8], s2[10], pv[7], s2[11],
                             (project, AHEAD), s3[9], pv[8], s3[10], pv[9], (turn_max, 2), s3[11]],
                     AHEAD, start=2, ring=R)


def feed_forward(nc, outer, c, router):
    AHEAD = 8
    x3 = outer.enter_context(semaphores(nc))("d_x3")
    router.open(nc, outer, x3)
    with ExitStack() as ctx:
        named = ctx.enter_context(semaphores(nc))

        def pair(name, shape, dt=F32):
            return [ctx.enter_context(nc.sbuf_tensor(f"d_{name}{u}", shape, dt)) for u in range(2)]

        def banks(name, n=2):
            return [ctx.enter_context(nc.psum_tensor(f"d_{name}{u}", [P, 512], F32)) for u in range(n)]

        junk, ss, se, rs = pair("junk", [P, D]), pair("ss", [P, 1]), pair("se", [P, 1]), pair("rs", [P, 1])
        nd, ndT, hT = pair("nd", [P, D]), pair("ndT", [P, P]), pair("hT", [P, F])
        ps_n, ps_h, ps_y = banks("n", 1)[0], banks("h"), banks("y")
        sq, sed, rsd, ndd, ndTd, ndTk, hd, hTd, yd = (
            named("d_" + n) for n in ("sq", "se", "rs", "nd", "ndT", "ndTk", "h", "hT", "y"))
        block = ctx.enter_context(nc.Block())

        def r_of(t):
            return c.r[:, bass.ds(t * D, D)]

        @block.scalar
        def _(act):
            def squares(t, u):
                after(act, sed, t, back=2)
                after(act, sq, t, back=2)
                nc.scalar.activation(junk[u % 2][:, :], r_of(t), ACT.Square, accum_out=ss[u % 2][:, :]).then_inc(sq, 1)

            def keep_turned(t, u):
                after(act, ndTd, t)
                after(act, hd, t, back=2)
                nc.scalar.activation(ndT[u % 2][:, :], ps_n[:, 0:P], ACT.Copy,
                                     scale=c.wT[:, VECS, V_LN2:V_LN2 + 1]).then_inc(ndTk, 1)

            def gelu(t, u):
                after(act, hd, t)
                after(act, yd, t, back=2)
                for k in range(FC):
                    ins = nc.scalar.activation(hT[u % 2][:, k * P:(k + 1) * P], ps_h[u % 2][:, k * P:(k + 1) * P], ACT.Gelu,
                                               bias=c.wT[:, VECS, V_FB1 + k:V_FB1 + k + 1])
                ins.then_inc(hTd, 1)

            pipeline(act, T, [(squares, 8), (keep_turned, 6), (router.keep_turned(act), 2), (gelu, 5),
                              (router.keep_projected(act), 2), (router.copy_row(act), 3)], AHEAD, start=4, ring=4)

        @block.gpsimd
        def _(pool):
            def root(t, u):
                after(pool, sq, t)
                apart(pool, t)
                nc.gpsimd.tensor_scalar(se[u % 2][:, :], ss[u % 2][:, :], 1.0 / D, RMS_EPS, ALU.mult, ALU.add).then_inc(sed, 1)
                after(pool, sed, t)
                after(pool, ndd, t, back=2)
                nc.gpsimd.tensor_tensor(rs[u % 2][:, :], se[u % 2][:, :], c.neghalf[:, 0:1], ALU.pow).then_inc(rsd, 1)

            pipeline(pool, T, [(root, 7), (router.root(pool), 3), (router.stamp(pool), 3), (router.send(pool), 0)], AHEAD,
                     start=4, ring=4)
            router.sent_all(pool)

        @block.vector
        def _(dve):
            def scale_rows(t, u):
                after(dve, rsd, t)
                after(dve, ndTd, t, back=2)
                nc.vector.tensor_scalar(nd[u % 2][:, :], r_of(t), rs[u % 2][:, 0:1], None, ALU.mult).then_inc(ndd, 1)

            def residual(t, u):
                after(dve, yd, t)
                x = c.x[:, bass.ds(t * D, D)]
                nc.vector.tensor_tensor(x, ps_y[u % 2][:, 0:D], x, ALU.add).then_inc(x3, 1)

            add_region, pick, as_row = router.place(dve)
            sums, moments = router.statistics(dve)
            keep, best, find, as_float, one_hot, both, count = router.select(dve)
            pipeline(dve, T, [(sums, 3), (add_region, 0), (moments, 3), (pick, 0), (keep, 1), (as_row, 0), (best, 1),
                              (scale_rows, 7), (find, 1), (router.normalise(dve), 3), (as_float, 1), (one_hot, 1),
                              (both, 1), (count, 1), (residual, 4)], AHEAD, start=4, ring=4)

        @block.tensor
        def _(pe):
            def turn(t, u):
                after(pe, ndd, t)
                after(pe, ndTk, t, back=1)
                nc.tensor.transpose(ps_n[:, 0:P], nd[u % 2][:, :], c.ident[:, :]).then_inc(ndTd, 1)

            def up(t, u):
                after(pe, ndTk, t)
                after(pe, hTd, t, back=2)
                for k in range(FC):
                    mm = nc.tensor.matmul(ps_h[u % 2][:, k * P:(k + 1) * P], c.wT[:, FF1 + k, :], ndT[u % 2][:, :], start=True,
                                          stop=True)
                mm.then_inc(hd, 1)

            def down(t, u):
                after(pe, hTd, t)
                after(pe, x3, t, back=2)
                for k in range(FC):
                    nc.tensor.matmul(ps_y[u % 2][:, 0:D], hT[u % 2][:, k * P:(k + 1) * P], c.wT[:, FF2 + k, :], start=(k == 0),
                                     stop=False)
                nc.tensor.matmul(ps_y[u % 2][:, 0:D], c.ones[:, :], c.rows[:, R_FB2, :], start=False,
                                 stop=True).then_inc(yd, 1)

            pipeline(pe, T, [(router.positions(pe), 0), (router.logits(pe), 1), (turn, 6), (router.turn(pe), 2), (up, 5),
                             (router.project(pe), 2), (down, 4)], AHEAD, start=4, ring=4)


@contextmanager
def expert_weights(nc, c, a, layer):
    names = ("L0_ffn_", "L1_ffn_")[layer]
    with ExitStack() as ctx:
        def sb(name, shape):
            return ctx.enter_context(nc.sbuf_tensor(f"{name}_{layer}", shape, F32))

        c.w1, c.w2 = sb("w1", [P, E, F]), sb("w2", [P, E * FC, D])
        c.b2bc = sb("b2bc", [P, E * D])
        c.e_in = ctx.enter_context(semaphores(nc))(f"e_in{layer}")
        with nc.Block() as block:
            @block.scalar
            def _(act):
                act.dma_start(c.b2bc[:, :], a[names + "b2"].rearrange("e d -> (e d)").unsqueeze(0)
                              .to_broadcast([P, E * D])).then_inc(c.e_in, 16)
                act.dma_start(c.w1[:, :, :], a[names + "W1"].rearrange("e d f -> d e f")).then_inc(c.e_in, 16)
                act.dma_start(c.w2[:, :, :], a[names + "W2"].rearrange("e (c p) d -> p (e c) d", p=P)
                              ).then_inc(c.e_in, 16)
        yield


def combine_and_store(nc, ctx, c, out):
    G = 4
    parts = T // G
    added, stored = (ctx.enter_context(nc.semaphore(s)) for s in ("added", "stored"))
    fetched = [ctx.enter_context(nc.semaphore(f"fetched{g}")) for g in range(parts)]
    res = c.res[0:TOPK * T * P, :].rearrange("(k t p) d -> k p t d", k=TOPK, p=P)
    outv = out.rearrange("b (h p) d -> p (b h) d", p=P)
    with ExitStack() as tmp:
        y = tmp.enter_context(nc.sbuf_tensor("y", [P, TOPK, T, D], F32))
        block = tmp.enter_context(nc.Block())

        @block.scalar
        def _(act):
            for g in range(parts):
                act.dma_start(y[:, 1, g * G:(g + 1) * G, :], res[1, :, g * G:(g + 1) * G, :]).then_inc(fetched[g], 16)

        @block.sync
        def _(sp):
            for g in range(parts):
                sp.dma_start(y[:, 0, g * G:(g + 1) * G, :], res[0, :, g * G:(g + 1) * G, :]).then_inc(fetched[g], 16)
            for g in range(parts):
                sp.wait_ge(added, 2 * g + 2)
                sp.dma_start(outv[:, g * G:(g + 1) * G, :],
                             c.x[:, g * G * D:(g + 1) * G * D].rearrange("p (t d) -> p t d", d=D)).then_inc(stored, 16)
            sp.wait_ge(stored, 16 * parts)

        @block.vector
        def _(dve):
            for g in range(parts):
                dve.wait_ge(fetched[g], 32)
                for k in range(TOPK):
                    for t in range(g * G, g * G + G):
                        xs = c.x[:, t * D:(t + 1) * D]
                        ins = nc.vector.scalar_tensor_tensor(out=xs, in0=y[:, k, t, :], scalar=c.gate[:, k, t:t + 1],
                                                             in1=xs, op0=ALU.mult, op1=ALU.add)
                    ins.then_inc(added, 1)
                    dve.wait_ge(added, TOPK * g + k + 1)


def transformer(nc, a, out, stage=9):
    with ExitStack() as ctx:
        c = Core()
        c.tile_e = ctx.enter_context(nc.sbuf_tensor("tile_e", [1, XT], U32))
        c.tile_r = ctx.enter_context(nc.sbuf_tensor("tile_r", [1, XT], U32))
        load_and_prepare(nc, ctx, c, a)
        with expert_weights(nc, c, a, 0):
            with ExitStack() as routed:
                first = Router(nc, c, "r0", False)
                head_attention(nc, routed, c, first)
                first.finish(nc, routed)
            run_experts(nc, c, "x0", V_B1A, with_masks=True)
        with ExitStack() as layer1:
            c.r = layer1.enter_context(nc.sbuf_tensor("r", [P, T * D], F32))
            causal_attention(nc, c)
            with expert_weights(nc, c, a, 1):
                with ExitStack() as routed:
                    second = Router(nc, c, "r1", True)
                    feed_forward(nc, routed, c, second)
                    second.finish(nc, routed)
                run_experts(nc, c, "x1", V_B1B)
        combine_and_store(nc, ctx, c, out)


def kernel(**inputs):
    import numpy as _np
    import concourse.bacc as _bacc
    from concourse import mybir as _mybir
    from concourse.bass_utils import run_bass_kernel_spmd as _run

    nc = _bacc.Bacc("TRN2", target_bir_lowering=False, num_devices=1)
    arrays, args = {}, {}
    for name, value in inputs.items():
        array = _np.ascontiguousarray(value)
        arrays[f"in_{name}_dram"] = array
        args[name] = nc.dram_tensor(f"in_{name}_dram", array.shape, _mybir.dt.from_np(array.dtype),
                                    kind="ExternalInput").ap()
    out = nc.dram_tensor("out_0_dram", (B, S, D), _mybir.dt.float32, kind="ExternalOutput").ap()
    transformer(nc, args, out)
    result = _run(nc, [arrays], core_ids=[0])
    return result.results[0]["out_0_dram"]
```
